# Optimizing a Trainium2 kernel written in Bass

```python
import numpy as np
import jax
import jax.numpy as jnp

def _softmax(x, axis=-1):
    return jax.nn.softmax(x, axis=axis)

def _gelu(x):
    return jax.nn.gelu(x, approximate=True)

def _silu(x):
    return jax.nn.silu(x)

def _sigmoid(x):
    return jax.nn.sigmoid(x)

def _layernorm(x, axis=-1, eps=1e-05):
    m = jnp.mean(x, axis=axis, keepdims=True)
    v = jnp.var(x, axis=axis, keepdims=True)
    return (x - m) / jnp.sqrt(v + eps)

def _scatter_add(tgt, idx, src, axis=0):
    return tgt.at[idx].add(src)

def _segment_sum(src, seg, n):
    return jax.ops.segment_sum(src, seg, n)
kernel_name = 'mk_adj_preln_d4_adj_r2_81b550'

def setup_inputs(seed: int=0):
    np.random.seed(seed)
    _w = jnp.asarray

    def _rec_inputs():
        import jax
        import jax.numpy as jnp
        _gk = jax.random.key(seed)
        x = -0.0003702 + 0.9999 * jax.random.normal(jax.random.fold_in(_gk, 1), (16, 500, 128), jnp.float32)
        _a = jax.random.bernoulli(jax.random.fold_in(_gk, 2), 0.032, (16, 500, 500))
        _af = _a.astype(jnp.float32)
        adj = _af
        return (x, adj)
    x, adj = _rec_inputs()

    def _L0_gnn_setup():
        import jax, jax.numpy as jnp
        import numpy as np
        N, D, L = (500, 128, 7)
        B = 64
        key = jax.random.key(seed)
        ks = jax.random.split(key, 8)
        x = jax.random.normal(ks[0], (B, N, D), dtype=jnp.float32)
        adj = (jax.random.uniform(ks[1], (B, N, N)) < 0.05).astype(jnp.float32)
        W_attn = jax.random.normal(ks[2], (L, D, D), dtype=jnp.float32) * 0.01
        b_attn = jnp.zeros((L, D), jnp.float32)
        W0 = jax.random.normal(ks[3], (L, D, D), dtype=jnp.float32) * 0.05
        b0 = jnp.zeros((L, D), jnp.float32)
        W1 = jax.random.normal(ks[4], (L, D, D), dtype=jnp.float32) * 0.05
        b1 = jnp.zeros((L, D), jnp.float32)
        Wf = jax.random.normal(ks[5], (D, D), dtype=jnp.float32) * 0.05
        bf = jnp.zeros((D,), jnp.float32)
        return {'x': x, 'adj': adj, 'W_attn': W_attn, 'b_attn': b_attn, 'W0': W0, 'b0': b0, 'W1': W1, 'b1': b1, 'Wf': Wf, 'bf': bf}
    _L0_gnn_all = _L0_gnn_setup()
    _L0_gnn_in = {k: v for k, v in _L0_gnn_all.items() if k in ('W_attn', 'b_attn', 'W0', 'b0', 'W1', 'b1', 'Wf', 'bf')}
    del _L0_gnn_all

    def _L1_gnn_setup():
        import jax, jax.numpy as jnp
        import numpy as np
        B, N, D_IN, D_OUT = (16, 512, 128, 128)
        NEG_INF = -9000000000000000.0
        LRELU_SLOPE = 0.2
        key = jax.random.key(seed)
        k1, k2, k3, k4 = jax.random.split(key, 4)
        x = jax.random.normal(k1, (B, N, D_IN), dtype=jnp.float32)
        adj_matrix = jax.random.randint(k2, (B, N, N), 0, 2).astype(jnp.float32)
        w_lim = float(np.sqrt(6.0 / (D_IN + D_OUT)))
        a_lim = float(np.sqrt(6.0 / (2 * D_OUT + 1)))
        W = jax.random.uniform(k3, (D_IN, D_OUT), minval=-w_lim, maxval=w_lim, dtype=jnp.float32)
        a = jax.random.uniform(k4, (2 * D_OUT, 1), minval=-a_lim, maxval=a_lim, dtype=jnp.float32)
        return {'x': x, 'adj_matrix': adj_matrix, 'W': W, 'a': a}
    _L1_gnn_all = _L1_gnn_setup()
    _L1_gnn_in = {k: v for k, v in _L1_gnn_all.items() if k in ('W', 'a')}
    del _L1_gnn_all

    def _L2_gnn_setup():
        import jax, jax.numpy as jnp
        import numpy as np
        GROUPS = [list(range(25)), [0, 1, 2, 3, 4, 5, 6, 7, 8], [0, 9, 10, 11, 12, 13, 14], [6, 7, 8, 12, 13, 14], [3, 4, 5, 9, 10, 11]]
        B, N, D_IN, D_HID = (4096, 25, 128, 256)

        def _graph_conv(x, adj, W, b):
            n = adj.shape[-1]
            A = adj + jnp.eye(n, dtype=adj.dtype)
            deg = jnp.sum(A, axis=-1)
            deg_safe = jnp.where(deg == 0, 1.0, deg)
            dinv = jnp.where(deg == 0, 0.0, deg_safe ** (-0.5))
            norm_adj = dinv[:, :, None] * A * dinv[:, None, :]
            support = jnp.einsum('bnd,de->bne', x, W)
            out = jnp.einsum('bnm,bme->bne', norm_adj, support) + b
            return jax.nn.relu(out)
        key = jax.random.key(seed)
        ks = jax.random.split(key, 7)
        s1 = float(np.sqrt(6.0 / (D_IN + D_HID)))
        s2 = float(np.sqrt(6.0 / (D_HID + D_IN)))
        return {'x': jax.random.normal(ks[0], (B, N, D_IN), dtype=jnp.float32), 'adj': jax.random.uniform(ks[1], (B, N, N), dtype=jnp.float32), 'W1': jax.random.uniform(ks[2], (5, D_IN, D_HID), jnp.float32, -s1, s1), 'b1': jnp.zeros((5, D_HID), dtype=jnp.float32), 'W2': jax.random.uniform(ks[3], (5, D_HID, D_IN), jnp.float32, -s2, s2), 'b2': jnp.zeros((5, D_IN), dtype=jnp.float32), 'fusion_w': jnp.ones((5,), dtype=jnp.float32)}
    _L2_gnn_all = _L2_gnn_setup()
    _L2_gnn_in = {k: v for k, v in _L2_gnn_all.items() if k in ('W1', 'b1', 'W2', 'b2', 'fusion_w')}
    del _L2_gnn_all

    def _L3_gnn_setup():
        import jax, jax.numpy as jnp
        import numpy as np
        B, K, H = (32, 512, 128)
        LN_EPS = 1e-05

        def layer_norm(x, gamma, beta):
            mu = jnp.mean(x, axis=-1, keepdims=True)
            var = jnp.mean(jnp.square(x - mu), axis=-1, keepdims=True)
            return (x - mu) * jax.lax.rsqrt(var + LN_EPS) * gamma + beta
        key = jax.random.key(seed)
        k1, k2, k3, k4 = jax.random.split(key, 4)
        x = jax.random.normal(k1, (B, K, H), dtype=jnp.float32)
        adj = jax.random.uniform(k2, (B, K, K), dtype=jnp.float32)
        s = 1.0 / np.sqrt(H)
        W_rel = jax.random.normal(k3, (H, H), dtype=jnp.float32) * s
        b_rel = jnp.zeros((H,), dtype=jnp.float32)
        W_root = jax.random.normal(k4, (H, H), dtype=jnp.float32) * s
        ln_gamma = jnp.ones((H,), dtype=jnp.float32)
        ln_beta = jnp.zeros((H,), dtype=jnp.float32)
        return {'x': x, 'adj': adj, 'W_rel': W_rel, 'b_rel': b_rel, 'W_root': W_root, 'ln_gamma': ln_gamma, 'ln_beta': ln_beta}
    _L3_gnn_all = _L3_gnn_setup()
    _L3_gnn_in = {k: v for k, v in _L3_gnn_all.items() if k in ('W_rel', 'b_rel', 'W_root', 'ln_gamma', 'ln_beta')}
    del _L3_gnn_all
    return {'x': x, 'adj': adj, 'L0_gnn_W_attn': _L0_gnn_in['W_attn'], 'L0_gnn_b_attn': _L0_gnn_in['b_attn'], 'L0_gnn_W0': _L0_gnn_in['W0'], 'L0_gnn_b0': _L0_gnn_in['b0'], 'L0_gnn_W1': _L0_gnn_in['W1'], 'L0_gnn_b1': _L0_gnn_in['b1'], 'L0_gnn_Wf': _L0_gnn_in['Wf'], 'L0_gnn_bf': _L0_gnn_in['bf'], 'L1_gnn_W': _L1_gnn_in['W'], 'L1_gnn_a': _L1_gnn_in['a'], 'L2_gnn_W1': _L2_gnn_in['W1'], 'L2_gnn_b1': _L2_gnn_in['b1'], 'L2_gnn_W2': _L2_gnn_in['W2'], 'L2_gnn_b2': _L2_gnn_in['b2'], 'L2_gnn_fusion_w': _L2_gnn_in['fusion_w'], 'L3_gnn_W_rel': _L3_gnn_in['W_rel'], 'L3_gnn_b_rel': _L3_gnn_in['b_rel'], 'L3_gnn_W_root': _L3_gnn_in['W_root'], 'L3_gnn_ln_gamma': _L3_gnn_in['ln_gamma'], 'L3_gnn_ln_beta': _L3_gnn_in['ln_beta']}

def reference(x, adj, L0_gnn_W_attn, L0_gnn_b_attn, L0_gnn_W0, L0_gnn_b0, L0_gnn_W1, L0_gnn_b1, L0_gnn_Wf, L0_gnn_bf, L1_gnn_W, L1_gnn_a, L2_gnn_W1, L2_gnn_b1, L2_gnn_W2, L2_gnn_b2, L2_gnn_fusion_w, L3_gnn_W_rel, L3_gnn_b_rel, L3_gnn_W_root, L3_gnn_ln_gamma, L3_gnn_ln_beta):
    import jax
    import jax.numpy as jnp

    def _L0_gnn_ref(x, adj, W_attn, b_attn, W0, b0, W1, b1, Wf, bf):
        import jax, jax.numpy as jnp
        import numpy as np
        N, D, L = (500, 128, 7)
        B = 64
        idx = jnp.arange(N)
        adj = adj.at[:, idx, idx].set(1.0)
        eps_eye = 1e-05 * jnp.eye(N, dtype=x.dtype)
        for l in range(L):
            x0 = x
            q = x @ W_attn[l].T + b_attn[l]
            s = jax.nn.sigmoid(jnp.einsum('bid,bjd->bij', q, x))
            s = (s + eps_eye) * adj
            s = s / jnp.sum(s, axis=-1, keepdims=True)
            x = jnp.einsum('bij,bjd->bid', s, x)
            x = jax.nn.relu(x @ W0[l].T + b0[l])
            x = jax.nn.relu(x @ W1[l].T + b1[l])
            x = x + x0
        return x @ Wf.T + bf

    def _L1_gnn_ref(x, adj_matrix, W, a):
        import jax, jax.numpy as jnp
        import numpy as np
        B, N, D_IN, D_OUT = (16, 512, 128, 128)
        NEG_INF = -9000000000000000.0
        LRELU_SLOPE = 0.2
        h = jnp.einsum('bni,io->bno', x, W)
        d = h.shape[-1]
        a1 = a[:d, 0]
        a2 = a[d:, 0]
        src = h @ a1
        dst = h @ a2
        e = src[:, :, None] + dst[:, None, :]
        e = jnp.where(e >= 0, e, LRELU_SLOPE * e)
        masked_e = jnp.where(adj_matrix > 0, e, NEG_INF)
        attention = jax.nn.softmax(masked_e, axis=2)
        h_out = jnp.einsum('bij,bjd->bid', attention, h)
        return h_out

    def _L2_gnn_ref(x, adj, W1, b1, W2, b2, fusion_w):
        import jax, jax.numpy as jnp
        import numpy as np
        GROUPS = [list(range(25)), [0, 1, 2, 3, 4, 5, 6, 7, 8], [0, 9, 10, 11, 12, 13, 14], [6, 7, 8, 12, 13, 14], [3, 4, 5, 9, 10, 11]]
        B, N, D_IN, D_HID = (4096, 25, 128, 256)

        def _graph_conv(x, adj, W, b):
            n = adj.shape[-1]
            A = adj + jnp.eye(n, dtype=adj.dtype)
            deg = jnp.sum(A, axis=-1)
            deg_safe = jnp.where(deg == 0, 1.0, deg)
            dinv = jnp.where(deg == 0, 0.0, deg_safe ** (-0.5))
            norm_adj = dinv[:, :, None] * A * dinv[:, None, :]
            support = jnp.einsum('bnd,de->bne', x, W)
            out = jnp.einsum('bnm,bme->bne', norm_adj, support) + b
            return jax.nn.relu(out)
        norm_w = jax.nn.softmax(fusion_w)
        fused = jnp.zeros_like(x)
        for g, idx_list in enumerate(GROUPS):
            idx = jnp.asarray(idx_list)
            x_g = x[:, idx, :]
            adj_g = adj[:, idx][:, :, idx]
            h = _graph_conv(x_g, adj_g, W1[g], b1[g])
            out_g = _graph_conv(h, adj_g, W2[g], b2[g])
            fused = fused.at[:, idx, :].add(norm_w[g] * out_g)
        return fused

    def _L3_gnn_ref(x, adj, W_rel, b_rel, W_root, ln_gamma, ln_beta):
        import jax, jax.numpy as jnp
        import numpy as np
        B, K, H = (32, 512, 128)
        LN_EPS = 1e-05

        def layer_norm(x, gamma, beta):
            mu = jnp.mean(x, axis=-1, keepdims=True)
            var = jnp.mean(jnp.square(x - mu), axis=-1, keepdims=True)
            return (x - mu) * jax.lax.rsqrt(var + LN_EPS) * gamma + beta
        h = layer_norm(x, ln_gamma, ln_beta)
        agg = jnp.einsum('bij,bjh->bih', adj, h)
        conv = jnp.einsum('bkh,ho->bko', agg, W_rel) + b_rel + jnp.einsum('bkh,ho->bko', h, W_root)
        return x + jax.nn.relu(conv)
    h = jnp.maximum(_layernorm(x, axis=-1), 0.0)
    x = x + _L0_gnn_ref(h, adj, L0_gnn_W_attn, L0_gnn_b_attn, L0_gnn_W0, L0_gnn_b0, L0_gnn_W1, L0_gnn_b1, L0_gnn_Wf, L0_gnn_bf)
    h = jnp.maximum(_layernorm(x, axis=-1), 0.0)
    x = x + _L1_gnn_ref(h, adj, L1_gnn_W, L1_gnn_a)
    h = jnp.maximum(_layernorm(x, axis=-1), 0.0)
    x = x + _L2_gnn_ref(h, adj, L2_gnn_W1, L2_gnn_b1, L2_gnn_W2, L2_gnn_b2, L2_gnn_fusion_w)
    h = jnp.maximum(_layernorm(x, axis=-1), 0.0)
    x = x + _L3_gnn_ref(h, adj, L3_gnn_W_rel, L3_gnn_b_rel, L3_gnn_W_root, L3_gnn_ln_gamma, L3_gnn_ln_beta)
    return x

_drawn_inputs = setup_inputs


def setup_inputs(seed=0):
    import zlib

    import numpy as np

    out = dict(_drawn_inputs(seed))
    spreads = {'L0_gnn_b_attn': (0.0, 0.8),
     'L0_gnn_b0': (0.0, 0.1),
     'L0_gnn_b1': (0.0, 0.1),
     'L0_gnn_bf': (0.0, 0.1),
     'L2_gnn_b1': (0.0, 0.8),
     'L2_gnn_b2': (0.0, 0.8),
     'L2_gnn_fusion_w': (1.0, 0.6),
     'L3_gnn_b_rel': (0.0, 0.8),
     'L3_gnn_ln_gamma': (1.0, 0.2),
     'L3_gnn_ln_beta': (0.0, 0.1)}
    factors = {'L0_gnn_W_attn': 8.0, 'L2_gnn_W1': 8.0, 'L2_gnn_W2': 7.126}
    for name, (base, spread) in spreads.items():
        noise = np.random.default_rng([zlib.crc32(name.encode()), seed]).standard_normal(out[name].shape)
        drawn = base * np.exp(spread * noise) if base else spread * noise
        out[name] = jnp.asarray(drawn.astype(out[name].dtype))
    for name, factor in factors.items():
        out[name] = (out[name] * factor).astype(out[name].dtype)
    return out
```

```python
from contextlib import ExitStack

import numpy as np

import concourse.bass as bass
from concourse import mybir

F32 = mybir.dt.float32
ALU = mybir.AluOpType
ACT = mybir.ActivationFunctionType
AX_X = mybir.AxisListType.X
ds = bass.ds

B, N, D = 16, 500, 128
LAYERS = 7
C, P = 4, 125
LANES = 2
PAIRS = B // LANES
STEPS = LAYERS * LANES
EPS_LN = 1e-5
EPS_EYE = 1e-5
NEG_INF = -9000000000000000.0
SLOPE = 0.2
GROUPS = [list(range(25)), [0, 1, 2, 3, 4, 5, 6, 7, 8], [0, 9, 10, 11, 12, 13, 14],
          [6, 7, 8, 12, 13, 14], [3, 4, 5, 9, 10, 11]]
G, GN, HID = len(GROUPS), 25, 256
FREE = 1
GB = 4
BLK = B // GB
R = GB * GN


def build(nc, t, out):
    ctx = ExitStack()
    with ctx:
        def sb(name, shape):
            return ctx.enter_context(nc.sbuf_tensor(name, shape, F32))

        def sem(name):
            return ctx.enter_context(nc.semaphore(name))

        ident = sb("ident", [128, 128])
        wqT = sb("wqT", [D, LAYERS, D])
        w0T = sb("w0T", [D, LAYERS, D])
        w1T = sb("w1T", [D, LAYERS, D])
        bq = sb("bq", [D, LAYERS])
        b0 = sb("b0", [D, LAYERS])
        b1 = sb("b1", [D, LAYERS])
        wfT = sb("wfT", [D, D])
        bf_rows = sb("bf_rows", [P, D])
        w_l1T = sb("w_l1T", [D, D])
        a_rep = sb("a_rep", [D, D + 1])
        w_aug = sb("w_aug", [D, D + 1])
        wa2_rep = sb("wa2_rep", [D, D])
        w1g = sb("w1g", [D, G, HID])
        w2g = sb("w2g", [D, G, 2, D])
        b1g = sb("b1g", [D, G, 2])
        b2g = sb("b2g", [D, G])
        fw = sb("fw", [D, G])
        gmask = sb("gmask", [R, G, GN])
        eye25 = sb("eye25", [R, GN])
        block_mask = sb("block_mask", [R, GB, GN])
        node_mask = sb("node_mask", [D, G, GN])
        adj25 = sb("adj25", [R, BLK, GN])
        w_rel = sb("w_rel", [D, D])
        w_root = sb("w_root", [D, D])
        b_rel = sb("b_rel", [D, 1])
        gamma = sb("gamma", [D, 1])
        beta = sb("beta", [D, 1])
        neg_half = sb("neg_half", [128, G * BLK])
        wq_now = sb("wq_now", [D, D])
        w1_now = sb("w1_now", [D, D])
        bq_now = sb("bq_now", [D, 1])
        b0_now = sb("b0_now", [D, 1])
        b1_now = sb("b1_now", [D, 1])

        X = sb("X", [P, B, C, D])
        adjT = [sb(f"adjT{a}", [P, C, N]) for a in range(LANES)]
        adjN = [sb(f"adjN{a}", [P, C, N]) for a in range(LANES)]
        xT = [sb(f"xT{a}", [D, N]) for a in range(LANES)]
        qT = sb("qT", [D, N])
        S = sb("S", [P, C, N])
        zaug = [sb(f"zaug{a}", [P, C, D + 1]) for a in range(LANES)]
        ysum = sb("ysum", [P, C, D + 1])
        yrec = sb("yrec", [P, C])
        yn = sb("yn", [P, C, D])
        tT = sb("tT", [D, N])
        uT = sb("uT", [D, N])
        stats = sb("stats", [P, B, 6])
        mv = sb("mv", [P, B, 2])
        var_eps = sb("var_eps", [P, B])
        rstd = sb("rstd", [P, B])
        xn = sb("xn", [P, C, D])
        haug = [sb(f"haug{a}", [P, C, D + 1]) for a in range(LANES)]
        E = [sb(f"E{i}", [P, N]) for i in range(2)]
        PT = [sb(f"PT{i}", [P, C, P]) for i in range(2)]
        rowmax = sb("rowmax", [P, LANES * C])
        negmax = sb("negmax", [P, LANES * C])
        expsum = sb("expsum", [P, LANES * C])
        exprec = sb("exprec", [P, LANES * C])

        L = ctx.enter_context(nc.psum_tensor("L", [128, C, 512], F32))
        Y = ctx.enter_context(nc.psum_tensor("Y", [128, 2, 512], F32))
        Z = ctx.enter_context(nc.psum_tensor("Z", [128, C, D], F32))
        M = ctx.enter_context(nc.psum_tensor("M", [128, 512], F32))

        def y_out(c):
            return Y[0:P, c // 2, (c % 2) * (D + 1):(c % 2 + 1) * (D + 1)]

        consts_loaded = sem("consts_loaded")
        x_loaded = sem("x_loaded")
        adjT_loaded = [sem(f"adjT_loaded{a}") for a in range(LANES)]
        adjN_loaded = [sem(f"adjN_loaded{a}") for a in range(LANES)]
        diag_set = [sem(f"diag_set{a}") for a in range(LANES)]
        half_set = sem("half_set")
        ones_set = sem("ones_set")
        wa_done, wa_ready = sem("wa_done"), sem("wa_ready")
        stats_ready, mv_ready, var_ready = sem("stats_ready"), sem("mv_ready"), sem("var_ready")
        rstd_ready, xn_ready = sem("rstd_ready"), sem("xn_ready")
        lnT_done, lnh_ready = sem("lnT_done"), sem("lnh_ready")
        wq_ready, w1_ready = sem("wq_ready"), sem("w1_ready")
        q_done, qT_ready = sem("q_done"), sem("qT_ready")
        z_done, z_ready = sem("z_done"), sem("z_ready")
        logit_done, sig_ready, S_ready = sem("logit_done"), sem("sig_ready"), sem("S_ready")
        y_done, ysum_ready, yrec_ready, yn_ready = (sem("y_done"), sem("ysum_ready"),
                                                    sem("yrec_ready"), sem("yn_ready"))
        t_done, tT_ready = sem("t_done"), sem("tT_ready")
        w_done, uT_ready, x_ready = sem("w_done"), sem("uT_ready"), sem("x_ready")
        fin_done, x1_part, x1_ready = sem("fin_done"), sem("x1_part"), sem("x1_ready")
        dst_done, h_done, haug_ready = sem("dst_done"), sem("h_done"), sem("haug_ready")
        pen_ready = sem("pen_ready")
        leaky_ready = sem("leaky_ready")
        e_ready, max_ready, negmax_ready = sem("e_ready"), sem("max_ready"), sem("negmax_ready")
        p_ready, pT_done, PT_ready, att_done = (sem("p_ready"), sem("pT_done"), sem("PT_ready"),
                                                sem("att_done"))
        exprec_ready, x2_ready = sem("exprec_ready"), sem("x2_ready")
        dve_passed, pool_passed = sem("dve_passed"), sem("pool_passed")

        const_loads = [
            (ident[:], t["ident"]), (wqT[:], t["wqT"]), (w0T[:], t["w0T"]), (w1T[:], t["w1T"]),
            (bq[:], t["bq"]), (b0[:], t["b0"]), (b1[:], t["b1"]), (wfT[:], t["wfT"]),
            (bf_rows[:], t["bf_rows"]), (w_l1T[:], t["w_l1T"]), (w_aug[:, 0:D], t["w_l1"]),
            (a_rep[:], t["a_rep"]), (w1g[:], t["w1g"]), (w2g[:], t["w2g"]), (b1g[:], t["b1g"]),
            (b2g[:], t["b2g"]), (fw[:], t["fw"]), (gmask[:], t["gmask"]), (eye25[:], t["eye25"]),
            (block_mask[:], t["block_mask"]), (node_mask[:], t["node_mask"]),
            (adj25[:], t["adj25"]), (w_rel[:], t["w_rel"]), (w_root[:], t["w_root"]),
            (b_rel[:], t["b_rel"]), (gamma[:], t["gamma"]), (beta[:], t["beta"]),
        ]
        consts_value = 16 * len(const_loads)
        x_rows = t["x"].rearrange("b (c p) d -> p b c d", p=P)
        adjT_rows = t["adjT"].rearrange("b (c p) n -> p b c n", p=P)
        adjN_rows = t["adj"].rearrange("b (c p) n -> p b c n", p=P)

        def pass_gate(eng, passed):
            eng.sem_inc(passed, 1)

        def chunk(c, width=P):
            return slice(c * width, (c + 1) * width)

        with nc.Block() as block:


            @block.sync
            def _(sp):
                def load_x(p):
                    sp.dma_start(X[:, ds(p * LANES, LANES)], x_rows[:, ds(p * LANES, LANES)])\
                        .then_inc(x_loaded, 16)

                def load_adjT(a, p):
                    sp.dma_start(adjT[a][:], adjT_rows[:, ds(p * LANES + a, 1)]
                                 .rearrange("p b c n -> p (b c) n")).then_inc(adjT_loaded[a], 16)

                def load_adjN(a, p):
                    sp.dma_start(adjN[a][:], adjN_rows[:, ds(p * LANES + a, 1)]
                                 .rearrange("p b c n -> p (b c) n")).then_inc(adjN_loaded[a], 16)

                load_x(0)
                for dst, src in const_loads:
                    sp.dma_start(dst, src).then_inc(consts_loaded, 16)
                for a in range(LANES):
                    load_adjT(a, 0)
                for a in range(LANES):
                    load_adjN(a, 0)
                with sp.Fori(0, PAIRS - 1) as p:
                    sp.wait_ge(x_loaded, 16 * p + 16)
                    load_x(p + 1)
                    for a in range(LANES):
                        sp.wait_ge(S_ready, C * (STEPS * p + STEPS - LANES + a) + C)
                        load_adjT(a, p + 1)
                    for a in range(LANES):
                        sp.wait_ge(max_ready, C * (LANES * p + a) + C)
                        load_adjN(a, p + 1)

            @block.gpsimd
            def _(pool):
                nc.gpsimd.memset(neg_half[:], -0.5).then_inc(half_set, 1)
                for a in range(LANES):
                    nc.gpsimd.memset(zaug[a][:, :, D:D + 1], 1.0).then_inc(ones_set, 1)
                pool.wait_ge(half_set, 1)
                pool.wait_ge(consts_loaded, consts_value)

                def set_diagonal(a, p):
                    pool.wait_ge(adjT_loaded[a], 16 * p + 16)
                    pass_gate(pool, pool_passed)
                    flat = adjT[a][:].rearrange("p c n -> p (c n)")
                    for c in range(C):
                        at = c * N + c * P
                        ins = nc.gpsimd.affine_select(
                            out=flat[:, at:at + P], in_=flat[:, at:at + P],
                            compare_op=ALU.not_equal, fill=1.0, base=0, pattern=[[-1, P]],
                            channel_multiplier=1)
                    ins.then_inc(diag_set[a], 1)

                def pow_ln(k):
                    pool.wait_ge(var_ready, k + 1)
                    nc.gpsimd.tensor_tensor(rstd[:, 0:C], var_eps[:, 0:C], neg_half[0:P, 0:C],
                                            ALU.pow).then_inc(rstd_ready, 1)

                def current_weights(p, l):
                    pool.wait_ge(qT_ready, STEPS * p + LANES * l + FREE)
                    pass_gate(pool, pool_passed)
                    nc.gpsimd.tensor_copy(wq_now[:], wqT[:, ds(l, 1)].rearrange("p l n -> p (l n)"))
                    nc.gpsimd.tensor_copy(bq_now[:], bq[:, ds(l, 1)]).then_inc(wq_ready, 1)
                    pool.wait_ge(uT_ready, STEPS * p + LANES * l + FREE)
                    pass_gate(pool, pool_passed)
                    nc.gpsimd.tensor_copy(w1_now[:], w1T[:, ds(l, 1)].rearrange("p l n -> p (l n)"))
                    nc.gpsimd.tensor_copy(b0_now[:], b0[:, ds(l, 1)])
                    nc.gpsimd.tensor_copy(b1_now[:], b1[:, ds(l, 1)]).then_inc(w1_ready, 1)

                with pool.Fori(0, PAIRS) as p:
                    for a in range(LANES):
                        pow_ln(2 * LANES * p + a)
                        set_diagonal(a, p)
                    with pool.Fori(0, LAYERS) as l:
                        current_weights(p, l)
                    for a in range(LANES):
                        pow_ln(2 * LANES * p + LANES + a)

            @block.tensor
            def _(pe):
                mm = nc.tensor.matmul
                pe.sem_inc(lnT_done, FREE)

                pe.wait_ge(consts_loaded, consts_value)
                mm(M[:, 0:D + 1], w_l1T[:], a_rep[:], start=True, stop=True).then_inc(wa_done, 1)
                pe.wait_ge(wa_ready, 1)

                def ln_transpose(k):
                    pe.wait_ge(xn_ready, k + 1)
                    for c in range(C):
                        ins = nc.tensor.transpose(M[:, chunk(c)], xn[:, c, :], ident[0:P, 0:P])
                    ins.then_inc(lnT_done, 1)

                def q_and_z(a, p, l):
                    n = STEPS * p + LANES * l + a
                    w0_layer = w0T[:, ds(l, 1)].rearrange("p l n -> p (l n)")
                    if a == 0:
                        pe.wait_ge(wq_ready, LAYERS * p + l + 1)
                    mm(M[:, 0:N], wq_now[:], xT[a][:], start=True, stop=True).then_inc(q_done, 1)
                    pe.wait_ge(z_ready, n + FREE)
                    for c in range(C):
                        ins = mm(Z[0:P, c, :], xT[a][:, chunk(c)], w0_layer, start=True, stop=True)
                    ins.then_inc(z_done, 1)

                def logits(a, p, l, c):
                    n = STEPS * p + LANES * l + a
                    if c == 0:
                        pe.wait_ge(qT_ready, n + 1 + FREE)
                    mm(L[0:P, c, 0:N], xT[a][:, chunk(c)], qT[:], start=True, stop=True)\
                        .then_inc(logit_done, 1)

                def y_sum(a, p, l):
                    n = STEPS * p + LANES * l + a
                    pe.wait_ge(z_ready, n + 1 + FREE)
                    pe.wait_ge(S_ready, C * n + C)
                    for ic in range(C):
                        for jc in range(C):
                            ins = mm(y_out(ic), S[:, jc, chunk(ic)], zaug[a][:, jc, :],
                                     start=(jc == 0), stop=(jc == C - 1))
                        if ic % 2:
                            ins.then_inc(y_done, 1)

                def y_transpose(a, p, l):
                    n = STEPS * p + LANES * l + a
                    pe.wait_ge(yn_ready, 2 * n + 2)
                    for c in range(C):
                        ins = nc.tensor.transpose(M[:, chunk(c)], yn[:, c, :], ident[0:P, 0:P])
                    ins.then_inc(t_done, 1)

                def second_linear(a, p, l):
                    n = STEPS * p + LANES * l + a
                    pe.wait_ge(w1_ready, LAYERS * p + l + 1)
                    pe.wait_ge(tT_ready, n + 1)
                    mm(M[:, 0:N], w1_now[:], tT[:], start=True, stop=True).then_inc(w_done, 1)

                def lane0_logits(p, l, before):
                    logits(0, p, l, 0)
                    if before:
                        y_transpose(1, p, l - 1)
                    logits(0, p, l, 1)
                    if before:
                        second_linear(1, p, l - 1)
                    logits(0, p, l, 2)
                    logits(0, p, l, 3)

                def layer(p, l, before):
                    if before:
                        pe.wait_ge(x_ready, STEPS * p + LANES * l - 1)
                    q_and_z(0, p, l)
                    if before:
                        y_sum(1, p, l - 1)
                    lane0_logits(p, l, before)
                    if before:
                        pe.wait_ge(x_ready, STEPS * p + LANES * l)
                    q_and_z(1, p, l)
                    y_sum(0, p, l)
                    logits(1, p, l, 0)
                    y_transpose(0, p, l)
                    logits(1, p, l, 1)
                    second_linear(0, p, l)
                    logits(1, p, l, 2)
                    logits(1, p, l, 3)

                def final_linear(a, p):
                    pe.wait_ge(x_ready, STEPS * p + STEPS - 1 + a)
                    if a == 1:
                        pe.wait_ge(x1_part, LANES * p + 1)
                    for c in range(C):
                        ins = mm(Z[0:P, c, :], xT[a][:, chunk(c)], wfT[:], start=True, stop=True)
                    ins.then_inc(fin_done, 1)

                def gnn1_linear(a, p):
                    m = LANES * p + a
                    pe.wait_ge(lnh_ready, 2 * LANES * p + LANES + a + 1)
                    mm(L[:, a, 0:N], wa2_rep[:], xT[a][:], start=True, stop=True)\
                        .then_inc(dst_done, 1)
                    pe.wait_ge(haug_ready, m + FREE)
                    for c in range(C):
                        ins = mm(y_out(c), xT[a][:, chunk(c)], w_aug[:], start=True, stop=True)
                    ins.then_inc(h_done, 1)

                def probs_transpose(a, p, c):
                    k = C * (LANES * p + a) + c
                    pe.wait_ge(p_ready, k + 1)
                    if a or c >= 2:
                        pe.wait_ge(PT_ready, k - 1)
                    for jc in range(C):
                        ins = nc.tensor.transpose(L[0:P, 2 + c % 2, chunk(jc)],
                                                  E[c % 2][:, chunk(jc)], ident[0:P, 0:P])
                    ins.then_inc(pT_done, 1)

                def attend(a, p, c):
                    k = C * (LANES * p + a) + c
                    pe.wait_ge(PT_ready, k + 1)
                    o = Z[0:P, c, :] if a == 0 else M[0:P, chunk(c, D)]
                    for jc in range(C):
                        ins = mm(o, PT[c % 2][:, jc, :], haug[a][:, jc, 0:D],
                                 start=(jc == 0), stop=(jc == C - 1))
                    ins.then_inc(att_done, 1)

                with pe.Fori(0, PAIRS) as p:
                    pe.wait_ge(x2_ready, LANES * p + FREE)
                    ln_transpose(2 * LANES * p)
                    pe.wait_ge(lnh_ready, 2 * LANES * p + 1)
                    ln_transpose(2 * LANES * p + 1)
                    pe.wait_ge(lnh_ready, 2 * LANES * p + 2)
                    layer(p, 0, False)
                    with pe.Fori(1, LAYERS) as l:
                        layer(p, l, True)
                    y_sum(1, p, LAYERS - 1)
                    final_linear(0, p)
                    y_transpose(1, p, LAYERS - 1)
                    second_linear(1, p, LAYERS - 1)
                    final_linear(1, p)
                    ln_transpose(2 * LANES * p + 2)
                    gnn1_linear(0, p)
                    ln_transpose(2 * LANES * p + 3)
                    gnn1_linear(1, p)
                    pe.wait_ge(haug_ready, LANES * p + 1 + FREE)
                    steps = [(a, c) for a in range(LANES) for c in range(C)]
                    for i, (a, c) in enumerate(steps):
                        probs_transpose(a, p, c)
                        if i:
                            attend(steps[i - 1][0], p, steps[i - 1][1])
                        if (a, c) == (1, 0):
                            pe.wait_ge(haug_ready, LANES * p + 2 + FREE)
                    attend(1, p, C - 1)

            @block.scalar
            def _(act):
                fn = nc.scalar.activation
                act.sem_inc(qT_ready, FREE)
                act.sem_inc(uT_ready, FREE)
                act.wait_ge(consts_loaded, consts_value)

                def ln_relu(k, a):
                    act.wait_ge(lnT_done, k + 1 + FREE)
                    fn(xT[a][:], M[:, 0:N], ACT.Relu).then_inc(lnh_ready, 1)

                def q_out(a, p, l):
                    n = STEPS * p + LANES * l + a
                    act.wait_ge(q_done, n + 1)
                    fn(qT[:], M[:, 0:N], ACT.Identity, bias=bq_now[:]).then_inc(qT_ready, 1)

                def sigmoid(a, p, l, c):
                    n = STEPS * p + LANES * l + a
                    act.wait_ge(logit_done, C * n + c + 1)
                    fn(S[:, c, :], L[0:P, c, 0:N], ACT.Sigmoid).then_inc(sig_ready, 1)

                def t_out(a, p, l):
                    n = STEPS * p + LANES * l + a
                    act.wait_ge(w1_ready, LAYERS * p + l + 1)
                    act.wait_ge(t_done, n + 1)
                    fn(tT[:], M[:, 0:N], ACT.Relu, bias=b0_now[:]).then_inc(tT_ready, 1)

                def u_out(a, p, l):
                    n = STEPS * p + LANES * l + a
                    act.wait_ge(w_done, n + 1)
                    fn(uT[:], M[:, 0:N], ACT.Relu, bias=b1_now[:]).then_inc(uT_ready, 1)

                def layer(p, l, before):
                    q_out(0, p, l)
                    sigmoid(0, p, l, 0)
                    if before:
                        t_out(1, p, l - 1)
                    sigmoid(0, p, l, 1)
                    if before:
                        u_out(1, p, l - 1)
                    sigmoid(0, p, l, 2)
                    sigmoid(0, p, l, 3)
                    q_out(1, p, l)
                    sigmoid(1, p, l, 0)
                    t_out(0, p, l)
                    sigmoid(1, p, l, 1)
                    u_out(0, p, l)
                    sigmoid(1, p, l, 2)
                    sigmoid(1, p, l, 3)

                def scores(a, p, c):
                    k = C * (LANES * p + a) + c
                    if c == 0:
                        act.wait_ge(dst_done, LANES * p + a + 1)
                        act.wait_ge(haug_ready, LANES * p + a + 1 + FREE)
                    if a or c >= 2:
                        act.wait_ge(pT_done, k - 1)
                    fn(E[c % 2][:], L[0:P, a, 0:N], ACT.Identity, bias=haug[a][:, c, D:D + 1])\
                        .then_inc(e_ready, 1)

                def exp(a, p, c):
                    k = C * (LANES * p + a) + c
                    act.wait_ge(negmax_ready, k + 1)
                    i = C * a + c
                    fn(E[c % 2][:], E[c % 2][:], ACT.Exp, bias=negmax[:, i:i + 1],
                       accum_out=expsum[:, i:i + 1]).then_inc(p_ready, 1)

                def probs_out(a, p, c):
                    k = C * (LANES * p + a) + c
                    act.wait_ge(pT_done, k + 1)
                    if a or c >= 2:
                        act.wait_ge(att_done, k - 1)
                    fn(PT[c % 2][:].rearrange("p c i -> p (c i)"), L[0:P, 2 + c % 2, 0:N],
                       ACT.Copy).then_inc(PT_ready, 1)

                with act.Fori(0, PAIRS) as p:
                    for a in range(LANES):
                        ln_relu(2 * LANES * p + a, a)
                    layer(p, 0, False)
                    with act.Fori(1, LAYERS) as l:
                        layer(p, l, True)
                    t_out(1, p, LAYERS - 1)
                    u_out(1, p, LAYERS - 1)
                    for a in range(LANES):
                        ln_relu(2 * LANES * p + LANES + a, a)
                    steps = [(a, c) for a in range(LANES) for c in range(C)]
                    scores(0, p, 0)
                    for i, (a, c) in enumerate(steps):
                        if i + 1 < len(steps):
                            scores(steps[i + 1][0], p, steps[i + 1][1])
                        exp(a, p, c)
                        if i:
                            probs_out(steps[i - 1][0], p, steps[i - 1][1])
                    probs_out(1, p, C - 1)

            @block.vector
            def _(dve):
                tt, ts, stt = (nc.vector.tensor_tensor, nc.vector.tensor_scalar,
                               nc.vector.scalar_tensor_tensor)
                for ready in (z_ready, x2_ready, haug_ready):
                    dve.sem_inc(ready, FREE)
                dve.wait_ge(consts_loaded, consts_value)
                dve.wait_ge(wa_done, 1)
                nc.vector.tensor_copy(wa2_rep[:], M[:, 0:D]).then_inc(wa_ready, 1)
                nc.vector.tensor_copy(w_aug[:, D:D + 1], M[:, D:D + 1]).then_inc(wa_ready, 1)
                dve.wait_ge(ones_set, LANES)

                def layer_norm(k, b):
                    pass_gate(dve, dve_passed)
                    for c in range(C):
                        ins = nc.vector.bn_stats(
                            stats[:, c, :], X[:, ds(b, 1), c, :].rearrange("p b d -> p (b d)"))
                    ins.then_inc(stats_ready, 1)
                    dve.wait_ge(stats_ready, k + 1)
                    pass_gate(dve, dve_passed)
                    for c in range(C):
                        ins = nc.vector.bn_aggr(mv[:, c, :], stats[:, c, :])
                    ins.then_inc(mv_ready, 1)
                    dve.wait_ge(mv_ready, k + 1)
                    ts(var_eps[:, 0:C], mv[:, 0:C, 1], EPS_LN, None, ALU.add)\
                        .then_inc(var_ready, 1)

                def normalise(k, b):
                    dve.wait_ge(rstd_ready, k + 1)
                    dve.wait_ge(lnT_done, k + FREE)
                    for c in range(C):
                        ins = ts(xn[:, c, :], X[:, ds(b, 1), c, :].rearrange("p b d -> p (b d)"),
                                 mv[:, c, 0:1], rstd[:, c:c + 1], ALU.subtract, ALU.mult)
                    ins.then_inc(xn_ready, 1)

                def z_out(a, p, l):
                    n = STEPS * p + LANES * l + a
                    dve.wait_ge(z_done, n + 1)
                    nc.vector.tensor_copy(zaug[a][:, :, 0:D], Z[0:P, :, :]).then_inc(z_ready, 1)

                def mask(a, p, l, c):
                    n = STEPS * p + LANES * l + a
                    dve.wait_ge(sig_ready, C * n + c + 1)
                    tt(S[:, c, :], S[:, c, :], adjT[a][:, c, :], ALU.mult).then_inc(S_ready, 1)

                def y_norm(a, p, l):
                    n = STEPS * p + LANES * l + a
                    w = D + 1
                    for h in range(2):
                        dve.wait_ge(y_done, 2 * n + h + 1)
                        stt(ysum[:, 2 * h:2 * h + 2, :],
                            zaug[a][:, 2 * h:2 * h + 2, :], EPS_EYE,
                            Y[0:P, h, 0:2 * w].rearrange("p (c w) -> p c w", w=w),
                            ALU.mult, ALU.add).then_inc(ysum_ready, 1)
                        dve.wait_ge(ysum_ready, 2 * n + h + 1)
                        nc.vector.reciprocal(yrec[:, 2 * h:2 * h + 2], ysum[:, 2 * h:2 * h + 2, D])\
                            .then_inc(yrec_ready, 1)
                        dve.wait_ge(yrec_ready, 2 * n + h + 1)
                        for c in range(2 * h, 2 * h + 2):
                            ins = ts(yn[:, c, :], ysum[:, c, 0:D], yrec[:, c:c + 1], None,
                                     ALU.mult)
                        ins.then_inc(yn_ready, 1)

                def x_add(a, p, l):
                    n = STEPS * p + LANES * l + a
                    dve.wait_ge(uT_ready, n + 1 + FREE)
                    tt(xT[a][:], xT[a][:], uT[:], ALU.add).then_inc(x_ready, 1)

                def layer(p, l, before):
                    z_out(0, p, l)
                    if before:
                        y_norm(1, p, l - 1)
                    mask(0, p, l, 0)
                    mask(0, p, l, 1)
                    if before:
                        x_add(1, p, l - 1)
                    mask(0, p, l, 2)
                    mask(0, p, l, 3)
                    z_out(1, p, l)
                    y_norm(0, p, l)
                    mask(1, p, l, 0)
                    mask(1, p, l, 1)
                    x_add(0, p, l)
                    mask(1, p, l, 2)
                    mask(1, p, l, 3)

                def final_add(a, p):
                    m = LANES * p + a
                    x = X[:, ds(m, 1), :, :].rearrange("p b c d -> p (b c) d")
                    dve.wait_ge(fin_done, m + 1)
                    tt(x, x, Z[0:P, :, :], ALU.add).then_inc(x1_part, 1)
                    dve.wait_ge(x1_part, m + 1)
                    tt(x, x, bf_rows[:].rearrange("p (c d) -> p c d", c=1)
                       .to_broadcast([P, C, D]), ALU.add).then_inc(x1_ready, 1)
                    dve.wait_ge(x1_ready, m + 1)

                def penalties(a, p):
                    dve.wait_ge(adjN_loaded[a], 16 * p + 16)
                    ts(adjN[a][:], adjN[a][:], 0.0, NEG_INF, ALU.is_le, ALU.mult)\
                        .then_inc(pen_ready, 1)

                def haug_out(a, p):
                    m = LANES * p + a
                    dve.wait_ge(h_done, m + 1)
                    nc.vector.tensor_copy(
                        haug[a][:].rearrange("p (h c) w -> p h (c w)", h=2),
                        Y[0:P, :, 0:2 * (D + 1)]).then_inc(haug_ready, 1)

                def masked_max(a, p, c):
                    k = C * (LANES * p + a) + c
                    i = C * a + c
                    dve.wait_ge(e_ready, k + 1)
                    stt(E[c % 2][:], E[c % 2][:], SLOPE, E[c % 2][:], ALU.mult, ALU.max)\
                        .then_inc(leaky_ready, 1)
                    dve.wait_ge(leaky_ready, k + 1)
                    pass_gate(dve, dve_passed)
                    nc.vector.tensor_tensor_reduce(
                        out=E[c % 2][:], in0=E[c % 2][:], in1=adjN[a][:, c, :], scale=1.0,
                        scalar=-3.0e38, op0=ALU.add, op1=ALU.max,
                        accum_out=rowmax[:, i:i + 1]).then_inc(max_ready, 1)
                    dve.wait_ge(max_ready, k + 1)
                    ts(negmax[:, i:i + 1], rowmax[:, i:i + 1], -1.0, None, ALU.mult)\
                        .then_inc(negmax_ready, 1)

                def attention_add(a, p):
                    m = LANES * p + a
                    dve.wait_ge(p_ready, C * m + C)
                    nc.vector.reciprocal(exprec[:, chunk(a, C)], expsum[:, chunk(a, C)])\
                        .then_inc(exprec_ready, 1)
                    dve.wait_ge(exprec_ready, m + 1)
                    dve.wait_ge(att_done, C * m + C)
                    for c in range(C):
                        x = X[:, ds(m, 1), c, :].rearrange("p b d -> p (b d)")
                        o = Z[0:P, c, :] if a == 0 else M[0:P, chunk(c, D)]
                        ins = stt(x, o, exprec[:, C * a + c:C * a + c + 1], x, ALU.mult, ALU.add)
                    ins.then_inc(x2_ready, 1)

                with dve.Fori(0, PAIRS) as p:
                    dve.wait_ge(x_loaded, 16 * p + 16)
                    for a in range(LANES):
                        layer_norm(2 * LANES * p + a, LANES * p + a)
                        normalise(2 * LANES * p + a, LANES * p + a)
                    dve.wait_ge(diag_set[0], p + 1)
                    dve.wait_ge(diag_set[1], p + 1)
                    layer(p, 0, False)
                    with dve.Fori(1, LAYERS) as l:
                        layer(p, l, True)
                    y_norm(1, p, LAYERS - 1)
                    final_add(0, p)
                    layer_norm(2 * LANES * p + 2, LANES * p)
                    normalise(2 * LANES * p + 2, LANES * p)
                    x_add(1, p, LAYERS - 1)
                    penalties(0, p)
                    final_add(1, p)
                    layer_norm(2 * LANES * p + 3, LANES * p + 1)
                    haug_out(0, p)
                    normalise(2 * LANES * p + 3, LANES * p + 1)
                    penalties(1, p)
                    dve.wait_ge(pen_ready, LANES * p + 2)
                    steps = [(a, c) for a in range(LANES) for c in range(C)]
                    for i, (a, c) in enumerate(steps):
                        masked_max(a, p, c)
                        if i == 0:
                            haug_out(1, p)
                        if (a, c) == (1, 2):
                            attention_add(0, p)
                    attention_add(1, p)
        GQ = G * BLK
        adj_self = sb("adj_self", [R, BLK, G, GN])
        deg = sb("deg", [R, GQ])
        dinv = sb("dinv", [R, GQ])
        is_zero = sb("is_zero", [R, GQ])
        not_zero = sb("not_zero", [R, GQ])
        adj_blocks = sb("adj_blocks", [R, GQ, R])
        normT = sb("normT", [R, GQ, R])
        xn25 = sb("xn25", [GN, B, D])
        h25T = sb("h25T", [D, B * GN])
        sup1 = sb("sup1", [R, BLK, HID])
        hidT = sb("hidT", [D, 2, B * GN])
        sup2 = sb("sup2", [R, BLK, D])
        gout = sb("gout", [D, B * GN])
        fused = sb("fused", [D, B * GN])
        fsum = sb("fsum", [D, 4])
        fexp = sb("fexp", [D, G])
        wmask = sb("wmask", [D, G, GN])

        l2_step = sem("l2_step")
        deg_ready, dinv_ready = sem("deg_ready"), sem("dinv_ready")
        blocks_ready, adjTr_done, normT_ready = (sem("blocks_ready"), sem("adjTr_done"),
                                                 sem("normT_ready"))
        fmax_ready, fexp_ready = sem("fmax_ready"), sem("fexp_ready")
        var25_ready, rstd25_ready, xn25_ready = (sem("var25_ready"), sem("rstd25_ready"),
                                                 sem("xn25_ready"))
        x25T_done, h25_ready = sem("x25T_done"), sem("h25_ready")
        sup1_done, sup1_ready = sem("sup1_done"), sem("sup1_ready")
        hid_done, hid_ready = sem("hid_done"), sem("hid_ready")
        sup2_done, sup2_ready = sem("sup2_done"), sem("sup2_ready")
        gout_done, gout_ready, fused_ready = sem("gout_done"), sem("gout_ready"), sem("fused_ready")
        back_done, x3_ready = sem("back_done"), sem("x3_ready")
        adj3 = [adjT[0], adjT[1], adjN[0], adjN[1]]
        adj3_loaded = [sem(f"adj3_loaded{i}") for i in range(4)]

        def load_adj3(sp, i, b):
            sp.dma_start(adj3[i][:], adjT_rows[:, ds(b, 1)].rearrange("p b c n -> p (b c) n"))\
                .then_inc(adj3_loaded[i], 16)

        def rows(q):
            return slice(q * R, (q + 1) * R)

        with nc.Block() as block:

            @block.sync
            def _(sp):
                sp.wait_ge(S_ready, C * STEPS * PAIRS)
                sp.wait_ge(max_ready, C * B)
                for i in range(4):
                    load_adj3(sp, i, i)

            @block.gpsimd
            def _(pool):
                pool.wait_ge(deg_ready, 1)
                nc.gpsimd.tensor_tensor(dinv[:], deg[:], neg_half[0:R, 0:GQ], ALU.pow)\
                    .then_inc(dinv_ready, 1)
                pool.wait_ge(var25_ready, 1)
                nc.gpsimd.tensor_tensor(rstd[0:GN, :], var_eps[0:GN, :], neg_half[0:GN, 0:B],
                                        ALU.pow).then_inc(rstd25_ready, 1)

            @block.tensor
            def _(pe):
                mm = nc.tensor.matmul
                pe.wait_ge(blocks_ready, 1)
                pe.wait_ge(x2_ready, B + FREE)
                for i in range(GQ):
                    ins = nc.tensor.transpose(L[0:R, i // G, (i % G) * R:(i % G + 1) * R],
                                              adj_blocks[:, i, :], ident[0:R, 0:R])
                ins.then_inc(adjTr_done, 1)
                pe.wait_ge(xn25_ready, 1)
                for b in range(B):
                    ins = nc.tensor.transpose(M[:, b * GN:(b + 1) * GN], xn25[:, b, :],
                                              ident[0:GN, 0:GN])
                ins.then_inc(x25T_done, 1)
                pe.wait_ge(h25_ready, 1)

                def support1(g):
                    if g:
                        pe.wait_ge(sup1_ready, g)
                    for q in range(BLK):
                        ins = mm(Y[0:R, q // 2, (q % 2) * HID:(q % 2 + 1) * HID],
                                 h25T[:, rows(q)], w1g[:, g, :], start=True, stop=True)
                    ins.then_inc(sup1_done, 1)

                support1(0)
                pe.wait_ge(normT_ready, 1)
                for g in range(G):
                    pe.wait_ge(sup1_ready, g + 1)
                    for f in range(2):
                        for q in range(BLK):
                            ins = mm(L[:, f, rows(q)], sup1[:, q, f * D:(f + 1) * D],
                                     normT[:, q * G + g, :], start=True, stop=True)
                    ins.then_inc(hid_done, 1)
                    if g + 1 < G:
                        support1(g + 1)
                    pe.wait_ge(hid_ready, g + 1)
                    for q in range(BLK):
                        for f in range(2):
                            ins = mm(Z[0:R, q, :], hidT[:, f, rows(q)], w2g[:, g, f, :],
                                     start=(f == 0), stop=(f == 1))
                    ins.then_inc(sup2_done, 1)
                    pe.wait_ge(sup2_ready, g + 1)
                    if g:
                        pe.wait_ge(gout_ready, g)
                    for q in range(BLK):
                        ins = mm(M[:, rows(q)], sup2[:, q, :], normT[:, q * G + g, :],
                                 start=True, stop=True)
                    ins.then_inc(gout_done, 1)
                pe.wait_ge(fused_ready, G)
                for b in range(B):
                    ins = nc.tensor.transpose(L[0:GN, b // 4, (b % 4) * D:(b % 4 + 1) * D],
                                              fused[:, b * GN:(b + 1) * GN], ident[:])
                ins.then_inc(back_done, 1)

            @block.scalar
            def _(act):
                fn = nc.scalar.activation
                act.wait_ge(fmax_ready, 1)
                fn(fexp[:], fw[:], ACT.Exp, bias=fsum[:, 1:2], accum_out=fsum[:, 2:3])\
                    .then_inc(fexp_ready, 1)
                act.wait_ge(x25T_done, 1)
                fn(h25T[:], M[:, 0:B * GN], ACT.Relu).then_inc(h25_ready, 1)
                for g in range(G):
                    act.wait_ge(hid_done, g + 1)
                    for f in range(2):
                        ins = fn(hidT[:, f, :], L[:, f, 0:B * GN], ACT.Relu,
                                 bias=b1g[:, g, f:f + 1])
                    ins.then_inc(hid_ready, 1)
                    act.wait_ge(gout_done, g + 1)
                    if g:
                        act.wait_ge(fused_ready, g)
                    fn(gout[:], M[:, 0:B * GN], ACT.Relu, bias=b2g[:, g:g + 1])\
                        .then_inc(gout_ready, 1)

            @block.vector
            def _(dve):
                tt, ts, stt = (nc.vector.tensor_tensor, nc.vector.tensor_scalar,
                               nc.vector.scalar_tensor_tensor)
                steps = [0]

                def link(ins):
                    steps[0] += 1
                    ins.then_inc(l2_step, 1)
                    dve.wait_ge(l2_step, steps[0])

                link(nc.vector.reduce_max(fsum[:, 0:1], fw[:], AX_X))
                ts(fsum[:, 1:2], fsum[:, 0:1], -1.0, None, ALU.mult).then_inc(fmax_ready, 1)
                for b in range(B):
                    ins = nc.vector.bn_stats(stats[0:GN, b, :], X[0:GN, b, 0, :])
                link(ins)
                for b in range(B):
                    ins = nc.vector.bn_aggr(mv[0:GN, b, :], stats[0:GN, b, :])
                link(ins)
                ts(var_eps[0:GN, :], mv[0:GN, :, 1], EPS_LN, None, ALU.add)\
                    .then_inc(var25_ready, 1)
                for q in range(BLK):
                    ins = tt(adj_self[:, q], adj25[:, q:q + 1, :].to_broadcast([R, G, GN]),
                             eye25[:].rearrange("p (g m) -> p g m", g=1).to_broadcast([R, G, GN]),
                             ALU.add)
                link(ins)
                for q in range(BLK):
                    ins = tt(adj_self[:, q], adj_self[:, q], gmask[:], ALU.mult)
                link(ins)
                link(nc.vector.reduce_sum(deg[:], adj_self[:].rearrange("p q g m -> p (q g) m"),
                                          AX_X))
                ts(is_zero[:], deg[:], 0.0, None, ALU.is_equal)
                link(ts(not_zero[:], deg[:], 0.0, None, ALU.not_equal))
                tt(deg[:], deg[:], is_zero[:], ALU.add).then_inc(deg_ready, 1)
                dve.wait_ge(dinv_ready, 1)
                link(tt(dinv[:], dinv[:], not_zero[:], ALU.mult))
                flat = adj_self[:].rearrange("p q g m -> p (q g) m")
                per_row = dinv[:].rearrange("p (i o) -> p i o", o=1)
                link(tt(flat, flat, per_row.to_broadcast([R, GQ, GN]), ALU.mult))
                for i in range(GQ):
                    ins = tt(adj_blocks[:, i, :].rearrange("p (k m) -> p k m", k=GB),
                             flat[:, i:i + 1, :].to_broadcast([R, GB, GN]), block_mask[:],
                             ALU.mult)
                ins.then_inc(blocks_ready, 1)
                dve.wait_ge(rstd25_ready, 1)
                for b in range(B):
                    ins = ts(xn25[:, b, :], X[0:GN, b, 0, :], mv[0:GN, b, 0:1],
                             rstd[0:GN, b:b + 1], ALU.subtract, ALU.mult)
                ins.then_inc(xn25_ready, 1)
                dve.wait_ge(adjTr_done, 1)
                for q in range(BLK):
                    ins = tt(normT[:, q * G:(q + 1) * G, :],
                             L[0:R, q, 0:G * R].rearrange("p (g n) -> p g n", g=G),
                             per_row[:, q * G:(q + 1) * G, :].to_broadcast([R, G, R]), ALU.mult)
                ins.then_inc(normT_ready, 1)
                dve.wait_ge(fexp_ready, 1)
                link(nc.vector.reciprocal(fsum[:, 3:4], fsum[:, 2:3]))
                link(ts(fexp[:], fexp[:], fsum[:, 3:4], None, ALU.mult))
                for g in range(G):
                    ins = ts(wmask[:, g, :], node_mask[:, g, :], fexp[:, g:g + 1], None, ALU.mult)
                link(ins)

                def add_group(g):
                    wm = wmask[:, g:g + 1, :].to_broadcast([D, B, GN])
                    rows_of = gout[:].rearrange("p (b n) -> p b n", b=B)
                    fused_of = fused[:].rearrange("p (b n) -> p b n", b=B)
                    dve.wait_ge(gout_ready, g + 1)
                    if g == 0:
                        link(tt(fused_of, rows_of, wm, ALU.mult))
                    else:
                        link(tt(rows_of, rows_of, wm, ALU.mult))
                        link(tt(fused[:], fused[:], gout[:], ALU.add))
                    dve.sem_inc(fused_ready, 1)

                for g in range(G):
                    dve.wait_ge(sup1_done, g + 1)
                    nc.vector.tensor_copy(sup1[:].rearrange("p (h q) e -> p h (q e)", h=2),
                                          Y[0:R, :, :]).then_inc(sup1_ready, 1)
                    if g:
                        add_group(g - 1)
                    dve.wait_ge(sup2_done, g + 1)
                    nc.vector.tensor_copy(sup2[:], Z[0:R, :, :]).then_inc(sup2_ready, 1)
                add_group(G - 1)
                for i in range(4):
                    dve.wait_ge(back_done, 1)
                    x = X[0:GN, 4 * i:4 * i + 4, 0, :]
                    tt(x, x, L[0:GN, i, :].rearrange("p (b d) -> p b d", b=4), ALU.add)\
                        .then_inc(x3_ready, 1)

        SLOTS = 4
        TURNS = B // SLOTS
        var3 = [sb(f"var3_{i}", [P, C]) for i in range(2)]
        rstd3 = [sb(f"rstd3_{i}", [P, C]) for i in range(2)]
        mv3 = [sb(f"mv3_{i}", [P, C, 2]) for i in range(2)]
        st3 = sb("st3", [P, C, 6])
        st_h = sb("st_h", [P, C, 6])
        mv_h = sb("mv_h", [P, C, 2])
        var_h = sb("var_h", [P, C])
        rstd_h = sb("rstd_h", [P, C])
        h1 = [sb(f"h1_{i}", [P, C, D]) for i in range(2)]
        xh = [sb(f"xh_{i}", [P, C, D]) for i in range(2)]
        hn = sb("hn", [P, C, D])
        hT = sb("hT", [D, N])
        hw = sb("hw", [P, C, D])
        cT = sb("cT", [D, N])
        ob = [sb(f"ob_{i}", [P, C, D]) for i in range(2)]

        st3_ready, mv3_ready, var3_ready, rstd3_ready = (sem("st3_ready"), sem("mv3_ready"),
                                                         sem("var3_ready"), sem("rstd3_ready"))
        xn3_ready, h1_ready, xh_ready = sem("xn3_ready"), sem("h1_ready"), sem("xh_ready")
        sth_ready, mvh_ready, varh_ready, rstdh_ready = (sem("sth_ready"), sem("mvh_ready"),
                                                         sem("varh_ready"), sem("rstdh_ready"))
        hn_ready, hnT_done, hT_ready = sem("hn_ready"), sem("hnT_done"), sem("hT_ready")
        hw_done, hw_ready, conv_done, cT_ready = (sem("hw_done"), sem("hw_ready"),
                                                  sem("conv_done"), sem("cT_ready"))
        cback_done, out_ready = sem("cback_done"), sem("out_ready")
        out_stored = [sem(f"out_stored{i}") for i in range(2)]
        out_rows = out.rearrange("b (c p) d -> p b c d", p=P)
        conv_out = [L[:, 0, 0:N], L[:, 1, 0:N]]
        back_out = [Y[0:P, 0, :].rearrange("p (c d) -> p c d", c=C),
                    Y[0:P, 1, :].rearrange("p (c d) -> p c d", c=C)]

        def turns(eng, body):
            body(0, True, False)
            with eng.Fori(1, TURNS - 1) as u:
                body(u, False, False)
            body(TURNS - 1, False, True)

        with nc.Block() as block:

            @block.sync
            def _(sp):
                def store(m, i):
                    sp.wait_ge(out_ready, m + 1)
                    sp.dma_start(out_rows[:, ds(m, 1)].rearrange("p b c d -> p (b c) d"),
                                 ob[i % 2][:]).then_inc(out_stored[i % 2], 16)

                def body(u, first, last):
                    for i in range(SLOTS):
                        m = SLOTS * u + i
                        if not (first and i == 0):
                            store(m - 1, i - 1)
                        if not last:
                            sp.wait_ge(conv_done, m + 1)
                            load_adj3(sp, i, m + SLOTS)

                turns(sp, body)
                store(B - 1, SLOTS - 1)
                for i in range(2):
                    sp.wait_ge(out_stored[i], 16 * (B // 2))

            @block.gpsimd
            def _(pool):
                def pow_x(m, i):
                    pool.wait_ge(var3_ready, m + 1)
                    nc.gpsimd.tensor_tensor(rstd3[i % 2][:], var3[i % 2][:], neg_half[0:P, 0:C],
                                            ALU.pow).then_inc(rstd3_ready, 1)

                def pow_h(m):
                    pool.wait_ge(varh_ready, m + 1)
                    nc.gpsimd.tensor_tensor(rstd_h[:], var_h[:], neg_half[0:P, 0:C],
                                            ALU.pow).then_inc(rstdh_ready, 1)

                def add_xh(m, i, first):
                    pool.wait_ge(h1_ready, m + 1)
                    if not first:
                        pool.wait_ge(out_ready, m - 1)
                    nc.gpsimd.tensor_tensor(
                        xh[i % 2][:], h1[i % 2][:],
                        X[:, ds(m, 1), :, :].rearrange("p b c d -> p (b c) d"), ALU.add)\
                        .then_inc(xh_ready, 1)

                pow_x(0, 0)
                pow_x(1, 1)
                pow_h(0)
                add_xh(0, 0, True)

                def body(u, first, last):
                    for i in range(SLOTS):
                        m = SLOTS * u + i
                        if not (last and i >= SLOTS - 2):
                            pow_x(m + 2, i)
                        if not (last and i == SLOTS - 1):
                            pow_h(m + 1)
                            add_xh(m + 1, i + 1, first and i == 0)

                turns(pool, body)

            @block.tensor
            def _(pe):
                mm = nc.tensor.matmul

                def back(m, i):
                    pe.wait_ge(cT_ready, m + 1)
                    for c in range(C):
                        ins = nc.tensor.transpose(back_out[i % 2][:, c, :], cT[:, chunk(c)],
                                                  ident[:])
                    ins.then_inc(cback_done, 1)

                def body(u, first, last):
                    for i in range(SLOTS):
                        m = SLOTS * u + i
                        pe.wait_ge(hn_ready, m + 1)
                        for c in range(C):
                            ins = nc.tensor.transpose(M[:, chunk(c)], hn[:, c, :],
                                                      ident[0:P, 0:P])
                        ins.then_inc(hnT_done, 1)
                        if not (first and i == 0):
                            back(m - 1, i - 1)
                        pe.wait_ge(hT_ready, m + 1)
                        for c in range(C):
                            ins = mm(Z[0:P, c, :], hT[:, chunk(c)], w_rel[:], start=True,
                                     stop=True)
                        ins.then_inc(hw_done, 1)
                        mm(conv_out[i % 2], w_root[:], hT[:], start=True, stop=False)
                        pe.wait_ge(hw_ready, m + 1)
                        pe.wait_ge(adj3_loaded[i], 16 * u + 16)
                        for c in range(C):
                            ins = mm(conv_out[i % 2], hw[:, c, :], adj3[i][:, c, :], start=False,
                                     stop=(c == C - 1))
                        ins.then_inc(conv_done, 1)

                turns(pe, body)
                back(B - 1, SLOTS - 1)

            @block.scalar
            def _(act):
                fn = nc.scalar.activation

                def body(u, first, last):
                    for i in range(SLOTS):
                        m = SLOTS * u + i
                        act.wait_ge(hnT_done, m + 1)
                        fn(hT[:], M[:, 0:N], ACT.Identity, bias=beta[:], scale=gamma[:])\
                            .then_inc(hT_ready, 1)
                        act.wait_ge(conv_done, m + 1)
                        if not (first and i == 0):
                            act.wait_ge(cback_done, m)
                        fn(cT[:], conv_out[i % 2], ACT.Relu, bias=b_rel[:]).then_inc(cT_ready, 1)

                turns(act, body)

            @block.vector
            def _(dve):
                tt, ts = nc.vector.tensor_tensor, nc.vector.tensor_scalar

                def stats_x(m, i):
                    for c in range(C):
                        ins = nc.vector.bn_stats(
                            st3[:, c, :], X[:, ds(m, 1), c, :].rearrange("p b d -> p (b d)"))
                    ins.then_inc(st3_ready, 1)
                    dve.wait_ge(st3_ready, m + 1)
                    pass_gate(dve, dve_passed)
                    for c in range(C):
                        ins = nc.vector.bn_aggr(mv3[i % 2][:, c, :], st3[:, c, :])
                    ins.then_inc(mv3_ready, 1)
                    dve.wait_ge(mv3_ready, m + 1)
                    ts(var3[i % 2][:], mv3[i % 2][:, :, 1], EPS_LN, None, ALU.add)\
                        .then_inc(var3_ready, 1)

                def outer_norm(m, i):
                    h = h1[i % 2]
                    dve.wait_ge(rstd3_ready, m + 1)
                    for c in range(C):
                        ins = ts(h[:, c, :], X[:, ds(m, 1), c, :].rearrange("p b d -> p (b d)"),
                                 mv3[i % 2][:, c, 0:1], rstd3[i % 2][:, c:c + 1], ALU.subtract,
                                 ALU.mult)
                    ins.then_inc(xn3_ready, 1)
                    dve.wait_ge(xn3_ready, m + 1)
                    ts(h[:], h[:], 0.0, None, ALU.max).then_inc(h1_ready, 1)
                    dve.wait_ge(h1_ready, m + 1)
                    pass_gate(dve, dve_passed)
                    for c in range(C):
                        ins = nc.vector.bn_stats(st_h[:, c, :], h[:, c, :])
                    ins.then_inc(sth_ready, 1)
                    dve.wait_ge(sth_ready, m + 1)
                    pass_gate(dve, dve_passed)
                    for c in range(C):
                        ins = nc.vector.bn_aggr(mv_h[:, c, :], st_h[:, c, :])
                    ins.then_inc(mvh_ready, 1)
                    dve.wait_ge(mvh_ready, m + 1)
                    ts(var_h[:], mv_h[:, :, 1], EPS_LN, None, ALU.add).then_inc(varh_ready, 1)

                def inner_norm(m, i, first):
                    dve.wait_ge(rstdh_ready, m + 1)
                    if not first:
                        dve.wait_ge(hnT_done, m)
                    for c in range(C):
                        ins = ts(hn[:, c, :], h1[i % 2][:, c, :], mv_h[:, c, 0:1],
                                 rstd_h[:, c:c + 1], ALU.subtract, ALU.mult)
                    ins.then_inc(hn_ready, 1)

                def finish(m, i, u, free):
                    dve.wait_ge(cback_done, m + 1)
                    dve.wait_ge(xh_ready, m + 1)
                    if not free:
                        dve.wait_ge(out_stored[i % 2], 16 * (SLOTS // 2 * u + i // 2))
                    tt(ob[i % 2][:], back_out[i % 2], xh[i % 2][:], ALU.add)\
                        .then_inc(out_ready, 1)

                def body(u, first, last):
                    for i in range(SLOTS):
                        m = SLOTS * u + i
                        if not (last and i >= SLOTS - 2):
                            stats_x(m + 2, i)
                        dve.wait_ge(hw_done, m + 1)
                        nc.vector.tensor_copy(hw[:], Z[0:P, :, :]).then_inc(hw_ready, 1)
                        if not (last and i == SLOTS - 1):
                            outer_norm(m + 1, i + 1)
                        if not (first and i == 0):
                            if i == 0:
                                finish(m - 1, SLOTS - 1, u - 1, False)
                            else:
                                finish(m - 1, i - 1, u, first and i <= 2)
                        if not (last and i == SLOTS - 1):
                            inner_norm(m + 1, i + 1, False)

                stats_x(0, 0)
                stats_x(1, 1)
                outer_norm(0, 0)
                inner_norm(0, 0, True)
                turns(dve, body)
                finish(B - 1, SLOTS - 1, TURNS - 1, False)


def kernel(**inputs):
    import concourse.bacc as bacc
    from concourse.bass_utils import run_bass_kernel_spmd

    a = {k: np.asarray(v) for k, v in inputs.items()}

    def rep(v, rows):
        return np.broadcast_to(v, (rows,) + v.shape)

    member = np.zeros((G, GN), np.float32)
    for g, nodes in enumerate(GROUPS):
        member[g, nodes] = 1.0
    pair_mask = member[:, :, None] * member[:, None, :]
    blocks = np.zeros((GB, GN, GB, GN), np.float32)
    for i in range(GB):
        blocks[i, :, i, :] = 1.0
    a_l1 = a["L1_gnn_a"]
    layout = {
        "x": a["x"],
        "adj": a["adj"],
        "adjT": a["adj"].transpose(0, 2, 1),
        "ident": np.eye(128, dtype=np.float32),
        "wqT": a["L0_gnn_W_attn"].transpose(2, 0, 1),
        "w0T": a["L0_gnn_W0"].transpose(2, 0, 1),
        "w1T": a["L0_gnn_W1"].transpose(2, 0, 1),
        "bq": a["L0_gnn_b_attn"].T,
        "b0": a["L0_gnn_b0"].T,
        "b1": a["L0_gnn_b1"].T,
        "wfT": a["L0_gnn_Wf"].T,
        "bf_rows": rep(a["L0_gnn_bf"], P),
        "w_l1": a["L1_gnn_W"],
        "w_l1T": a["L1_gnn_W"].T,
        "a_rep": np.concatenate([np.broadcast_to(a_l1[D:], (D, D)), a_l1[:D]], axis=1),
        "w1g": a["L2_gnn_W1"].transpose(1, 0, 2),
        "w2g": a["L2_gnn_W2"].reshape(G, 2, D, D).transpose(2, 0, 1, 3),
        "b1g": a["L2_gnn_b1"].reshape(G, 2, D).transpose(2, 0, 1),
        "b2g": a["L2_gnn_b2"].T,
        "fw": rep(a["L2_gnn_fusion_w"], D),
        "gmask": np.tile(pair_mask.transpose(1, 0, 2), (GB, 1, 1)),
        "eye25": np.tile(np.eye(GN, dtype=np.float32), (GB, 1)),
        "block_mask": blocks.reshape(R, GB, GN),
        "node_mask": rep(member, D),
        "adj25": a["adj"][:, :GN, :GN].reshape(BLK, R, GN).transpose(1, 0, 2),
        "w_rel": a["L3_gnn_W_rel"],
        "w_root": a["L3_gnn_W_root"],
        "b_rel": a["L3_gnn_b_rel"][:, None],
        "gamma": a["L3_gnn_ln_gamma"][:, None],
        "beta": a["L3_gnn_ln_beta"][:, None],
    }
    nc = bacc.Bacc("TRN2", target_bir_lowering=False, num_devices=1)
    arrays, t = {}, {}
    for name, v in layout.items():
        v = np.ascontiguousarray(v)
        arrays[f"in_{name}"] = v
        t[name] = nc.dram_tensor(f"in_{name}", v.shape, mybir.dt.from_np(v.dtype),
                                 kind="ExternalInput").ap()
    out = nc.dram_tensor("out_x", (B, N, D), F32, kind="ExternalOutput").ap()
    build(nc, t, out)
    r = run_bass_kernel_spmd(nc, [arrays], core_ids=[0])
    return r.results[0]["out_x"]
```

```python
from contextlib import ExitStack

import numpy as np

import concourse.bass as bass
from concourse import mybir

F32 = mybir.dt.float32
ALU = mybir.AluOpType
ACT = mybir.ActivationFunctionType
AX_X = mybir.AxisListType.X
ds = bass.ds

B, N, D = 16, 500, 128
LAYERS = 7
C, P = 4, 125
LANES = 2
PAIRS = B // LANES
STEPS = LAYERS * LANES
EPS_LN = 1e-5
EPS_EYE = 1e-5
NEG_INF = -9000000000000000.0
SLOPE = 0.2
GROUPS = [list(range(25)), [0, 1, 2, 3, 4, 5, 6, 7, 8], [0, 9, 10, 11, 12, 13, 14],
          [6, 7, 8, 12, 13, 14], [3, 4, 5, 9, 10, 11]]
G, GN, HID = len(GROUPS), 25, 256
FREE = 1
GB = 4
BLK = B // GB
R = GB * GN


def build(nc, t, out):
    ctx = ExitStack()
    with ctx:
        def sb(name, shape):
            return ctx.enter_context(nc.sbuf_tensor(name, shape, F32))

        def sem(name):
            return ctx.enter_context(nc.semaphore(name))

        ident = sb("ident", [128, 128])
        wqT = sb("wqT", [D, LAYERS, D])
        w0T = sb("w0T", [D, LAYERS, D])
        w1T = sb("w1T", [D, LAYERS, D])
        bq = sb("bq", [D, LAYERS])
        b0 = sb("b0", [D, LAYERS])
        b1 = sb("b1", [D, LAYERS])
        wfT = sb("wfT", [D, D])
        bf_rows = sb("bf_rows", [P, D])
        w_l1T = sb("w_l1T", [D, D])
        a_rep = sb("a_rep", [D, D + 1])
        w_aug = sb("w_aug", [D, D + 1])
        wa2_rep = sb("wa2_rep", [D, D])
        w1g = sb("w1g", [D, G, HID])
        w2g = sb("w2g", [D, G, 2, D])
        b1g = sb("b1g", [D, G, 2])
        b2g = sb("b2g", [D, G])
        fw = sb("fw", [D, G])
        gmask = sb("gmask", [R, G, GN])
        eye25 = sb("eye25", [R, GN])
        block_mask = sb("block_mask", [R, GB, GN])
        node_mask = sb("node_mask", [D, G, GN])
        adj25 = sb("adj25", [R, BLK, GN])
        w_rel = sb("w_rel", [D, D])
        w_root = sb("w_root", [D, D])
        b_rel = sb("b_rel", [D, 1])
        gamma = sb("gamma", [D, 1])
        beta = sb("beta", [D, 1])
        neg_half = sb("neg_half", [128, G * BLK])
        wq_now = sb("wq_now", [D, D])
        w1_now = sb("w1_now", [D, D])
        bq_now = sb("bq_now", [D, 1])
        b0_now = sb("b0_now", [D, 1])
        b1_now = sb("b1_now", [D, 1])

        X = sb("X", [P, B, C, D])
        adjT = [sb(f"adjT{a}", [P, 2, C, N]) for a in range(LANES)]
        adjN = [sb(f"adjN{a}", [P, C, N]) for a in range(LANES)]
        off_diag = sb("off_diag", [P, P])
        stats = sb("stats", [P, 2 * LANES * C, 6])
        mv = sb("mv", [P, 2 * LANES * C, 2])
        var_eps = sb("var_eps", [P, 2 * LANES * C])
        rstd = sb("rstd", [P, 2 * LANES * C])
        gnn01 = ExitStack()

        def sb01(name, shape):
            return gnn01.enter_context(nc.sbuf_tensor(name, shape, F32))

        xT = [sb01(f"xT{a}", [D, N]) for a in range(LANES)]
        qT = sb01("qT", [D, N])
        S = sb01("S", [P, C, N])
        zaug = [sb01(f"zaug{a}", [P, C, D + 1]) for a in range(LANES)]
        ysum = sb01("ysum", [P, C, D + 1])
        yrec = sb01("yrec", [P, C])
        yn = sb01("yn", [P, C, D])
        tT = sb01("tT", [D, N])
        uT = sb01("uT", [D, N])
        xn = [sb01(f"xn{i}", [P, C, D]) for i in range(LANES + 1)]
        hT = [sb01(f"hT{a}", [D, N]) for a in range(LANES)]
        haug = [sb01(f"haug{a}", [P, C, D + 1]) for a in range(LANES)]
        dst = [sb01(f"dst{a}", [P, N]) for a in range(LANES)]
        E = [sb01(f"E{a}", [P, N]) for a in range(LANES)]
        pen = [sb01(f"pen{a}", [P, N]) for a in range(LANES)]
        PT = [sb01(f"PT{a}", [P, C, P]) for a in range(LANES)]
        rowmax = sb01("rowmax", [P, LANES])
        negmax = sb01("negmax", [P, LANES])
        expsum = sb01("expsum", [P, LANES])
        exprec = sb01("exprec", [P, LANES])

        L = ctx.enter_context(nc.psum_tensor("L", [128, 4, 512], F32))
        Y = ctx.enter_context(nc.psum_tensor("Y", [128, 2, 512], F32))
        Z = ctx.enter_context(nc.psum_tensor("Z", [128, C, D], F32))
        M = ctx.enter_context(nc.psum_tensor("M", [128, 512], F32))
        LOGIT = [L[0:P, c % 2, 0:N] for c in range(C)]
        TR = L[:, 2, :]
        ATT = L[:, 3, :]

        def y_out(c):
            return Y[0:P, c // 2, (c % 2) * (D + 1):(c % 2 + 1) * (D + 1)]

        first_loaded, consts_loaded = sem("first_loaded"), sem("consts_loaded")
        x_loaded = sem("x_loaded")
        adjT_loaded = [sem(f"adjT_loaded{a}") for a in range(LANES)]
        adjN_loaded = [sem(f"adjN_loaded{a}") for a in range(LANES)]
        diag_cut = [sem(f"diag_cut{a}") for a in range(LANES)]
        diag_set = [sem(f"diag_set{a}") for a in range(LANES)]
        half_set = sem("half_set")
        ones_set = sem("ones_set")
        wa_done, wa_ready = sem("wa_done"), sem("wa_ready")
        stats_ready = [sem(f"stats_ready{i}") for i in range(2)]
        mv_ready = [sem(f"mv_ready{i}") for i in range(2)]
        var_ready = [sem(f"var_ready{i}") for i in range(2)]
        rstd_ready = [sem(f"rstd_ready{i}") for i in range(2)]
        xn_ready = [sem(f"xn_ready{i}") for i in range(2)]
        lnT_done = [sem(f"lnT_done{i}") for i in range(2)]
        lnh_ready = [sem(f"lnh_ready{i}") for i in range(2)]
        wq_ready, w1_ready = sem("wq_ready"), sem("w1_ready")
        q_done, qT_ready = sem("q_done"), sem("qT_ready")
        z_done, z_ready = sem("z_done"), sem("z_ready")
        logit_done, sig_ready, S_ready = sem("logit_done"), sem("sig_ready"), sem("S_ready")
        y_done, ysum_ready, yrec_ready, yn_ready = (sem("y_done"), sem("ysum_ready"),
                                                    sem("yrec_ready"), sem("yn_ready"))
        t_done, tT_ready = sem("t_done"), sem("tT_ready")
        w_done, uT_ready, x_ready = sem("w_done"), sem("uT_ready"), sem("x_ready")
        fin_done, x1_part, x1_ready = sem("fin_done"), sem("x1_part"), sem("x1_ready")
        dst_done, dst_ready = sem("dst_done"), sem("dst_ready")
        h_done, haug_ready = sem("h_done"), sem("haug_ready")
        pen_ready, e_ready, leaky_ready = sem("pen_ready"), sem("e_ready"), sem("leaky_ready")
        max_ready, negmax_ready = sem("max_ready"), sem("negmax_ready")
        p_ready, pT_done, PT_ready, att_done = (sem("p_ready"), sem("pT_done"), sem("PT_ready"),
                                                sem("att_done"))
        exprec_ready, x2_ready = sem("exprec_ready"), sem("x2_ready")
        dve_passed, pool_passed, pe_passed = sem("dve_passed"), sem("pool_passed"), sem("pe_passed")

        first_loads = [
            (ident[:], t["ident"]), (off_diag[:], t["off_diag"]), (wqT[:], t["wqT"]),
            (bq[:], t["bq"]), (w0T[:], t["w0T"]), (w1T[:], t["w1T"]), (b0[:], t["b0"]),
            (b1[:], t["b1"]), (wfT[:], t["wfT"]), (bf_rows[:], t["bf_rows"]),
        ]
        const_loads = [
            (w_l1T[:], t["w_l1T"]),
            (w_aug[:, 0:D], t["w_l1"]), (a_rep[:], t["a_rep"]), (w1g[:], t["w1g"]),
            (w2g[:], t["w2g"]), (b1g[:], t["b1g"]), (b2g[:], t["b2g"]), (fw[:], t["fw"]),
            (gmask[:], t["gmask"]), (eye25[:], t["eye25"]), (block_mask[:], t["block_mask"]),
            (node_mask[:], t["node_mask"]), (adj25[:], t["adj25"]), (w_rel[:], t["w_rel"]),
            (w_root[:], t["w_root"]), (b_rel[:], t["b_rel"]), (gamma[:], t["gamma"]),
            (beta[:], t["beta"]),
        ]
        first_value = 16 * len(first_loads)
        consts_value = 16 * len(const_loads)
        x_rows = t["x"].rearrange("b (c p) d -> p b c d", p=P)
        adjT_rows = t["adjT"].rearrange("b (c p) n -> p b c n", p=P)
        adjN_rows = t["adj"].rearrange("b (c p) n -> p b c n", p=P)

        def pass_gate(eng, passed):
            eng.sem_inc(passed, 1)

        def chunk(c, width=P):
            return slice(c * width, (c + 1) * width)

        def lane_layer(a, p, l):
            return STEPS * p + LANES * l + a

        def lane_chunk(a, p, c):
            return LANES * C * p + LANES * c + a

        FIRST_SIDE, LAST_SIDE = 2, 2 + C

        def other(a, l):
            return (1, l - 1) if a == 0 else (0, l)

        def run_pairs(eng, turn, tail):
            turn(0, True, False)
            with eng.Fori(1, PAIRS - 1) as p:
                turn(p, False, False)
            turn(PAIRS - 1, False, True)
            tail(PAIRS - 1)

        def run_layers(eng, p, first, half):
            for l in (0, 1):
                for a in range(LANES):
                    half(a, p, l, l, first)
            with eng.Fori(FIRST_SIDE, LAST_SIDE) as l:
                for a in range(LANES):
                    half(a, p, l, "chunk", first)
            for a in range(LANES):
                half(a, p, LAYERS - 1, "last", first)

        with nc.Block() as block:

            @block.sync
            def _(sp):
                def load_x(p):
                    sp.dma_start(X[:, ds(p * LANES, LANES)], x_rows[:, ds(p * LANES, LANES)])\
                        .then_inc(x_loaded, 16)

                def load_adjT(a, p):
                    sp.dma_start(adjT[a][:, ds(p % 2, 1)].rearrange("p o c n -> p (o c) n"),
                                 adjT_rows[:, ds(p * LANES + a, 1)]
                                 .rearrange("p b c n -> p (b c) n")).then_inc(adjT_loaded[a], 16)

                def load_adjN(a, p):
                    sp.dma_start(adjN[a][:], adjN_rows[:, ds(p * LANES + a, 1)]
                                 .rearrange("p b c n -> p (b c) n")).then_inc(adjN_loaded[a], 16)

                load_x(0)
                for to, src in first_loads:
                    sp.dma_start(to, src).then_inc(first_loaded, 16)
                for a in range(LANES):
                    load_adjT(a, 0)
                for to, src in const_loads:
                    sp.dma_start(to, src).then_inc(consts_loaded, 16)
                sp.wait_ge(x_loaded, 16)
                load_x(1)
                for a in range(LANES):
                    sp.wait_ge(adjT_loaded[a], 16)
                    load_adjT(a, 1)
                for a in range(LANES):
                    load_adjN(a, 0)
                with sp.Fori(1, PAIRS - 1) as p:
                    sp.wait_ge(x_loaded, 16 * p + 16)
                    load_x(p + 1)
                    for a in range(LANES):
                        sp.wait_ge(S_ready, C * (STEPS * p - LANES + a) + C)
                        sp.wait_ge(adjT_loaded[a], 16 * p + 16)
                        load_adjT(a, p + 1)
                    for a in range(LANES):
                        sp.wait_ge(pen_ready, lane_chunk(a, p - 1, C - 1) + 1)
                        load_adjN(a, p)
                for a in range(LANES):
                    sp.wait_ge(pen_ready, lane_chunk(a, PAIRS - 2, C - 1) + 1)
                    load_adjN(a, PAIRS - 1)

            @block.gpsimd
            def _(pool):
                nc.gpsimd.memset(neg_half[:], -0.5).then_inc(half_set, 1)
                for a in range(LANES):
                    nc.gpsimd.memset(zaug[a][:, :, D:D + 1], 1.0).then_inc(ones_set, 1)
                pool.wait_ge(half_set, 1)
                pool.wait_ge(first_loaded, first_value)

                def set_diagonal(a, p):
                    blocks = [adjT[a][:, ds(p % 2, 1), c, chunk(c)].rearrange("p o n -> p (o n)")
                              for c in range(C)]
                    pool.wait_ge(adjT_loaded[a], 16 * p + 16)
                    pass_gate(pool, pool_passed)
                    for c in range(C):
                        ins = nc.gpsimd.tensor_tensor(blocks[c], blocks[c], off_diag[:], ALU.mult)
                    ins.then_inc(diag_cut[a], 1)
                    pool.wait_ge(diag_cut[a], p + 1)
                    pass_gate(pool, pool_passed)
                    for c in range(C):
                        ins = nc.gpsimd.tensor_tensor(blocks[c], blocks[c], ident[0:P, 0:P],
                                                      ALU.add)
                    ins.then_inc(diag_set[a], 1)

                def pow_ln(g, a, m):
                    cols = chunk(LANES * g + a, C)
                    pool.wait_ge(var_ready[g], m + 1)
                    nc.gpsimd.tensor_tensor(rstd[:, cols], var_eps[:, cols], neg_half[0:P, 0:C],
                                            ALU.pow).then_inc(rstd_ready[g], 1)

                def current_wq(p, l):
                    pool.wait_ge(qT_ready, lane_layer(0, p, l) + FREE)
                    pass_gate(pool, pool_passed)
                    nc.gpsimd.tensor_copy(wq_now[:], wqT[:, ds(l, 1)].rearrange("p l n -> p (l n)"))
                    nc.gpsimd.tensor_copy(bq_now[:], bq[:, ds(l, 1)]).then_inc(wq_ready, 1)

                def current_w1(p, l):
                    pool.wait_ge(uT_ready, lane_layer(0, p, l) + FREE)
                    pass_gate(pool, pool_passed)
                    nc.gpsimd.tensor_copy(w1_now[:], w1T[:, ds(l, 1)].rearrange("p l n -> p (l n)"))
                    nc.gpsimd.tensor_copy(b0_now[:], b0[:, ds(l, 1)])
                    nc.gpsimd.tensor_copy(b1_now[:], b1[:, ds(l, 1)]).then_inc(w1_ready, 1)

                def turn(p, first):
                    current_wq(p, 0)
                    current_w1(p, 0)
                    if not first:
                        pow_ln(1, 0, LANES * p - LANES)
                    current_wq(p, 1)
                    if not first:
                        pow_ln(1, 1, LANES * p - LANES + 1)
                    current_w1(p, 1)
                    with pool.Fori(FIRST_SIDE, LAST_SIDE) as l:
                        current_wq(p, l)
                        current_w1(p, l)
                    for a in range(LANES):
                        set_diagonal(a, p + 1)
                    current_wq(p, LAYERS - 1)
                    current_w1(p, LAYERS - 1)
                    for a in range(LANES):
                        pow_ln(0, a, LANES * (p + 1) + a)

                for a in range(LANES):
                    pow_ln(0, a, a)
                for a in range(LANES):
                    set_diagonal(a, 0)
                turn(0, True)
                with pool.Fori(1, PAIRS - 1) as p:
                    turn(p, False)
                p = PAIRS - 1
                current_wq(p, 0)
                current_w1(p, 0)
                pow_ln(1, 0, LANES * p - LANES)
                current_wq(p, 1)
                pow_ln(1, 1, LANES * p - LANES + 1)
                current_w1(p, 1)
                with pool.Fori(FIRST_SIDE, LAYERS) as l:
                    current_wq(p, l)
                    current_w1(p, l)
                for a in range(LANES):
                    pow_ln(1, a, LANES * p + a)

            @block.tensor
            def _(pe):
                mm = nc.tensor.matmul

                def ln_transpose(g, a, m):
                    pe.wait_ge(xn_ready[g], m + 1)
                    src = xn[a] if g == 0 else xn[LANES]
                    for c in range(C):
                        ins = nc.tensor.transpose(TR[:, chunk(c)], src[:, c, :], ident[0:P, 0:P])
                    ins.then_inc(lnT_done[g], 1)

                def q_and_z(a, p, l, z_free, z_count):
                    w0_layer = w0T[:, ds(l, 1)].rearrange("p l n -> p (l n)")
                    if a == 0:
                        pe.wait_ge(wq_ready, LAYERS * p + l + 1)
                    mm(M[:, 0:N], wq_now[:], xT[a][:], start=True, stop=True).then_inc(q_done, 1)
                    pe.wait_ge(z_free, z_count)
                    for c in range(C):
                        ins = mm(Z[0:P, c, :], xT[a][:, chunk(c)], w0_layer, start=True, stop=True)
                    ins.then_inc(z_done, 1)

                def logits(a, p, l, c):
                    n = lane_layer(a, p, l)
                    if c >= 2:
                        pe.wait_ge(sig_ready, C * n + c - 1)
                    mm(LOGIT[c], xT[a][:, chunk(c)], qT[:], start=True, stop=True)\
                        .then_inc(logit_done, 1)

                def y_sum(a, p, l):
                    n = lane_layer(a, p, l)
                    pe.wait_ge(z_ready, n + 1 + FREE)
                    pe.wait_ge(S_ready, C * n + C)
                    for ic in range(C):
                        for jc in range(C):
                            ins = mm(y_out(ic), S[:, jc, chunk(ic)], zaug[a][:, jc, :],
                                     start=(jc == 0), stop=(jc == C - 1))
                        if ic % 2:
                            ins.then_inc(y_done, 1)

                def y_transpose(a, p, l, h):
                    n = lane_layer(a, p, l)
                    pe.wait_ge(yn_ready, 2 * n + h + 1)
                    for c in range(2 * h, 2 * h + 2):
                        ins = nc.tensor.transpose(M[:, chunk(c)], yn[:, c, :], ident[0:P, 0:P])
                    if h:
                        ins.then_inc(t_done, 1)

                def second_linear(a, p, l):
                    n = lane_layer(a, p, l)
                    pe.wait_ge(w1_ready, LAYERS * p + l + 1)
                    pe.wait_ge(tT_ready, n + 1)
                    mm(M[:, 0:N], w1_now[:], tT[:], start=True, stop=True).then_inc(w_done, 1)

                def final_linear(a, p, z_read):
                    pe.wait_ge(x_ready, lane_layer(a, p, LAYERS - 1) + 1)
                    if z_read:
                        pe.wait_ge(*z_read)
                    for c in range(C):
                        ins = mm(Z[0:P, c, :], xT[a][:, chunk(c)], wfT[:], start=True, stop=True)
                    ins.then_inc(fin_done, 1)

                def gnn1_project(a, p):
                    pe.wait_ge(lnh_ready[1], LANES * p + a + 1)
                    mm(ATT[0:P, 0:N], wa2_rep[:, 0:P], hT[a][:], start=True, stop=True)\
                        .then_inc(dst_done, 1)
                    for c in range(C - 1):
                        mm(TR[0:P, chunk(c, D + 1)], hT[a][:, chunk(c)], w_aug[:], start=True,
                           stop=True)

                def gnn1_project_last(a, p):
                    pe.wait_ge(dst_ready, LANES * p + a + 1)
                    mm(ATT[0:P, 0:D + 1], hT[a][:, chunk(C - 1)], w_aug[:], start=True, stop=True)\
                        .then_inc(h_done, 1)

                def probs_transpose(a, p, c):
                    pe.wait_ge(p_ready, lane_chunk(a, p, c) + 1)
                    for jc in range(C):
                        ins = nc.tensor.transpose(TR[0:P, chunk(jc)], E[a][:, chunk(jc)],
                                                  ident[0:P, 0:P])
                    ins.then_inc(pT_done, 1)

                def attend(a, p, c, fresh=False):
                    k = lane_chunk(a, p, c)
                    pe.wait_ge(PT_ready, k + 1)
                    pe.wait_ge(x2_ready, k + FREE)
                    for jc in range(C):
                        ins = mm(ATT[0:P, 0:D], PT[a][:, jc, :], haug[a][:, jc, 0:D],
                                 start=(jc == 0), stop=(jc == C - 1))
                    ins.then_inc(att_done, 1)

                def half(a, p, l, kind, first, last):
                    b, lb = other(a, l)
                    side = not first
                    end = not (first and kind == 0 and a == 0)
                    if kind == 0:
                        pe.wait_ge(lnh_ready[0], LANES * p + a + 1)
                        if first:
                            q_and_z(a, p, l, z_ready, lane_layer(a, p, l) + FREE)
                        else:
                            q_and_z(a, p, l, x1_part, LANES * (p - 1) + a + 1)
                    else:
                        pe.wait_ge(x_ready, lane_layer(a, p, l - 1) + 1)
                        q_and_z(a, p, l, z_ready, lane_layer(a, p, l) + FREE)
                    if end:
                        y_sum(b, p, lb)
                    pe.wait_ge(qT_ready, lane_layer(a, p, l) + 1 + FREE)
                    if end:
                        y_transpose(b, p, lb, 0)
                    if side and kind == 1:
                        if a == 1:
                            pe.wait_ge(haug_ready, LANES * (p - 1) + 1 + FREE)
                        ln_transpose(1, a, LANES * (p - 1) + a)
                    if side and kind == "chunk" and a == 1:
                        pe.wait_ge(haug_ready, LANES * p + FREE)
                        probs_transpose(0, p - 1, l - FIRST_SIDE)
                    logits(a, p, l, 0)
                    if end:
                        y_transpose(b, p, lb, 1)
                    logits(a, p, l, 1)
                    if end:
                        second_linear(b, p, lb)
                    if side and kind == 1:
                        gnn1_project(a, p - 1)
                    if side and kind == "chunk" and a == 1:
                        attend(0, p - 1, l - FIRST_SIDE)
                        probs_transpose(1, p - 1, l - FIRST_SIDE)
                    logits(a, p, l, 2)
                    if kind == 0 and a == 0:
                        ln_transpose(0, 1, LANES * p + 1)
                        if not first:
                            final_linear(1, p - 1, (z_ready, lane_layer(0, p, 0) + 1 + FREE))
                    if kind == "last" and a == 1:
                        if not last:
                            ln_transpose(0, 0, LANES * (p + 1))
                        final_linear(0, p, (z_ready, lane_layer(1, p, l) + 1 + FREE))
                    logits(a, p, l, 3)
                    if side and kind == 1:
                        gnn1_project_last(a, p - 1)
                    if side and kind == "chunk" and a == 1:
                        attend(1, p - 1, l - FIRST_SIDE)

                def turn(p, first, last):
                    run_layers(pe, p, first, lambda a, p, l, kind, first:
                               half(a, p, l, kind, first, last))
                    if first:
                        pe.wait_ge(consts_loaded, consts_value)
                        mm(ATT[:, 0:D + 1], w_l1T[:], a_rep[:], start=True, stop=True)\
                            .then_inc(wa_done, 1)
                        pe.wait_ge(wa_ready, 2)

                pe.wait_ge(first_loaded, first_value)
                ln_transpose(0, 0, 0)
                turn(0, True, False)
                with pe.Fori(1, PAIRS - 1) as p:
                    turn(p, False, False)
                turn(PAIRS - 1, False, True)
                p = PAIRS - 1
                y_sum(1, p, LAYERS - 1)
                y_transpose(1, p, LAYERS - 1, 0)
                y_transpose(1, p, LAYERS - 1, 1)
                ln_transpose(1, 0, LANES * p)
                second_linear(1, p, LAYERS - 1)
                gnn1_project(0, p)
                gnn1_project_last(0, p)
                final_linear(1, p, (x1_part, LANES * p + 1))
                pe.wait_ge(haug_ready, LANES * p + 1 + FREE)
                ln_transpose(1, 1, LANES * p + 1)
                gnn1_project(1, p)
                gnn1_project_last(1, p)
                pe.wait_ge(haug_ready, LANES * p + 2 + FREE)
                steps = [(a, c) for c in range(C) for a in range(LANES)]
                for i, (a, c) in enumerate(steps):
                    if i:
                        pe.wait_ge(PT_ready, lane_chunk(a, p, c))
                    probs_transpose(a, p, c)
                    attend(a, p, c)

            @block.scalar
            def _(act):
                fn = nc.scalar.activation
                act.sem_inc(qT_ready, FREE)
                act.sem_inc(uT_ready, FREE)

                def ln_relu(g, a, m, after_final):
                    act.wait_ge(lnT_done[g], m + 1)
                    if after_final is not None:
                        act.wait_ge(fin_done, after_final)
                    fn((hT if g else xT)[a][:], TR[:, 0:N], ACT.Relu).then_inc(lnh_ready[g], 1)

                def q_out(a, p, l):
                    act.wait_ge(q_done, lane_layer(a, p, l) + 1)
                    fn(qT[:], M[:, 0:N], ACT.Identity, bias=bq_now[:]).then_inc(qT_ready, 1)

                def sigmoid(a, p, l, c):
                    act.wait_ge(logit_done, C * lane_layer(a, p, l) + c + 1)
                    fn(S[:, c, :], LOGIT[c], ACT.Sigmoid).then_inc(sig_ready, 1)

                def t_out(a, p, l):
                    act.wait_ge(w1_ready, LAYERS * p + l + 1)
                    act.wait_ge(t_done, lane_layer(a, p, l) + 1)
                    fn(tT[:], M[:, 0:N], ACT.Relu, bias=b0_now[:]).then_inc(tT_ready, 1)

                def u_out(a, p, l):
                    act.wait_ge(w_done, lane_layer(a, p, l) + 1)
                    fn(uT[:], M[:, 0:N], ACT.Relu, bias=b1_now[:]).then_inc(uT_ready, 1)

                def dst_out(a, p):
                    act.wait_ge(dst_done, LANES * p + a + 1)
                    fn(dst[a][:], ATT[0:P, 0:N], ACT.Copy).then_inc(dst_ready, 1)

                def exp(a, p, c):
                    act.wait_ge(negmax_ready, lane_chunk(a, p, c) + 1)
                    fn(E[a][:], E[a][:], ACT.Exp, bias=negmax[:, a:a + 1],
                       accum_out=expsum[:, a:a + 1]).then_inc(p_ready, 1)

                def probs_out(a, p, c):
                    act.wait_ge(pT_done, lane_chunk(a, p, c) + 1)
                    fn(PT[a][:].rearrange("p c i -> p (c i)"), TR[0:P, 0:N], ACT.Copy)\
                        .then_inc(PT_ready, 1)

                def half(a, p, l, kind, first, last):
                    b, lb = other(a, l)
                    side = not first
                    end = not (first and kind == 0 and a == 0)
                    q_out(a, p, l)
                    if side and kind == "chunk" and a == 1:
                        exp(0, p - 1, l - FIRST_SIDE)
                        exp(1, p - 1, l - FIRST_SIDE)
                        nc.scalar.preload_act_table(ACT.Sigmoid)
                        probs_out(0, p - 1, l - FIRST_SIDE)
                    if side and kind == 1:
                        ln_relu(1, a, LANES * (p - 1) + a, None)
                    if end:
                        t_out(b, p, lb)
                    sigmoid(a, p, l, 0)
                    sigmoid(a, p, l, 1)
                    if end:
                        u_out(b, p, lb)
                    if side and kind == 1:
                        dst_out(a, p - 1)
                    if side and kind == "chunk" and a == 1:
                        probs_out(1, p - 1, l - FIRST_SIDE)
                    sigmoid(a, p, l, 2)
                    if kind == 0 and a == 0:
                        ln_relu(0, 1, LANES * p + 1, None if first else LANES * (p - 1) + 2)
                    if kind == "last" and a == 1 and not last:
                        ln_relu(0, 0, LANES * (p + 1), LANES * p + 1)
                    sigmoid(a, p, l, 3)

                def turn(p, first, last):
                    run_layers(act, p, first, lambda a, p, l, kind, first:
                               half(a, p, l, kind, first, last))

                def tail(p):
                    t_out(1, p, LAYERS - 1)
                    ln_relu(1, 0, LANES * p, None)
                    u_out(1, p, LAYERS - 1)
                    dst_out(0, p)
                    ln_relu(1, 1, LANES * p + 1, None)
                    dst_out(1, p)
                    steps = [(a, c) for c in range(C) for a in range(LANES)]
                    for i, (a, c) in enumerate(steps):
                        exp(a, p, c)
                        probs_out(a, p, c)

                ln_relu(0, 0, 0, None)
                run_pairs(act, turn, tail)

            @block.vector
            def _(dve):
                tt, ts, stt = (nc.vector.tensor_tensor, nc.vector.tensor_scalar,
                               nc.vector.scalar_tensor_tensor)
                for ready in (z_ready, x2_ready, haug_ready):
                    dve.sem_inc(ready, FREE)
                dve.wait_ge(ones_set, LANES)
                dve.wait_ge(first_loaded, first_value)

                def x_chunk(m, c):
                    return X[:, ds(m, 1), c, :].rearrange("p b d -> p (b d)")

                def ln_stats(g, a, m):
                    i = C * (LANES * g + a)
                    for c in range(C):
                        ins = nc.vector.bn_stats(stats[:, i + c, :], x_chunk(m, c))
                    ins.then_inc(stats_ready[g], 1)
                    dve.wait_ge(stats_ready[g], m + 1)
                    pass_gate(dve, dve_passed)
                    for c in range(C):
                        ins = nc.vector.bn_aggr(mv[:, i + c, :], stats[:, i + c, :])
                    ins.then_inc(mv_ready[g], 1)
                    dve.wait_ge(mv_ready[g], m + 1)
                    ts(var_eps[:, i:i + C], mv[:, i:i + C, 1], EPS_LN, None, ALU.add)\
                        .then_inc(var_ready[g], 1)

                def ln_rows(g, a, m):
                    i = C * (LANES * g + a)
                    to = xn[a] if g == 0 else xn[LANES]
                    dve.wait_ge(rstd_ready[g], m + 1)
                    for c in range(C):
                        ins = ts(to[:, c, :], x_chunk(m, c), mv[:, i + c, 0:1],
                                 rstd[:, i + c:i + c + 1], ALU.subtract, ALU.mult)
                    ins.then_inc(xn_ready[g], 1)

                def z_out(a, p, l):
                    dve.wait_ge(z_done, lane_layer(a, p, l) + 1)
                    nc.vector.tensor_copy(zaug[a][:, :, 0:D], Z[0:P, :, :]).then_inc(z_ready, 1)

                def mask(a, p, l, c):
                    dve.wait_ge(sig_ready, C * lane_layer(a, p, l) + c + 1)
                    tt(S[:, c, :], S[:, c, :],
                       adjT[a][:, ds(p % 2, 1), c, :].rearrange("p o n -> p (o n)"), ALU.mult)\
                        .then_inc(S_ready, 1)

                def y_norm(a, p, l):
                    n = lane_layer(a, p, l)
                    w = D + 1
                    for h in range(2):
                        dve.wait_ge(y_done, 2 * n + h + 1)
                        stt(ysum[:, 2 * h:2 * h + 2, :],
                            zaug[a][:, 2 * h:2 * h + 2, :], EPS_EYE,
                            Y[0:P, h, 0:2 * w].rearrange("p (c w) -> p c w", w=w),
                            ALU.mult, ALU.add).then_inc(ysum_ready, 1)
                        dve.wait_ge(ysum_ready, 2 * n + h + 1)
                        nc.vector.reciprocal(yrec[:, 2 * h:2 * h + 2], ysum[:, 2 * h:2 * h + 2, D])\
                            .then_inc(yrec_ready, 1)
                        dve.wait_ge(yrec_ready, 2 * n + h + 1)
                        for c in range(2 * h, 2 * h + 2):
                            ins = ts(yn[:, c, :], ysum[:, c, 0:D], yrec[:, c:c + 1], None,
                                     ALU.mult)
                        ins.then_inc(yn_ready, 1)

                def x_add(a, p, l):
                    dve.wait_ge(uT_ready, lane_layer(a, p, l) + 1 + FREE)
                    tt(xT[a][:], xT[a][:], uT[:], ALU.add).then_inc(x_ready, 1)

                def final_add(a, p):
                    m = LANES * p + a
                    x = X[:, ds(m, 1), :, :].rearrange("p b c d -> p (b c) d")
                    dve.wait_ge(fin_done, m + 1)
                    tt(x, x, Z[0:P, :, :], ALU.add).then_inc(x1_part, 1)

                def final_bias(a, p):
                    m = LANES * p + a
                    x = X[:, ds(m, 1), :, :].rearrange("p b c d -> p (b c) d")
                    dve.wait_ge(x1_part, m + 1)
                    tt(x, x, bf_rows[:].rearrange("p (c d) -> p c d", c=1)
                       .to_broadcast([P, C, D]), ALU.add).then_inc(x1_ready, 1)

                def haug_out(a, p):
                    flat = haug[a][:].rearrange("p c w -> p (c w)")
                    w = (C - 1) * (D + 1)
                    dve.wait_ge(h_done, LANES * p + a + 1)
                    nc.vector.tensor_copy(flat[:, 0:w], TR[0:P, 0:w])
                    nc.vector.tensor_copy(flat[:, w:w + D + 1], ATT[0:P, 0:D + 1])\
                        .then_inc(haug_ready, 1)

                def raw_scores(a, p, c):
                    k = lane_chunk(a, p, c)
                    dve.wait_ge(adjN_loaded[a], 16 * p + 16)
                    ts(pen[a][:], adjN[a][:, ds(c, 1), :].rearrange("p o n -> p (o n)"), 0.0,
                       NEG_INF, ALU.is_le, ALU.mult).then_inc(pen_ready, 1)
                    dve.wait_ge(haug_ready, LANES * p + a + 1 + FREE)
                    dve.wait_ge(dst_ready, LANES * p + a + 1)
                    ts(E[a][:], dst[a][:], haug[a][:, ds(c, 1), D:D + 1]
                       .rearrange("p o w -> p (o w)"), None, ALU.add).then_inc(e_ready, 1)

                def masked_scores(a, p, c):
                    k = lane_chunk(a, p, c)
                    dve.wait_ge(e_ready, k + 1)
                    stt(E[a][:], E[a][:], SLOPE, E[a][:], ALU.mult, ALU.max)\
                        .then_inc(leaky_ready, 1)
                    dve.wait_ge(pen_ready, k + 1)
                    dve.wait_ge(leaky_ready, k + 1)
                    pass_gate(dve, dve_passed)
                    nc.vector.tensor_tensor_reduce(
                        out=E[a][:], in0=E[a][:], in1=pen[a][:], scale=1.0, scalar=-3.0e38,
                        op0=ALU.add, op1=ALU.max, accum_out=rowmax[:, a:a + 1])\
                        .then_inc(max_ready, 1)
                    dve.wait_ge(max_ready, k + 1)
                    ts(negmax[:, a:a + 1], rowmax[:, a:a + 1], -1.0, None, ALU.mult)\
                        .then_inc(negmax_ready, 1)

                def attention_add(a, p, c):
                    k = lane_chunk(a, p, c)
                    m = LANES * p + a
                    x = X[:, ds(m, 1), ds(c, 1), :].rearrange("p b c d -> p (b c d)")
                    dve.wait_ge(p_ready, k + 1)
                    nc.vector.reciprocal(exprec[:, a:a + 1], expsum[:, a:a + 1])\
                        .then_inc(exprec_ready, 1)
                    dve.wait_ge(exprec_ready, k + 1)
                    dve.wait_ge(att_done, k + 1)
                    stt(x, ATT[0:P, 0:D], exprec[:, a:a + 1], x, ALU.mult, ALU.add)\
                        .then_inc(x2_ready, 1)

                def half(a, p, l, kind, first, norms):
                    b, lb = other(a, l)
                    side = not first
                    end = not (first and kind == 0 and a == 0)
                    if side and kind == "chunk" and a == 0:
                        raw_scores(0, p - 1, l - FIRST_SIDE)
                    z_out(a, p, l)
                    if side and kind == 1:
                        if a == 1:
                            dve.wait_ge(lnT_done[1], LANES * (p - 1) + 1)
                        ln_rows(1, a, LANES * (p - 1) + a)
                    if side and kind == "chunk" and a == 0:
                        masked_scores(0, p - 1, l - FIRST_SIDE)
                    if norms:
                        dve.wait_ge(x_loaded, 16 * (p + 1) + 16)
                        pass_gate(dve, dve_passed)
                        ln_stats(0, a, LANES * (p + 1) + a)
                    if end:
                        y_norm(b, p, lb)
                    if kind == 0:
                        dve.wait_ge(diag_set[a], p + 1)
                    mask(a, p, l, 0)
                    mask(a, p, l, 1)
                    if side and kind == "chunk" and a == 0:
                        raw_scores(1, p - 1, l - FIRST_SIDE)
                    if end:
                        x_add(b, p, lb)
                    if side and kind == "chunk" and a == 1:
                        attention_add(0, p - 1, l - FIRST_SIDE)
                    mask(a, p, l, 2)
                    if side and kind == 0 and a == 0:
                        final_add(1, p - 1)
                    if kind == "last" and a == 1:
                        final_add(0, p)
                    mask(a, p, l, 3)
                    if norms:
                        ln_rows(0, a, LANES * (p + 1) + a)
                    if side and kind == 0 and a == 0:
                        final_bias(1, p - 1)
                    if kind == "last" and a == 1:
                        final_bias(0, p)
                    if side and kind == 0:
                        dve.wait_ge(x1_ready, LANES * (p - 1) + a + 1)
                        pass_gate(dve, dve_passed)
                        ln_stats(1, a, LANES * (p - 1) + a)
                    if side and kind == 1:
                        haug_out(a, p - 1)
                    if side and kind == "chunk":
                        if a == 0:
                            masked_scores(1, p - 1, l - FIRST_SIDE)
                        else:
                            attention_add(1, p - 1, l - FIRST_SIDE)

                def turn(p, first, last):
                    run_layers(dve, p, first, lambda a, p, l, kind, first:
                               half(a, p, l, kind, first, kind == "last" and not last))

                dve.wait_ge(x_loaded, 16)
                for a in range(LANES):
                    ln_stats(0, a, a)
                for a in range(LANES):
                    ln_rows(0, a, a)
                turn(0, True, False)
                dve.wait_ge(consts_loaded, consts_value)
                dve.wait_ge(wa_done, 1)
                nc.vector.tensor_copy(wa2_rep[:], ATT[:, 0:D]).then_inc(wa_ready, 1)
                nc.vector.tensor_copy(w_aug[:, D:D + 1], ATT[:, D:D + 1]).then_inc(wa_ready, 1)
                with dve.Fori(1, PAIRS - 1) as p:
                    turn(p, False, False)
                turn(PAIRS - 1, False, True)
                p = PAIRS - 1
                dve.wait_ge(x1_ready, LANES * p + 1)
                ln_stats(1, 0, LANES * p)
                y_norm(1, p, LAYERS - 1)
                ln_rows(1, 0, LANES * p)
                x_add(1, p, LAYERS - 1)
                haug_out(0, p)
                final_add(1, p)
                final_bias(1, p)
                dve.wait_ge(x1_ready, LANES * p + 2)
                ln_stats(1, 1, LANES * p + 1)
                ln_rows(1, 1, LANES * p + 1)
                haug_out(1, p)
                for c in range(C):
                    for a in range(LANES):
                        raw_scores(a, p, c)
                        masked_scores(a, p, c)
                    for a in range(LANES):
                        attention_add(a, p, c)

        gnn01.close()

        GQ = G * BLK
        adj_self = sb("adj_self", [R, BLK, G, GN])
        deg = sb("deg", [R, GQ])
        dinv = sb("dinv", [R, GQ])
        is_zero = sb("is_zero", [R, GQ])
        not_zero = sb("not_zero", [R, GQ])
        adj_blocks = sb("adj_blocks", [R, GQ, R])
        normT = sb("normT", [R, GQ, R])
        xn25 = sb("xn25", [GN, B, D])
        h25T = sb("h25T", [D, B * GN])
        sup1 = sb("sup1", [R, BLK, HID])
        hidT = sb("hidT", [D, 2, B * GN])
        sup2 = sb("sup2", [R, BLK, D])
        gout = sb("gout", [D, B * GN])
        fused = sb("fused", [D, B * GN])
        fsum = sb("fsum", [D, 4])
        fexp = sb("fexp", [D, G])
        wmask = sb("wmask", [D, G, GN])

        l2_step = sem("l2_step")
        deg_ready, dinv_ready = sem("deg_ready"), sem("dinv_ready")
        blocks_ready, adjTr_done, normT_ready = (sem("blocks_ready"), sem("adjTr_done"),
                                                 sem("normT_ready"))
        fmax_ready, fexp_ready = sem("fmax_ready"), sem("fexp_ready")
        var25_ready, rstd25_ready, xn25_ready = (sem("var25_ready"), sem("rstd25_ready"),
                                                 sem("xn25_ready"))
        x25T_done, h25_ready = sem("x25T_done"), sem("h25_ready")
        sup1_done, sup1_ready = sem("sup1_done"), sem("sup1_ready")
        hid_done, hid_ready = sem("hid_done"), sem("hid_ready")
        sup2_done, sup2_ready = sem("sup2_done"), sem("sup2_ready")
        gout_done, gout_ready, fused_ready = sem("gout_done"), sem("gout_ready"), sem("fused_ready")
        back_done, x3_ready = sem("back_done"), sem("x3_ready")
        adj3 = [adjT[a][:, i] for i in range(2) for a in range(LANES)]
        adj3_loaded = [sem(f"adj3_loaded{i}") for i in range(4)]

        def load_adj3(sp, i, b):
            sp.dma_start(adj3[i], adjT_rows[:, ds(b, 1)].rearrange("p b c n -> p (b c) n"))\
                .then_inc(adj3_loaded[i], 16)

        def rows(q):
            return slice(q * R, (q + 1) * R)

        with nc.Block() as block:

            @block.sync
            def _(sp):
                sp.wait_ge(S_ready, C * STEPS * PAIRS)
                sp.wait_ge(pen_ready, C * B)
                for i in range(4):
                    load_adj3(sp, i, i)

            @block.gpsimd
            def _(pool):
                pool.wait_ge(deg_ready, 1)
                nc.gpsimd.tensor_tensor(dinv[:], deg[:], neg_half[0:R, 0:GQ], ALU.pow)\
                    .then_inc(dinv_ready, 1)
                pool.wait_ge(var25_ready, 1)
                nc.gpsimd.tensor_tensor(rstd[0:GN, :], var_eps[0:GN, :], neg_half[0:GN, 0:B],
                                        ALU.pow).then_inc(rstd25_ready, 1)

            @block.tensor
            def _(pe):
                mm = nc.tensor.matmul
                pe.wait_ge(blocks_ready, 1)
                pe.wait_ge(x2_ready, C * B + FREE)
                for i in range(GQ):
                    ins = nc.tensor.transpose(L[0:R, i // G, (i % G) * R:(i % G + 1) * R],
                                              adj_blocks[:, i, :], ident[0:R, 0:R])
                ins.then_inc(adjTr_done, 1)
                pe.wait_ge(xn25_ready, 1)
                for b in range(B):
                    ins = nc.tensor.transpose(M[:, b * GN:(b + 1) * GN], xn25[:, b, :],
                                              ident[0:GN, 0:GN])
                ins.then_inc(x25T_done, 1)
                pe.wait_ge(h25_ready, 1)

                def support1(g):
                    if g:
                        pe.wait_ge(sup1_ready, g)
                    for q in range(BLK):
                        ins = mm(Y[0:R, q // 2, (q % 2) * HID:(q % 2 + 1) * HID],
                                 h25T[:, rows(q)], w1g[:, g, :], start=True, stop=True)
                    ins.then_inc(sup1_done, 1)

                support1(0)
                pe.wait_ge(normT_ready, 1)
                for g in range(G):
                    pe.wait_ge(sup1_ready, g + 1)
                    for f in range(2):
                        for q in range(BLK):
                            ins = mm(L[:, f, rows(q)], sup1[:, q, f * D:(f + 1) * D],
                                     normT[:, q * G + g, :], start=True, stop=True)
                    ins.then_inc(hid_done, 1)
                    if g + 1 < G:
                        support1(g + 1)
                    pe.wait_ge(hid_ready, g + 1)
                    for q in range(BLK):
                        for f in range(2):
                            ins = mm(Z[0:R, q, :], hidT[:, f, rows(q)], w2g[:, g, f, :],
                                     start=(f == 0), stop=(f == 1))
                    ins.then_inc(sup2_done, 1)
                    pe.wait_ge(sup2_ready, g + 1)
                    if g:
                        pe.wait_ge(gout_ready, g)
                    for q in range(BLK):
                        ins = mm(M[:, rows(q)], sup2[:, q, :], normT[:, q * G + g, :],
                                 start=True, stop=True)
                    ins.then_inc(gout_done, 1)
                pe.wait_ge(fused_ready, G)
                for b in range(B):
                    ins = nc.tensor.transpose(L[0:GN, b // 4, (b % 4) * D:(b % 4 + 1) * D],
                                              fused[:, b * GN:(b + 1) * GN], ident[:])
                ins.then_inc(back_done, 1)

            @block.scalar
            def _(act):
                fn = nc.scalar.activation
                act.wait_ge(consts_loaded, consts_value)
                act.wait_ge(fmax_ready, 1)
                fn(fexp[:], fw[:], ACT.Exp, bias=fsum[:, 1:2], accum_out=fsum[:, 2:3])\
                    .then_inc(fexp_ready, 1)
                act.wait_ge(x25T_done, 1)
                fn(h25T[:], M[:, 0:B * GN], ACT.Relu).then_inc(h25_ready, 1)
                for g in range(G):
                    act.wait_ge(hid_done, g + 1)
                    for f in range(2):
                        ins = fn(hidT[:, f, :], L[:, f, 0:B * GN], ACT.Relu,
                                 bias=b1g[:, g, f:f + 1])
                    ins.then_inc(hid_ready, 1)
                    act.wait_ge(gout_done, g + 1)
                    if g:
                        act.wait_ge(fused_ready, g)
                    fn(gout[:], M[:, 0:B * GN], ACT.Relu, bias=b2g[:, g:g + 1])\
                        .then_inc(gout_ready, 1)

            @block.vector
            def _(dve):
                tt, ts, stt = (nc.vector.tensor_tensor, nc.vector.tensor_scalar,
                               nc.vector.scalar_tensor_tensor)
                steps = [0]

                def link(ins):
                    steps[0] += 1
                    ins.then_inc(l2_step, 1)
                    dve.wait_ge(l2_step, steps[0])

                link(nc.vector.reduce_max(fsum[:, 0:1], fw[:], AX_X))
                ts(fsum[:, 1:2], fsum[:, 0:1], -1.0, None, ALU.mult).then_inc(fmax_ready, 1)
                for b in range(B):
                    ins = nc.vector.bn_stats(stats[0:GN, b, :], X[0:GN, b, 0, :])
                link(ins)
                for b in range(B):
                    ins = nc.vector.bn_aggr(mv[0:GN, b, :], stats[0:GN, b, :])
                link(ins)
                ts(var_eps[0:GN, :], mv[0:GN, :, 1], EPS_LN, None, ALU.add)\
                    .then_inc(var25_ready, 1)
                for q in range(BLK):
                    ins = tt(adj_self[:, q], adj25[:, q:q + 1, :].to_broadcast([R, G, GN]),
                             eye25[:].rearrange("p (g m) -> p g m", g=1).to_broadcast([R, G, GN]),
                             ALU.add)
                link(ins)
                for q in range(BLK):
                    ins = tt(adj_self[:, q], adj_self[:, q], gmask[:], ALU.mult)
                link(ins)
                link(nc.vector.reduce_sum(deg[:], adj_self[:].rearrange("p q g m -> p (q g) m"),
                                          AX_X))
                ts(is_zero[:], deg[:], 0.0, None, ALU.is_equal)
                link(ts(not_zero[:], deg[:], 0.0, None, ALU.not_equal))
                tt(deg[:], deg[:], is_zero[:], ALU.add).then_inc(deg_ready, 1)
                dve.wait_ge(dinv_ready, 1)
                link(tt(dinv[:], dinv[:], not_zero[:], ALU.mult))
                flat = adj_self[:].rearrange("p q g m -> p (q g) m")
                per_row = dinv[:].rearrange("p (i o) -> p i o", o=1)
                link(tt(flat, flat, per_row.to_broadcast([R, GQ, GN]), ALU.mult))
                for i in range(GQ):
                    ins = tt(adj_blocks[:, i, :].rearrange("p (k m) -> p k m", k=GB),
                             flat[:, i:i + 1, :].to_broadcast([R, GB, GN]), block_mask[:],
                             ALU.mult)
                ins.then_inc(blocks_ready, 1)
                dve.wait_ge(rstd25_ready, 1)
                for b in range(B):
                    ins = ts(xn25[:, b, :], X[0:GN, b, 0, :], mv[0:GN, b, 0:1],
                             rstd[0:GN, b:b + 1], ALU.subtract, ALU.mult)
                ins.then_inc(xn25_ready, 1)
                dve.wait_ge(adjTr_done, 1)
                for q in range(BLK):
                    ins = tt(normT[:, q * G:(q + 1) * G, :],
                             L[0:R, q, 0:G * R].rearrange("p (g n) -> p g n", g=G),
                             per_row[:, q * G:(q + 1) * G, :].to_broadcast([R, G, R]), ALU.mult)
                ins.then_inc(normT_ready, 1)
                dve.wait_ge(fexp_ready, 1)
                link(nc.vector.reciprocal(fsum[:, 3:4], fsum[:, 2:3]))
                link(ts(fexp[:], fexp[:], fsum[:, 3:4], None, ALU.mult))
                for g in range(G):
                    ins = ts(wmask[:, g, :], node_mask[:, g, :], fexp[:, g:g + 1], None, ALU.mult)
                link(ins)

                def add_group(g):
                    wm = wmask[:, g:g + 1, :].to_broadcast([D, B, GN])
                    rows_of = gout[:].rearrange("p (b n) -> p b n", b=B)
                    fused_of = fused[:].rearrange("p (b n) -> p b n", b=B)
                    dve.wait_ge(gout_ready, g + 1)
                    if g == 0:
                        link(tt(fused_of, rows_of, wm, ALU.mult))
                    else:
                        link(tt(rows_of, rows_of, wm, ALU.mult))
                        link(tt(fused[:], fused[:], gout[:], ALU.add))
                    dve.sem_inc(fused_ready, 1)

                for g in range(G):
                    dve.wait_ge(sup1_done, g + 1)
                    nc.vector.tensor_copy(sup1[:].rearrange("p (h q) e -> p h (q e)", h=2),
                                          Y[0:R, :, :]).then_inc(sup1_ready, 1)
                    if g:
                        add_group(g - 1)
                    dve.wait_ge(sup2_done, g + 1)
                    nc.vector.tensor_copy(sup2[:], Z[0:R, :, :]).then_inc(sup2_ready, 1)
                add_group(G - 1)
                for i in range(4):
                    dve.wait_ge(back_done, 1)
                    x = X[0:GN, 4 * i:4 * i + 4, 0, :]
                    tt(x, x, L[0:GN, i, :].rearrange("p (b d) -> p b d", b=4), ALU.add)\
                        .then_inc(x3_ready, 1)

        SLOTS = 4
        TURNS = B // SLOTS
        var3 = [sb(f"var3_{i}", [P, C]) for i in range(2)]
        rstd3 = [sb(f"rstd3_{i}", [P, C]) for i in range(2)]
        mv3 = [sb(f"mv3_{i}", [P, C, 2]) for i in range(2)]
        st3 = sb("st3", [P, C, 6])
        st_h = sb("st_h", [P, C, 6])
        mv_h = sb("mv_h", [P, C, 2])
        var_h = sb("var_h", [P, C])
        rstd_h = sb("rstd_h", [P, C])
        h1 = [sb(f"h1_{i}", [P, C, D]) for i in range(2)]
        xh = [sb(f"xh_{i}", [P, C, D]) for i in range(2)]
        hn = sb("hn", [P, C, D])
        hT = sb("hT", [D, N])
        hw = sb("hw", [P, C, D])
        cT = sb("cT", [D, N])
        ob = [sb(f"ob_{i}", [P, C, D]) for i in range(2)]

        st3_ready, mv3_ready, var3_ready, rstd3_ready = (sem("st3_ready"), sem("mv3_ready"),
                                                         sem("var3_ready"), sem("rstd3_ready"))
        xn3_ready, h1_ready, xh_ready = sem("xn3_ready"), sem("h1_ready"), sem("xh_ready")
        sth_ready, mvh_ready, varh_ready, rstdh_ready = (sem("sth_ready"), sem("mvh_ready"),
                                                         sem("varh_ready"), sem("rstdh_ready"))
        hn_ready, hnT_done, hT_ready = sem("hn_ready"), sem("hnT_done"), sem("hT_ready")
        hw_done, hw_ready, conv_done, cT_ready = (sem("hw_done"), sem("hw_ready"),
                                                  sem("conv_done"), sem("cT_ready"))
        cback_done, out_ready = sem("cback_done"), sem("out_ready")
        out_stored = [sem(f"out_stored{i}") for i in range(2)]
        out_rows = out.rearrange("b (c p) d -> p b c d", p=P)
        conv_out = [L[:, 0, 0:N], L[:, 1, 0:N]]
        back_out = [Y[0:P, 0, :].rearrange("p (c d) -> p c d", c=C),
                    Y[0:P, 1, :].rearrange("p (c d) -> p c d", c=C)]

        def turns(eng, body):
            body(0, True, False)
            with eng.Fori(1, TURNS - 1) as u:
                body(u, False, False)
            body(TURNS - 1, False, True)

        with nc.Block() as block:

            @block.sync
            def _(sp):
                def store(m, i):
                    sp.wait_ge(out_ready, m + 1)
                    sp.dma_start(out_rows[:, ds(m, 1)].rearrange("p b c d -> p (b c) d"),
                                 ob[i % 2][:]).then_inc(out_stored[i % 2], 16)

                def body(u, first, last):
                    for i in range(SLOTS):
                        m = SLOTS * u + i
                        if not (first and i == 0):
                            store(m - 1, i - 1)
                        if not last:
                            sp.wait_ge(conv_done, m + 1)
                            load_adj3(sp, i, m + SLOTS)

                turns(sp, body)
                store(B - 1, SLOTS - 1)
                for i in range(2):
                    sp.wait_ge(out_stored[i], 16 * (B // 2))

            @block.gpsimd
            def _(pool):
                def pow_x(m, i):
                    pool.wait_ge(var3_ready, m + 1)
                    nc.gpsimd.tensor_tensor(rstd3[i % 2][:], var3[i % 2][:], neg_half[0:P, 0:C],
                                            ALU.pow).then_inc(rstd3_ready, 1)

                def pow_h(m):
                    pool.wait_ge(varh_ready, m + 1)
                    nc.gpsimd.tensor_tensor(rstd_h[:], var_h[:], neg_half[0:P, 0:C],
                                            ALU.pow).then_inc(rstdh_ready, 1)

                def add_xh(m, i, first):
                    pool.wait_ge(h1_ready, m + 1)
                    if not first:
                        pool.wait_ge(out_ready, m - 1)
                    nc.gpsimd.tensor_tensor(
                        xh[i % 2][:], h1[i % 2][:],
                        X[:, ds(m, 1), :, :].rearrange("p b c d -> p (b c) d"), ALU.add)\
                        .then_inc(xh_ready, 1)

                pow_x(0, 0)
                pow_x(1, 1)
                pow_h(0)
                add_xh(0, 0, True)

                def body(u, first, last):
                    for i in range(SLOTS):
                        m = SLOTS * u + i
                        if not (last and i >= SLOTS - 2):
                            pow_x(m + 2, i)
                        if not (last and i == SLOTS - 1):
                            pow_h(m + 1)
                            add_xh(m + 1, i + 1, first and i == 0)

                turns(pool, body)

            @block.tensor
            def _(pe):
                mm = nc.tensor.matmul

                def back(m, i):
                    pe.wait_ge(cT_ready, m + 1)
                    for c in range(C):
                        ins = nc.tensor.transpose(back_out[i % 2][:, c, :], cT[:, chunk(c)],
                                                  ident[:])
                    ins.then_inc(cback_done, 1)

                def body(u, first, last):
                    for i in range(SLOTS):
                        m = SLOTS * u + i
                        pe.wait_ge(hn_ready, m + 1)
                        for c in range(C):
                            ins = nc.tensor.transpose(M[:, chunk(c)], hn[:, c, :],
                                                      ident[0:P, 0:P])
                        ins.then_inc(hnT_done, 1)
                        if not (first and i == 0):
                            back(m - 1, i - 1)
                        pe.wait_ge(hT_ready, m + 1)
                        for c in range(C):
                            ins = mm(Z[0:P, c, :], hT[:, chunk(c)], w_rel[:], start=True,
                                     stop=True)
                        ins.then_inc(hw_done, 1)
                        mm(conv_out[i % 2], w_root[:], hT[:], start=True, stop=False)
                        pe.wait_ge(hw_ready, m + 1)
                        pe.wait_ge(adj3_loaded[i], 16 * u + 16)
                        for c in range(C):
                            ins = mm(conv_out[i % 2], hw[:, c, :], adj3[i][:, c, :], start=False,
                                     stop=(c == C - 1))
                        ins.then_inc(conv_done, 1)

                turns(pe, body)
                back(B - 1, SLOTS - 1)

            @block.scalar
            def _(act):
                fn = nc.scalar.activation

                def body(u, first, last):
                    for i in range(SLOTS):
                        m = SLOTS * u + i
                        act.wait_ge(hnT_done, m + 1)
                        fn(hT[:], M[:, 0:N], ACT.Identity, bias=beta[:], scale=gamma[:])\
                            .then_inc(hT_ready, 1)
                        act.wait_ge(conv_done, m + 1)
                        if not (first and i == 0):
                            act.wait_ge(cback_done, m)
                        fn(cT[:], conv_out[i % 2], ACT.Relu, bias=b_rel[:]).then_inc(cT_ready, 1)

                turns(act, body)

            @block.vector
            def _(dve):
                tt, ts = nc.vector.tensor_tensor, nc.vector.tensor_scalar

                def stats_x(m, i):
                    for c in range(C):
                        ins = nc.vector.bn_stats(
                            st3[:, c, :], X[:, ds(m, 1), c, :].rearrange("p b d -> p (b d)"))
                    ins.then_inc(st3_ready, 1)
                    dve.wait_ge(st3_ready, m + 1)
                    pass_gate(dve, dve_passed)
                    for c in range(C):
                        ins = nc.vector.bn_aggr(mv3[i % 2][:, c, :], st3[:, c, :])
                    ins.then_inc(mv3_ready, 1)
                    dve.wait_ge(mv3_ready, m + 1)
                    ts(var3[i % 2][:], mv3[i % 2][:, :, 1], EPS_LN, None, ALU.add)\
                        .then_inc(var3_ready, 1)

                def outer_norm(m, i):
                    h = h1[i % 2]
                    dve.wait_ge(rstd3_ready, m + 1)
                    for c in range(C):
                        ins = ts(h[:, c, :], X[:, ds(m, 1), c, :].rearrange("p b d -> p (b d)"),
                                 mv3[i % 2][:, c, 0:1], rstd3[i % 2][:, c:c + 1], ALU.subtract,
                                 ALU.mult)
                    ins.then_inc(xn3_ready, 1)
                    dve.wait_ge(xn3_ready, m + 1)
                    ts(h[:], h[:], 0.0, None, ALU.max).then_inc(h1_ready, 1)
                    dve.wait_ge(h1_ready, m + 1)
                    pass_gate(dve, dve_passed)
                    for c in range(C):
                        ins = nc.vector.bn_stats(st_h[:, c, :], h[:, c, :])
                    ins.then_inc(sth_ready, 1)
                    dve.wait_ge(sth_ready, m + 1)
                    pass_gate(dve, dve_passed)
                    for c in range(C):
                        ins = nc.vector.bn_aggr(mv_h[:, c, :], st_h[:, c, :])
                    ins.then_inc(mvh_ready, 1)
                    dve.wait_ge(mvh_ready, m + 1)
                    ts(var_h[:], mv_h[:, :, 1], EPS_LN, None, ALU.add).then_inc(varh_ready, 1)

                def inner_norm(m, i, first):
                    dve.wait_ge(rstdh_ready, m + 1)
                    if not first:
                        dve.wait_ge(hnT_done, m)
                    for c in range(C):
                        ins = ts(hn[:, c, :], h1[i % 2][:, c, :], mv_h[:, c, 0:1],
                                 rstd_h[:, c:c + 1], ALU.subtract, ALU.mult)
                    ins.then_inc(hn_ready, 1)

                def finish(m, i, u, free):
                    dve.wait_ge(cback_done, m + 1)
                    dve.wait_ge(xh_ready, m + 1)
                    if not free:
                        dve.wait_ge(out_stored[i % 2], 16 * (SLOTS // 2 * u + i // 2))
                    tt(ob[i % 2][:], back_out[i % 2], xh[i % 2][:], ALU.add)\
                        .then_inc(out_ready, 1)

                def body(u, first, last):
                    for i in range(SLOTS):
                        m = SLOTS * u + i
                        if not (last and i >= SLOTS - 2):
                            stats_x(m + 2, i)
                        dve.wait_ge(hw_done, m + 1)
                        nc.vector.tensor_copy(hw[:], Z[0:P, :, :]).then_inc(hw_ready, 1)
                        if not (last and i == SLOTS - 1):
                            outer_norm(m + 1, i + 1)
                        if not (first and i == 0):
                            if i == 0:
                                finish(m - 1, SLOTS - 1, u - 1, False)
                            else:
                                finish(m - 1, i - 1, u, first and i <= 2)
                        if not (last and i == SLOTS - 1):
                            inner_norm(m + 1, i + 1, False)

                stats_x(0, 0)
                stats_x(1, 1)
                outer_norm(0, 0)
                inner_norm(0, 0, True)
                turns(dve, body)
                finish(B - 1, SLOTS - 1, TURNS - 1, False)


def kernel(**inputs):
    import concourse.bacc as bacc
    from concourse.bass_utils import run_bass_kernel_spmd

    a = {k: np.asarray(v) for k, v in inputs.items()}

    def rep(v, rows):
        return np.broadcast_to(v, (rows,) + v.shape)

    member = np.zeros((G, GN), np.float32)
    for g, nodes in enumerate(GROUPS):
        member[g, nodes] = 1.0
    pair_mask = member[:, :, None] * member[:, None, :]
    blocks = np.zeros((GB, GN, GB, GN), np.float32)
    for i in range(GB):
        blocks[i, :, i, :] = 1.0
    a_l1 = a["L1_gnn_a"]
    layout = {
        "x": a["x"],
        "adj": a["adj"],
        "adjT": a["adj"].transpose(0, 2, 1),
        "ident": np.eye(128, dtype=np.float32),
        "off_diag": 1 - np.eye(P, dtype=np.float32),
        "wqT": a["L0_gnn_W_attn"].transpose(2, 0, 1),
        "w0T": a["L0_gnn_W0"].transpose(2, 0, 1),
        "w1T": a["L0_gnn_W1"].transpose(2, 0, 1),
        "bq": a["L0_gnn_b_attn"].T,
        "b0": a["L0_gnn_b0"].T,
        "b1": a["L0_gnn_b1"].T,
        "wfT": a["L0_gnn_Wf"].T,
        "bf_rows": rep(a["L0_gnn_bf"], P),
        "w_l1": a["L1_gnn_W"],
        "w_l1T": a["L1_gnn_W"].T,
        "a_rep": np.concatenate([np.broadcast_to(a_l1[D:], (D, D)), a_l1[:D]], axis=1),
        "w1g": a["L2_gnn_W1"].transpose(1, 0, 2),
        "w2g": a["L2_gnn_W2"].reshape(G, 2, D, D).transpose(2, 0, 1, 3),
        "b1g": a["L2_gnn_b1"].reshape(G, 2, D).transpose(2, 0, 1),
        "b2g": a["L2_gnn_b2"].T,
        "fw": rep(a["L2_gnn_fusion_w"], D),
        "gmask": np.tile(pair_mask.transpose(1, 0, 2), (GB, 1, 1)),
        "eye25": np.tile(np.eye(GN, dtype=np.float32), (GB, 1)),
        "block_mask": blocks.reshape(R, GB, GN),
        "node_mask": rep(member, D),
        "adj25": a["adj"][:, :GN, :GN].reshape(BLK, R, GN).transpose(1, 0, 2),
        "w_rel": a["L3_gnn_W_rel"],
        "w_root": a["L3_gnn_W_root"],
        "b_rel": a["L3_gnn_b_rel"][:, None],
        "gamma": a["L3_gnn_ln_gamma"][:, None],
        "beta": a["L3_gnn_ln_beta"][:, None],
    }
    nc = bacc.Bacc("TRN2", target_bir_lowering=False, num_devices=1)
    arrays, t = {}, {}
    for name, v in layout.items():
        v = np.ascontiguousarray(v)
        arrays[f"in_{name}"] = v
        t[name] = nc.dram_tensor(f"in_{name}", v.shape, mybir.dt.from_np(v.dtype),
                                 kind="ExternalInput").ap()
    out = nc.dram_tensor("out_x", (B, N, D), F32, kind="ExternalOutput").ap()
    build(nc, t, out)
    r = run_bass_kernel_spmd(nc, [arrays], core_ids=[0])
    return r.results[0]["out_x"]
```

```python
from contextlib import ExitStack

import numpy as np

import concourse.bass as bass
from concourse import mybir

F32 = mybir.dt.float32
ALU = mybir.AluOpType
ACT = mybir.ActivationFunctionType
AX_X = mybir.AxisListType.X
ds = bass.ds

B, N, D = 16, 500, 128
LAYERS = 7
C, P = 4, 125
LANES = 2
PAIRS = B // LANES
STEPS = LAYERS * LANES
EPS_LN = 1e-5
EPS_EYE = 1e-5
NEG_INF = -9000000000000000.0
SLOPE = 0.2
GROUPS = [list(range(25)), [0, 1, 2, 3, 4, 5, 6, 7, 8], [0, 9, 10, 11, 12, 13, 14],
          [6, 7, 8, 12, 13, 14], [3, 4, 5, 9, 10, 11]]
G, GN, HID = len(GROUPS), 25, 256
FREE = 1
GB = 4
BLK = B // GB
R = GB * GN
GQ = G * BLK


def build(nc, t, out):
    ctx = ExitStack()
    with ctx:
        def sb(name, shape):
            return ctx.enter_context(nc.sbuf_tensor(name, shape, F32))

        def sem(name):
            return ctx.enter_context(nc.semaphore(name))

        ident = sb("ident", [128, 128])
        wqT = sb("wqT", [D, LAYERS, D])
        w0T = sb("w0T", [D, LAYERS, D])
        w1T = sb("w1T", [D, LAYERS, D])
        bq = sb("bq", [D, LAYERS])
        b0 = sb("b0", [D, LAYERS])
        b1 = sb("b1", [D, LAYERS])
        wfT = sb("wfT", [D, D])
        bf_rows = sb("bf_rows", [P, D])
        w_l1T = sb("w_l1T", [D, D])
        a_rep = sb("a_rep", [D, D + 1])
        w_aug = sb("w_aug", [D, D + 1])
        wa2_rep = sb("wa2_rep", [D, D])
        w1g = sb("w1g", [D, G, HID])
        w2g = sb("w2g", [D, G, 2, D])
        b1g = sb("b1g", [D, G, 2])
        b2g = sb("b2g", [D, G])
        fw = sb("fw", [D, G])
        gmask = sb("gmask", [R, G, GN])
        eye25 = sb("eye25", [R, GN])
        block_mask = sb("block_mask", [R, GB, GN])
        node_mask = sb("node_mask", [D, G, GN])
        adj25 = sb("adj25", [R, BLK, GN])
        w_rel = sb("w_rel", [D, D])
        w_root = sb("w_root", [D, D])
        b_rel = sb("b_rel", [D, 1])
        gamma = sb("gamma", [D, 1])
        beta = sb("beta", [D, 1])
        neg_half = sb("neg_half", [128, G * BLK])
        wq_now = sb("wq_now", [D, D])
        w1_now = sb("w1_now", [D, D])
        bq_now = sb("bq_now", [D, 1])
        b0_now = sb("b0_now", [D, 1])
        b1_now = sb("b1_now", [D, 1])

        X = sb("X", [P, B, C, D])
        adjT = [sb(f"adjT{a}", [P, 2, C, N]) for a in range(LANES)]
        adjN = [sb(f"adjN{a}", [P, C, N]) for a in range(LANES)]
        off_diag = sb("off_diag", [P, P])
        stats = sb("stats", [P, 2 * LANES * C, 6])
        mv = sb("mv", [P, 2 * LANES * C, 2])
        var_eps = sb("var_eps", [P, 2 * LANES * C])
        rstd = sb("rstd", [P, 2 * LANES * C])
        adj_self = sb("adj_self", [R, BLK, G, GN])
        deg = sb("deg", [R, GQ])
        dinv = sb("dinv", [R, GQ])
        is_zero = sb("is_zero", [R, GQ])
        not_zero = sb("not_zero", [R, GQ])
        adj_blocks = sb("adj_blocks", [R, GQ, R])
        st25 = sb("st25", [GN, B, 6])
        mv25 = sb("mv25", [GN, B, 2])
        var25 = sb("var25", [GN, B])
        rstd25 = sb("rstd25", [GN, B])
        xn25 = sb("xn25", [GN, B, D])
        gnn01 = ExitStack()

        def sb01(name, shape):
            return gnn01.enter_context(nc.sbuf_tensor(name, shape, F32))

        xT = [sb01(f"xT{a}", [D, N]) for a in range(LANES)]
        qT = sb01("qT", [D, N])
        S = sb01("S", [P, C, N])
        zaug = [sb01(f"zaug{a}", [P, C, D + 1]) for a in range(LANES)]
        ysum = sb01("ysum", [P, C, D + 1])
        yrec = sb01("yrec", [P, C])
        yn = sb01("yn", [P, C, D])
        tT = sb01("tT", [D, N])
        uT = sb01("uT", [D, N])
        xn = [sb01(f"xn{i}", [P, C, D]) for i in range(LANES + 1)]
        hT = [sb01(f"hT{a}", [D, N]) for a in range(LANES)]
        haug = [sb01(f"haug{a}", [P, C, D + 1]) for a in range(LANES)]
        dst = [sb01(f"dst{a}", [P, N]) for a in range(LANES)]
        E = [sb01(f"E{a}", [P, N]) for a in range(LANES)]
        pen = [sb01(f"pen{a}", [P, N]) for a in range(LANES)]
        PT = [sb01(f"PT{a}", [P, C, P]) for a in range(LANES)]
        rowmax = sb01("rowmax", [P, LANES])
        negmax = sb01("negmax", [P, LANES])
        expsum = sb01("expsum", [P, LANES])
        exprec = sb01("exprec", [P, LANES])

        L = ctx.enter_context(nc.psum_tensor("L", [128, 4, 512], F32))
        Y = ctx.enter_context(nc.psum_tensor("Y", [128, 2, 512], F32))
        Z = ctx.enter_context(nc.psum_tensor("Z", [128, C, D], F32))
        M = ctx.enter_context(nc.psum_tensor("M", [128, 512], F32))
        LOGIT = [L[0:P, c % 2, 0:N] for c in range(C)]
        TR = L[:, 2, :]
        ATT = L[:, 3, :]

        TAIL_TR, TAIL_ATT = [M, TR], [L[:, 0, :], ATT]

        def y_out(c):
            return Y[0:P, c // 2, (c % 2) * (D + 1):(c % 2 + 1) * (D + 1)]

        start_loaded, first_loaded, consts_loaded = (sem("start_loaded"), sem("first_loaded"),
                                                     sem("consts_loaded"))
        x_loaded = sem("x_loaded")
        adjT_loaded = [sem(f"adjT_loaded{a}") for a in range(LANES)]
        adjN_loaded = [sem(f"adjN_loaded{a}") for a in range(LANES)]
        diag_cut = [sem(f"diag_cut{a}") for a in range(LANES)]
        diag_set = [sem(f"diag_set{a}") for a in range(LANES)]
        half_set = sem("half_set")
        ones_set = sem("ones_set")
        wa_done, wa_ready = sem("wa_done"), sem("wa_ready")
        stats_ready = [sem(f"stats_ready{i}") for i in range(2)]
        mv_ready = [sem(f"mv_ready{i}") for i in range(2)]
        var_ready = [sem(f"var_ready{i}") for i in range(2)]
        rstd_ready = [sem(f"rstd_ready{i}") for i in range(2)]
        xn_ready = [sem(f"xn_ready{i}") for i in range(2)]
        lnT_done = [sem(f"lnT_done{i}") for i in range(2)]
        lnh_ready = [sem(f"lnh_ready{i}") for i in range(2)]
        wq_ready, w1_ready = sem("wq_ready"), sem("w1_ready")
        q_done, qT_ready = sem("q_done"), sem("qT_ready")
        z_done, z_ready = sem("z_done"), sem("z_ready")
        logit_done, sig_ready, S_ready = sem("logit_done"), sem("sig_ready"), sem("S_ready")
        y_done, ysum_ready, yrec_ready, yn_ready = (sem("y_done"), sem("ysum_ready"),
                                                    sem("yrec_ready"), sem("yn_ready"))
        t_done, tT_ready = sem("t_done"), sem("tT_ready")
        w_done, uT_ready, x_ready = sem("w_done"), sem("uT_ready"), sem("x_ready")
        fin_done, x1_part, x1_ready = sem("fin_done"), sem("x1_part"), sem("x1_ready")
        dst_done, dst_ready = sem("dst_done"), sem("dst_ready")
        h_done, haug_ready = sem("h_done"), sem("haug_ready")
        pen_ready, e_ready, leaky_ready = sem("pen_ready"), sem("e_ready"), sem("leaky_ready")
        max_ready, negmax_ready = sem("max_ready"), sem("negmax_ready")
        p_ready, pT_done, PT_ready, att_done = (sem("p_ready"), sem("pT_done"), sem("PT_ready"),
                                                sem("att_done"))
        exprec_ready, x2_ready = sem("exprec_ready"), sem("x2_ready")
        dve_passed, pool_passed = sem("dve_passed"), sem("pool_passed")

        self_ready, deg_step, deg_ready = sem("self_ready"), sem("deg_step"), sem("deg_ready")
        dinv_ready, scaled_ready, blocks_ready = (sem("dinv_ready"), sem("scaled_ready"),
                                                  sem("blocks_ready"))
        st25_ready, mv25_ready, var25_ready = (sem("st25_ready"), sem("mv25_ready"),
                                               sem("var25_ready"))
        rstd25_ready, xn25_ready = sem("rstd25_ready"), sem("xn25_ready")

        start_loads = [
            (ident[:], t["ident"]), (bq[:], t["bq"]), (wqT[:], t["wqT"]), (w0T[:], t["w0T"]),
        ]
        first_loads = [
            (off_diag[:], t["off_diag"]), (w1T[:], t["w1T"]), (b0[:], t["b0"]),
            (b1[:], t["b1"]), (wfT[:], t["wfT"]), (bf_rows[:], t["bf_rows"]),
        ]
        const_loads = [
            (w_l1T[:], t["w_l1T"]),
            (w_aug[:, 0:D], t["w_l1"]), (a_rep[:], t["a_rep"]), (w1g[:], t["w1g"]),
            (w2g[:], t["w2g"]), (b1g[:], t["b1g"]), (b2g[:], t["b2g"]), (fw[:], t["fw"]),
            (gmask[:], t["gmask"]), (eye25[:], t["eye25"]), (block_mask[:], t["block_mask"]),
            (node_mask[:], t["node_mask"]), (adj25[:], t["adj25"]), (w_rel[:], t["w_rel"]),
            (w_root[:], t["w_root"]), (b_rel[:], t["b_rel"]), (gamma[:], t["gamma"]),
            (beta[:], t["beta"]),
        ]
        start_value = 16 * len(start_loads)
        first_value = 16 * len(first_loads)
        consts_value = 16 * len(const_loads)
        x_rows = t["x"].rearrange("b (c p) d -> p b c d", p=P)
        adjT_rows = t["adjT"].rearrange("b (c p) n -> p b c n", p=P)
        adjN_rows = t["adj"].rearrange("b (c p) n -> p b c n", p=P)

        def pass_gate(eng, passed):
            eng.sem_inc(passed, 1)

        def chunk(c, width=P):
            return slice(c * width, (c + 1) * width)

        def lane_layer(a, p, l):
            return STEPS * p + LANES * l + a

        def lane_chunk(a, p, c):
            return LANES * C * p + LANES * c + a

        FIRST_SIDE, LAST_SIDE = 2, 2 + C

        def other(a, l):
            return (1, l - 1) if a == 0 else (0, l)

        def run_pairs(eng, turn, tail):
            turn(0, True, False)
            with eng.Fori(1, PAIRS - 1) as p:
                turn(p, False, False)
            turn(PAIRS - 1, False, True)
            tail(PAIRS - 1)

        def run_layers(eng, p, first, half):
            for l in (0, 1):
                for a in range(LANES):
                    half(a, p, l, l, first)
            with eng.Fori(FIRST_SIDE, LAST_SIDE) as l:
                for a in range(LANES):
                    half(a, p, l, "chunk", first)
            for a in range(LANES):
                half(a, p, LAYERS - 1, "last", first)

        with nc.Block() as block:

            @block.sync
            def _(sp):
                def load_x(p):
                    sp.dma_start(X[:, ds(p * LANES, LANES)], x_rows[:, ds(p * LANES, LANES)])\
                        .then_inc(x_loaded, 16)

                def load_adjT(a, p):
                    sp.dma_start(adjT[a][:, ds(p % 2, 1)].rearrange("p o c n -> p (o c) n"),
                                 adjT_rows[:, ds(p * LANES + a, 1)]
                                 .rearrange("p b c n -> p (b c) n")).then_inc(adjT_loaded[a], 16)

                def load_adjN(a, p):
                    sp.dma_start(adjN[a][:], adjN_rows[:, ds(p * LANES + a, 1)]
                                 .rearrange("p b c n -> p (b c) n")).then_inc(adjN_loaded[a], 16)

                load_x(0)
                for to, src in start_loads:
                    sp.dma_start(to, src).then_inc(start_loaded, 16)
                for to, src in first_loads:
                    sp.dma_start(to, src).then_inc(first_loaded, 16)
                for a in range(LANES):
                    load_adjT(a, 0)
                for to, src in const_loads:
                    sp.dma_start(to, src).then_inc(consts_loaded, 16)
                sp.wait_ge(x_loaded, 16)
                load_x(1)
                for a in range(LANES):
                    sp.wait_ge(adjT_loaded[a], 16)
                    load_adjT(a, 1)
                for a in range(LANES):
                    load_adjN(a, 0)
                with sp.Fori(1, PAIRS - 1) as p:
                    sp.wait_ge(x_loaded, 16 * p + 16)
                    load_x(p + 1)
                    for a in range(LANES):
                        sp.wait_ge(S_ready, C * (STEPS * p - LANES + a) + C)
                        sp.wait_ge(adjT_loaded[a], 16 * p + 16)
                        load_adjT(a, p + 1)
                    for a in range(LANES):
                        sp.wait_ge(pen_ready, lane_chunk(a, p - 1, C - 1) + 1)
                        load_adjN(a, p)
                for a in range(LANES):
                    sp.wait_ge(pen_ready, lane_chunk(a, PAIRS - 2, C - 1) + 1)
                    load_adjN(a, PAIRS - 1)

            @block.gpsimd
            def _(pool):
                nc.gpsimd.memset(neg_half[:], -0.5).then_inc(half_set, 1)
                for a in range(LANES):
                    nc.gpsimd.memset(zaug[a][:, :, D:D + 1], 1.0).then_inc(ones_set, 1)
                pool.wait_ge(half_set, 1)

                def set_diagonal(a, p):
                    blocks = [adjT[a][:, ds(p % 2, 1), c, chunk(c)].rearrange("p o n -> p (o n)")
                              for c in range(C)]
                    pool.wait_ge(adjT_loaded[a], 16 * p + 16)
                    pass_gate(pool, pool_passed)
                    for c in range(C):
                        ins = nc.gpsimd.tensor_tensor(blocks[c], blocks[c], off_diag[:], ALU.mult)
                    ins.then_inc(diag_cut[a], 1)
                    pool.wait_ge(diag_cut[a], p + 1)
                    pass_gate(pool, pool_passed)
                    for c in range(C):
                        ins = nc.gpsimd.tensor_tensor(blocks[c], blocks[c], ident[0:P, 0:P],
                                                      ALU.add)
                    ins.then_inc(diag_set[a], 1)

                def pow_ln(g, a, m):
                    cols = chunk(LANES * g + a, C)
                    pool.wait_ge(var_ready[g], m + 1)
                    nc.gpsimd.tensor_tensor(rstd[:, cols], var_eps[:, cols], neg_half[0:P, 0:C],
                                            ALU.pow).then_inc(rstd_ready[g], 1)

                def current_wq(p, l):
                    pool.wait_ge(qT_ready, lane_layer(0, p, l) + FREE)
                    pass_gate(pool, pool_passed)
                    nc.gpsimd.tensor_copy(wq_now[:], wqT[:, ds(l, 1)].rearrange("p l n -> p (l n)"))
                    nc.gpsimd.tensor_copy(bq_now[:], bq[:, ds(l, 1)]).then_inc(wq_ready, 1)

                def current_w1(p, l):
                    pool.wait_ge(uT_ready, lane_layer(0, p, l) + FREE)
                    pass_gate(pool, pool_passed)
                    nc.gpsimd.tensor_copy(w1_now[:], w1T[:, ds(l, 1)].rearrange("p l n -> p (l n)"))
                    nc.gpsimd.tensor_copy(b0_now[:], b0[:, ds(l, 1)])
                    nc.gpsimd.tensor_copy(b1_now[:], b1[:, ds(l, 1)]).then_inc(w1_ready, 1)

                def turn(p, first):
                    if first:
                        pool.wait_ge(start_loaded, start_value)
                    current_wq(p, 0)
                    if first:
                        pool.wait_ge(first_loaded, first_value)
                    current_w1(p, 0)
                    if first:
                        for a in range(LANES):
                            set_diagonal(a, 0)
                    if not first:
                        pow_ln(1, 0, LANES * p - LANES)
                    current_wq(p, 1)
                    if not first:
                        pow_ln(1, 1, LANES * p - LANES + 1)
                    current_w1(p, 1)
                    with pool.Fori(FIRST_SIDE, LAST_SIDE) as l:
                        current_wq(p, l)
                        current_w1(p, l)
                    for a in range(LANES):
                        set_diagonal(a, p + 1)
                    current_wq(p, LAYERS - 1)
                    current_w1(p, LAYERS - 1)
                    for a in range(LANES):
                        pow_ln(0, a, LANES * (p + 1) + a)

                for a in range(LANES):
                    pow_ln(0, a, a)
                turn(0, True)
                with pool.Fori(1, PAIRS - 1) as p:
                    turn(p, False)
                p = PAIRS - 1
                current_wq(p, 0)
                current_w1(p, 0)
                pow_ln(1, 0, LANES * p - LANES)
                current_wq(p, 1)
                pow_ln(1, 1, LANES * p - LANES + 1)
                current_w1(p, 1)
                with pool.Fori(FIRST_SIDE, LAYERS) as l:
                    current_wq(p, l)
                    current_w1(p, l)
                pool.wait_ge(consts_loaded, consts_value)
                for q in range(BLK):
                    nc.gpsimd.tensor_tensor(
                        adj_self[:, q], adj25[:, q:q + 1, :].to_broadcast([R, G, GN]),
                        eye25[:].rearrange("p (g m) -> p g m", g=1).to_broadcast([R, G, GN]),
                        ALU.add).then_inc(self_ready, 1)
                for q in range(BLK):
                    pool.wait_ge(self_ready, BLK + q)
                    nc.gpsimd.tensor_tensor(adj_self[:, q], adj_self[:, q], gmask[:], ALU.mult)\
                        .then_inc(self_ready, 1)
                pow_ln(1, 0, LANES * p)
                pool.wait_ge(deg_ready, 1)
                nc.gpsimd.tensor_tensor(dinv[:], deg[:], neg_half[0:R, 0:GQ], ALU.pow)\
                    .then_inc(dinv_ready, 1)
                pool.wait_ge(dinv_ready, 1)
                nc.gpsimd.tensor_tensor(dinv[:], dinv[:], not_zero[:], ALU.mult)\
                    .then_inc(dinv_ready, 1)
                pow_ln(1, 1, LANES * p + 1)
                pool.wait_ge(var25_ready, 1)
                nc.gpsimd.tensor_tensor(rstd25[:, 0:B - LANES], var25[:, 0:B - LANES],
                                        neg_half[0:GN, 0:B - LANES], ALU.pow)\
                    .then_inc(rstd25_ready, 1)
                pool.wait_ge(dinv_ready, 2)
                flat = adj_self[:].rearrange("p q g m -> p (q g) m")
                nc.gpsimd.tensor_tensor(
                    flat, flat, dinv[:].rearrange("p (i o) -> p i o", o=1)
                    .to_broadcast([R, GQ, GN]), ALU.mult).then_inc(scaled_ready, 1)
                pool.wait_ge(var25_ready, 2)
                nc.gpsimd.tensor_tensor(rstd25[:, B - LANES:B], var25[:, B - LANES:B],
                                        neg_half[0:GN, 0:LANES], ALU.pow)\
                    .then_inc(rstd25_ready, 1)
                pool.wait_ge(scaled_ready, 1)
                for i in range(GQ):
                    ins = nc.gpsimd.tensor_tensor(
                        adj_blocks[:, i, :].rearrange("p (k m) -> p k m", k=GB),
                        flat[:, i:i + 1, :].to_broadcast([R, GB, GN]), block_mask[:], ALU.mult)
                ins.then_inc(blocks_ready, 1)

            @block.tensor
            def _(pe):
                mm = nc.tensor.matmul

                def ln_transpose(g, a, m):
                    pe.wait_ge(xn_ready[g], m + 1)
                    src = xn[a] if g == 0 else xn[LANES]
                    for c in range(C):
                        ins = nc.tensor.transpose(TR[:, chunk(c)], src[:, c, :], ident[0:P, 0:P])
                    ins.then_inc(lnT_done[g], 1)

                def q_and_z(a, p, l, z_free, z_count):
                    w0_layer = w0T[:, ds(l, 1)].rearrange("p l n -> p (l n)")
                    if a == 0:
                        pe.wait_ge(wq_ready, LAYERS * p + l + 1)
                    mm(M[:, 0:N], wq_now[:], xT[a][:], start=True, stop=True).then_inc(q_done, 1)
                    pe.wait_ge(z_free, z_count)
                    for c in range(C):
                        ins = mm(Z[0:P, c, :], xT[a][:, chunk(c)], w0_layer, start=True, stop=True)
                    ins.then_inc(z_done, 1)

                def logits(a, p, l, c):
                    n = lane_layer(a, p, l)
                    if c >= 2:
                        pe.wait_ge(sig_ready, C * n + c - 1)
                    mm(LOGIT[c], xT[a][:, chunk(c)], qT[:], start=True, stop=True)\
                        .then_inc(logit_done, 1)

                def y_sum(a, p, l):
                    n = lane_layer(a, p, l)
                    pe.wait_ge(z_ready, n + 1 + FREE)
                    pe.wait_ge(S_ready, C * n + C)
                    for ic in range(C):
                        for jc in range(C):
                            ins = mm(y_out(ic), S[:, jc, chunk(ic)], zaug[a][:, jc, :],
                                     start=(jc == 0), stop=(jc == C - 1))
                        if ic % 2:
                            ins.then_inc(y_done, 1)

                def y_transpose(a, p, l, h):
                    n = lane_layer(a, p, l)
                    pe.wait_ge(yn_ready, 2 * n + h + 1)
                    for c in range(2 * h, 2 * h + 2):
                        ins = nc.tensor.transpose(M[:, chunk(c)], yn[:, c, :], ident[0:P, 0:P])
                    if h:
                        ins.then_inc(t_done, 1)

                def second_linear(a, p, l):
                    n = lane_layer(a, p, l)
                    pe.wait_ge(w1_ready, LAYERS * p + l + 1)
                    pe.wait_ge(tT_ready, n + 1)
                    mm(M[:, 0:N], w1_now[:], tT[:], start=True, stop=True).then_inc(w_done, 1)

                def final_linear(a, p, z_read):
                    pe.wait_ge(x_ready, lane_layer(a, p, LAYERS - 1) + 1)
                    if z_read:
                        pe.wait_ge(*z_read)
                    for c in range(C):
                        ins = mm(Z[0:P, c, :], xT[a][:, chunk(c)], wfT[:], start=True, stop=True)
                    ins.then_inc(fin_done, 1)

                def gnn1_project(a, p):
                    pe.wait_ge(lnh_ready[1], LANES * p + a + 1)
                    mm(ATT[0:P, 0:N], wa2_rep[:, 0:P], hT[a][:], start=True, stop=True)\
                        .then_inc(dst_done, 1)
                    for c in range(C - 1):
                        mm(TR[0:P, chunk(c, D + 1)], hT[a][:, chunk(c)], w_aug[:], start=True,
                           stop=True)

                def gnn1_project_last(a, p):
                    pe.wait_ge(dst_ready, LANES * p + a + 1)
                    mm(ATT[0:P, 0:D + 1], hT[a][:, chunk(C - 1)], w_aug[:], start=True, stop=True)\
                        .then_inc(h_done, 1)

                def probs_transpose(a, p, c, bank=TR):
                    pe.wait_ge(p_ready, lane_chunk(a, p, c) + 1)
                    for jc in range(C):
                        ins = nc.tensor.transpose(bank[0:P, chunk(jc)], E[a][:, chunk(jc)],
                                                  ident[0:P, 0:P])
                    ins.then_inc(pT_done, 1)

                def attend(a, p, c, bank=ATT, adds_since=0):
                    k = lane_chunk(a, p, c)
                    pe.wait_ge(PT_ready, k + 1)
                    pe.wait_ge(x2_ready, k - adds_since + FREE)
                    for jc in range(C):
                        ins = mm(bank[0:P, 0:D], PT[a][:, jc, :], haug[a][:, jc, 0:D],
                                 start=(jc == 0), stop=(jc == C - 1))
                    ins.then_inc(att_done, 1)

                def half(a, p, l, kind, first, last):
                    b, lb = other(a, l)
                    side = not first
                    end = not (first and kind == 0 and a == 0)
                    if kind == 0:
                        pe.wait_ge(lnh_ready[0], LANES * p + a + 1)
                        if first:
                            q_and_z(a, p, l, z_ready, lane_layer(a, p, l) + FREE)
                        else:
                            q_and_z(a, p, l, x1_part, LANES * (p - 1) + a + 1)
                    else:
                        pe.wait_ge(x_ready, lane_layer(a, p, l - 1) + 1)
                        q_and_z(a, p, l, z_ready, lane_layer(a, p, l) + FREE)
                    if end:
                        y_sum(b, p, lb)
                    pe.wait_ge(qT_ready, lane_layer(a, p, l) + 1 + FREE)
                    if end:
                        y_transpose(b, p, lb, 0)
                    if side and kind == 1:
                        if a == 1:
                            pe.wait_ge(haug_ready, LANES * (p - 1) + 1 + FREE)
                        ln_transpose(1, a, LANES * (p - 1) + a)
                    if side and kind == "chunk" and a == 1:
                        pe.wait_ge(haug_ready, LANES * p + FREE)
                        probs_transpose(0, p - 1, l - FIRST_SIDE)
                    logits(a, p, l, 0)
                    if end:
                        y_transpose(b, p, lb, 1)
                    logits(a, p, l, 1)
                    if end:
                        second_linear(b, p, lb)
                    if side and kind == 1:
                        gnn1_project(a, p - 1)
                    if side and kind == "chunk" and a == 1:
                        attend(0, p - 1, l - FIRST_SIDE)
                        probs_transpose(1, p - 1, l - FIRST_SIDE)
                    logits(a, p, l, 2)
                    if kind == 0 and a == 0:
                        ln_transpose(0, 1, LANES * p + 1)
                        if not first:
                            final_linear(1, p - 1, (z_ready, lane_layer(0, p, 0) + 1 + FREE))
                    if kind == "last" and a == 1:
                        if not last:
                            ln_transpose(0, 0, LANES * (p + 1))
                        final_linear(0, p, (z_ready, lane_layer(1, p, l) + 1 + FREE))
                    logits(a, p, l, 3)
                    if side and kind == 1:
                        gnn1_project_last(a, p - 1)
                    if side and kind == "chunk" and a == 1:
                        attend(1, p - 1, l - FIRST_SIDE)

                def turn(p, first, last):
                    run_layers(pe, p, first, lambda a, p, l, kind, first:
                               half(a, p, l, kind, first, last))
                    if first:
                        pe.wait_ge(consts_loaded, consts_value)
                        mm(ATT[:, 0:D + 1], w_l1T[:], a_rep[:], start=True, stop=True)\
                            .then_inc(wa_done, 1)
                        pe.wait_ge(wa_ready, 2)

                pe.wait_ge(start_loaded, start_value)
                ln_transpose(0, 0, 0)
                turn(0, True, False)
                with pe.Fori(1, PAIRS - 1) as p:
                    turn(p, False, False)
                turn(PAIRS - 1, False, True)
                p = PAIRS - 1
                y_sum(1, p, LAYERS - 1)
                y_transpose(1, p, LAYERS - 1, 0)
                y_transpose(1, p, LAYERS - 1, 1)
                ln_transpose(1, 0, LANES * p)
                second_linear(1, p, LAYERS - 1)
                gnn1_project(0, p)
                gnn1_project_last(0, p)
                final_linear(1, p, (x1_part, LANES * p + 1))
                pe.wait_ge(haug_ready, LANES * p + 1 + FREE)
                ln_transpose(1, 1, LANES * p + 1)
                gnn1_project(1, p)
                gnn1_project_last(1, p)
                pe.wait_ge(uT_ready, lane_layer(1, p, LAYERS - 1) + 1 + FREE)
                pe.wait_ge(sig_ready, C * STEPS * PAIRS)
                probs_transpose(0, p, 0, TAIL_TR[0])
                pe.wait_ge(haug_ready, LANES * p + 2 + FREE)
                steps = [(c, a) for c in range(C) for a in range(LANES)]
                for (c, a), following in zip(steps, steps[1:] + [None]):
                    if following:
                        next_c, next_a = following
                        probs_transpose(next_a, p, next_c, TAIL_TR[next_a])
                    attend(a, p, c, TAIL_ATT[a], 1 if c else 0)

            @block.scalar
            def _(act):
                fn = nc.scalar.activation
                act.sem_inc(qT_ready, FREE)
                act.sem_inc(uT_ready, FREE)

                def ln_relu(g, a, m, after_final):
                    act.wait_ge(lnT_done[g], m + 1)
                    if after_final is not None:
                        act.wait_ge(fin_done, after_final)
                    fn((hT if g else xT)[a][:], TR[:, 0:N], ACT.Relu).then_inc(lnh_ready[g], 1)

                def q_out(a, p, l):
                    act.wait_ge(q_done, lane_layer(a, p, l) + 1)
                    fn(qT[:], M[:, 0:N], ACT.Identity, bias=bq_now[:]).then_inc(qT_ready, 1)

                def sigmoid(a, p, l, c):
                    act.wait_ge(logit_done, C * lane_layer(a, p, l) + c + 1)
                    fn(S[:, c, :], LOGIT[c], ACT.Sigmoid).then_inc(sig_ready, 1)

                def t_out(a, p, l):
                    act.wait_ge(w1_ready, LAYERS * p + l + 1)
                    act.wait_ge(t_done, lane_layer(a, p, l) + 1)
                    fn(tT[:], M[:, 0:N], ACT.Relu, bias=b0_now[:]).then_inc(tT_ready, 1)

                def u_out(a, p, l):
                    act.wait_ge(w_done, lane_layer(a, p, l) + 1)
                    fn(uT[:], M[:, 0:N], ACT.Relu, bias=b1_now[:]).then_inc(uT_ready, 1)

                def dst_out(a, p):
                    act.wait_ge(dst_done, LANES * p + a + 1)
                    fn(dst[a][:], ATT[0:P, 0:N], ACT.Copy).then_inc(dst_ready, 1)

                def exp(a, p, c):
                    act.wait_ge(negmax_ready, lane_chunk(a, p, c) + 1)
                    fn(E[a][:], E[a][:], ACT.Exp, bias=negmax[:, a:a + 1],
                       accum_out=expsum[:, a:a + 1]).then_inc(p_ready, 1)

                def probs_out(a, p, c, bank=TR):
                    act.wait_ge(pT_done, lane_chunk(a, p, c) + 1)
                    fn(PT[a][:].rearrange("p c i -> p (c i)"), bank[0:P, 0:N], ACT.Copy)\
                        .then_inc(PT_ready, 1)

                def half(a, p, l, kind, first, last):
                    b, lb = other(a, l)
                    side = not first
                    end = not (first and kind == 0 and a == 0)
                    q_out(a, p, l)
                    if side and kind == "chunk" and a == 1:
                        exp(0, p - 1, l - FIRST_SIDE)
                        exp(1, p - 1, l - FIRST_SIDE)
                        nc.scalar.preload_act_table(ACT.Sigmoid)
                        probs_out(0, p - 1, l - FIRST_SIDE)
                    if side and kind == 1:
                        ln_relu(1, a, LANES * (p - 1) + a, None)
                    if end:
                        t_out(b, p, lb)
                    sigmoid(a, p, l, 0)
                    sigmoid(a, p, l, 1)
                    if end:
                        u_out(b, p, lb)
                    if side and kind == 1:
                        dst_out(a, p - 1)
                    if side and kind == "chunk" and a == 1:
                        probs_out(1, p - 1, l - FIRST_SIDE)
                    sigmoid(a, p, l, 2)
                    if kind == 0 and a == 0:
                        ln_relu(0, 1, LANES * p + 1, None if first else LANES * (p - 1) + 2)
                    if kind == "last" and a == 1 and not last:
                        ln_relu(0, 0, LANES * (p + 1), LANES * p + 1)
                    sigmoid(a, p, l, 3)

                def turn(p, first, last):
                    run_layers(act, p, first, lambda a, p, l, kind, first:
                               half(a, p, l, kind, first, last))

                def tail(p):
                    t_out(1, p, LAYERS - 1)
                    ln_relu(1, 0, LANES * p, None)
                    u_out(1, p, LAYERS - 1)
                    dst_out(0, p)
                    ln_relu(1, 1, LANES * p + 1, None)
                    exp(0, p, 0)
                    dst_out(1, p)
                    probs_out(0, p, 0, TAIL_TR[0])
                    for c in range(C):
                        for a in range(LANES):
                            if c or a:
                                exp(a, p, c)
                                if c:
                                    act.wait_ge(att_done, lane_chunk(a, p, c - 1) + 1)
                                probs_out(a, p, c, TAIL_TR[a])

                ln_relu(0, 0, 0, None)
                run_pairs(act, turn, tail)

            @block.vector
            def _(dve):
                tt, ts, stt = (nc.vector.tensor_tensor, nc.vector.tensor_scalar,
                               nc.vector.scalar_tensor_tensor)
                for ready in (z_ready, x2_ready, haug_ready):
                    dve.sem_inc(ready, FREE)
                dve.wait_ge(ones_set, LANES)

                def x_chunk(m, c):
                    return X[:, ds(m, 1), c, :].rearrange("p b d -> p (b d)")

                def ln_stats(g, a, m):
                    i = C * (LANES * g + a)
                    for c in range(C):
                        ins = nc.vector.bn_stats(stats[:, i + c, :], x_chunk(m, c))
                    ins.then_inc(stats_ready[g], 1)
                    dve.wait_ge(stats_ready[g], m + 1)
                    pass_gate(dve, dve_passed)
                    for c in range(C):
                        ins = nc.vector.bn_aggr(mv[:, i + c, :], stats[:, i + c, :])
                    ins.then_inc(mv_ready[g], 1)
                    dve.wait_ge(mv_ready[g], m + 1)
                    ts(var_eps[:, i:i + C], mv[:, i:i + C, 1], EPS_LN, None, ALU.add)\
                        .then_inc(var_ready[g], 1)

                def ln_rows(g, a, m):
                    i = C * (LANES * g + a)
                    to = xn[a] if g == 0 else xn[LANES]
                    dve.wait_ge(rstd_ready[g], m + 1)
                    for c in range(C):
                        ins = ts(to[:, c, :], x_chunk(m, c), mv[:, i + c, 0:1],
                                 rstd[:, i + c:i + c + 1], ALU.subtract, ALU.mult)
                    ins.then_inc(xn_ready[g], 1)

                def z_out(a, p, l):
                    dve.wait_ge(z_done, lane_layer(a, p, l) + 1)
                    nc.vector.tensor_copy(zaug[a][:, :, 0:D], Z[0:P, :, :]).then_inc(z_ready, 1)

                def mask(a, p, l, c):
                    dve.wait_ge(sig_ready, C * lane_layer(a, p, l) + c + 1)
                    tt(S[:, c, :], S[:, c, :],
                       adjT[a][:, ds(p % 2, 1), c, :].rearrange("p o n -> p (o n)"), ALU.mult)\
                        .then_inc(S_ready, 1)

                def y_norm(a, p, l):
                    n = lane_layer(a, p, l)
                    w = D + 1
                    for h in range(2):
                        dve.wait_ge(y_done, 2 * n + h + 1)
                        stt(ysum[:, 2 * h:2 * h + 2, :],
                            zaug[a][:, 2 * h:2 * h + 2, :], EPS_EYE,
                            Y[0:P, h, 0:2 * w].rearrange("p (c w) -> p c w", w=w),
                            ALU.mult, ALU.add).then_inc(ysum_ready, 1)
                        dve.wait_ge(ysum_ready, 2 * n + h + 1)
                        nc.vector.reciprocal(yrec[:, 2 * h:2 * h + 2], ysum[:, 2 * h:2 * h + 2, D])\
                            .then_inc(yrec_ready, 1)
                        dve.wait_ge(yrec_ready, 2 * n + h + 1)
                        for c in range(2 * h, 2 * h + 2):
                            ins = ts(yn[:, c, :], ysum[:, c, 0:D], yrec[:, c:c + 1], None,
                                     ALU.mult)
                        ins.then_inc(yn_ready, 1)

                def x_add(a, p, l):
                    dve.wait_ge(uT_ready, lane_layer(a, p, l) + 1 + FREE)
                    tt(xT[a][:], xT[a][:], uT[:], ALU.add).then_inc(x_ready, 1)

                def final_add(a, p):
                    m = LANES * p + a
                    x = X[:, ds(m, 1), :, :].rearrange("p b c d -> p (b c) d")
                    dve.wait_ge(fin_done, m + 1)
                    tt(x, x, Z[0:P, :, :], ALU.add).then_inc(x1_part, 1)

                def final_bias(a, p):
                    m = LANES * p + a
                    x = X[:, ds(m, 1), :, :].rearrange("p b c d -> p (b c) d")
                    dve.wait_ge(x1_part, m + 1)
                    tt(x, x, bf_rows[:].rearrange("p (c d) -> p c d", c=1)
                       .to_broadcast([P, C, D]), ALU.add).then_inc(x1_ready, 1)

                def haug_out(a, p):
                    flat = haug[a][:].rearrange("p c w -> p (c w)")
                    w = (C - 1) * (D + 1)
                    dve.wait_ge(h_done, LANES * p + a + 1)
                    nc.vector.tensor_copy(flat[:, 0:w], TR[0:P, 0:w])
                    nc.vector.tensor_copy(flat[:, w:w + D + 1], ATT[0:P, 0:D + 1])\
                        .then_inc(haug_ready, 1)

                def raw_scores(a, p, c):
                    dve.wait_ge(adjN_loaded[a], 16 * p + 16)
                    ts(pen[a][:], adjN[a][:, ds(c, 1), :].rearrange("p o n -> p (o n)"), 0.0,
                       NEG_INF, ALU.is_le, ALU.mult).then_inc(pen_ready, 1)
                    dve.wait_ge(haug_ready, LANES * p + a + 1 + FREE)
                    dve.wait_ge(dst_ready, LANES * p + a + 1)
                    ts(E[a][:], dst[a][:], haug[a][:, ds(c, 1), D:D + 1]
                       .rearrange("p o w -> p (o w)"), None, ALU.add).then_inc(e_ready, 1)

                def masked_scores(a, p, c):
                    k = lane_chunk(a, p, c)
                    dve.wait_ge(e_ready, k + 1)
                    stt(E[a][:], E[a][:], SLOPE, E[a][:], ALU.mult, ALU.max)\
                        .then_inc(leaky_ready, 1)
                    dve.wait_ge(pen_ready, k + 1)
                    dve.wait_ge(leaky_ready, k + 1)
                    pass_gate(dve, dve_passed)
                    nc.vector.tensor_tensor_reduce(
                        out=E[a][:], in0=E[a][:], in1=pen[a][:], scale=1.0, scalar=-3.0e38,
                        op0=ALU.add, op1=ALU.max, accum_out=rowmax[:, a:a + 1])\
                        .then_inc(max_ready, 1)
                    dve.wait_ge(max_ready, k + 1)
                    ts(negmax[:, a:a + 1], rowmax[:, a:a + 1], -1.0, None, ALU.mult)\
                        .then_inc(negmax_ready, 1)

                def sum_reciprocal(a, p, c):
                    dve.wait_ge(p_ready, lane_chunk(a, p, c) + 1)
                    nc.vector.reciprocal(exprec[:, a:a + 1], expsum[:, a:a + 1])\
                        .then_inc(exprec_ready, 1)

                def attention_add(a, p, c, bank=ATT):
                    k = lane_chunk(a, p, c)
                    m = LANES * p + a
                    x = X[:, ds(m, 1), ds(c, 1), :].rearrange("p b c d -> p (b c d)")
                    dve.wait_ge(exprec_ready, k + 1)
                    dve.wait_ge(att_done, k + 1)
                    stt(x, bank[0:P, 0:D], exprec[:, a:a + 1], x, ALU.mult, ALU.add)\
                        .then_inc(x2_ready, 1)

                def x25_stats(lo, hi, call):
                    for b in range(lo, hi):
                        ins = nc.vector.bn_stats(st25[:, b, :], X[0:GN, b, 0, :])
                    ins.then_inc(st25_ready, 1)
                    dve.wait_ge(st25_ready, call)
                    for b in range(lo, hi):
                        ins = nc.vector.bn_aggr(mv25[:, b, :], st25[:, b, :])
                    ins.then_inc(mv25_ready, 1)
                    dve.wait_ge(mv25_ready, call)
                    ts(var25[:, lo:hi], mv25[:, lo:hi, 1], EPS_LN, None, ALU.add)\
                        .then_inc(var25_ready, 1)

                def x25_rows(lo, hi, call):
                    dve.wait_ge(rstd25_ready, call)
                    for b in range(lo, hi):
                        ins = ts(xn25[:, b, :], X[0:GN, b, 0, :], mv25[:, b, 0:1],
                                 rstd25[:, b:b + 1], ALU.subtract, ALU.mult)
                    ins.then_inc(xn25_ready, 1)

                def half(a, p, l, kind, first, norms):
                    b, lb = other(a, l)
                    side = not first
                    end = not (first and kind == 0 and a == 0)
                    if side and kind == "chunk" and a == 0:
                        raw_scores(0, p - 1, l - FIRST_SIDE)
                    z_out(a, p, l)
                    if side and kind == 1:
                        if a == 1:
                            dve.wait_ge(lnT_done[1], LANES * (p - 1) + 1)
                        ln_rows(1, a, LANES * (p - 1) + a)
                    if norms:
                        dve.wait_ge(x_loaded, 16 * (p + 1) + 16)
                        pass_gate(dve, dve_passed)
                        ln_stats(0, a, LANES * (p + 1) + a)
                    if end:
                        y_norm(b, p, lb)
                    if side and kind == "chunk" and a == 0:
                        masked_scores(0, p - 1, l - FIRST_SIDE)
                    if kind == 0:
                        dve.wait_ge(diag_set[a], p + 1)
                    mask(a, p, l, 0)
                    mask(a, p, l, 1)
                    if end:
                        x_add(b, p, lb)
                    if side and kind == "chunk" and a == 0:
                        raw_scores(1, p - 1, l - FIRST_SIDE)
                    if side and kind == "chunk" and a == 1:
                        sum_reciprocal(0, p - 1, l - FIRST_SIDE)
                        attention_add(0, p - 1, l - FIRST_SIDE)
                    mask(a, p, l, 2)
                    if side and kind == 0 and a == 0:
                        final_add(1, p - 1)
                    if kind == "last" and a == 1:
                        final_add(0, p)
                    mask(a, p, l, 3)
                    if norms:
                        ln_rows(0, a, LANES * (p + 1) + a)
                    if side and kind == 0 and a == 0:
                        final_bias(1, p - 1)
                    if kind == "last" and a == 1:
                        final_bias(0, p)
                    if side and kind == 0:
                        dve.wait_ge(x1_ready, LANES * (p - 1) + a + 1)
                        pass_gate(dve, dve_passed)
                        ln_stats(1, a, LANES * (p - 1) + a)
                    if side and kind == 1:
                        haug_out(a, p - 1)
                    if side and kind == "chunk":
                        if a == 0:
                            masked_scores(1, p - 1, l - FIRST_SIDE)
                        else:
                            sum_reciprocal(1, p - 1, l - FIRST_SIDE)
                            attention_add(1, p - 1, l - FIRST_SIDE)

                def turn(p, first, last):
                    run_layers(dve, p, first, lambda a, p, l, kind, first:
                               half(a, p, l, kind, first, kind == "last" and not last))

                dve.wait_ge(x_loaded, 16)
                for a in range(LANES):
                    ln_stats(0, a, a)
                for a in range(LANES):
                    ln_rows(0, a, a)
                turn(0, True, False)
                dve.wait_ge(consts_loaded, consts_value)
                dve.wait_ge(wa_done, 1)
                nc.vector.tensor_copy(wa2_rep[:], ATT[:, 0:D]).then_inc(wa_ready, 1)
                nc.vector.tensor_copy(w_aug[:, D:D + 1], ATT[:, D:D + 1]).then_inc(wa_ready, 1)
                with dve.Fori(1, PAIRS - 1) as p:
                    turn(p, False, False)
                turn(PAIRS - 1, False, True)
                p = PAIRS - 1
                dve.wait_ge(self_ready, 2 * BLK)
                nc.vector.reduce_sum(deg[:], adj_self[:].rearrange("p q g m -> p (q g) m"),
                                     AX_X).then_inc(deg_step, 1)
                dve.wait_ge(deg_step, 1)
                ts(is_zero[:], deg[:], 0.0, None, ALU.is_equal).then_inc(deg_step, 1)
                ts(not_zero[:], deg[:], 0.0, None, ALU.not_equal).then_inc(deg_step, 1)
                dve.wait_ge(deg_step, 3)
                tt(deg[:], deg[:], is_zero[:], ALU.add).then_inc(deg_ready, 1)
                dve.wait_ge(x1_ready, LANES * p + 1)
                ln_stats(1, 0, LANES * p)
                y_norm(1, p, LAYERS - 1)
                ln_rows(1, 0, LANES * p)
                x_add(1, p, LAYERS - 1)
                haug_out(0, p)
                final_add(1, p)
                final_bias(1, p)
                dve.wait_ge(x1_ready, LANES * p + 2)
                ln_stats(1, 1, LANES * p + 1)
                raw_scores(0, p, 0)
                ln_rows(1, 1, LANES * p + 1)
                masked_scores(0, p, 0)
                x25_stats(0, B - LANES, 1)
                haug_out(1, p)
                raw_scores(1, p, 0)
                masked_scores(1, p, 0)
                for c in range(C):
                    for a in range(LANES):
                        sum_reciprocal(a, p, c)
                        if c + 1 < C:
                            dve.wait_ge(pT_done, lane_chunk(a, p, c) + 1)
                            raw_scores(a, p, c + 1)
                            masked_scores(a, p, c + 1)
                        attention_add(a, p, c, TAIL_ATT[a])
                    if c == 0:
                        dve.wait_ge(x2_ready, lane_chunk(LANES - 1, p, 0) + 1 + FREE)
                        x25_stats(B - LANES, B, 2)
                    if c == 1:
                        x25_rows(0, B - LANES, 1)
                        x25_rows(B - LANES, B, 2)

        gnn01.close()

        normT = sb("normT", [R, GQ, R])
        h25T = sb("h25T", [D, B * GN])
        sup1 = sb("sup1", [R, BLK, HID])
        hidT = sb("hidT", [D, 2, B * GN])
        sup2 = sb("sup2", [R, BLK, D])
        gout = sb("gout", [D, B * GN])
        fused = sb("fused", [D, B * GN])
        fsum = sb("fsum", [D, 4])
        fexp = sb("fexp", [D, G])
        wmask = sb("wmask", [D, G, GN])

        l2_step = sem("l2_step")
        adjTr_done, normT_ready = sem("adjTr_done"), sem("normT_ready")
        fmax_ready, fexp_ready = sem("fmax_ready"), sem("fexp_ready")
        x25T_done, h25_ready = sem("x25T_done"), sem("h25_ready")
        sup1_done, sup1_ready = sem("sup1_done"), sem("sup1_ready")
        hid_done, hid_ready = sem("hid_done"), sem("hid_ready")
        sup2_done, sup2_ready = sem("sup2_done"), sem("sup2_ready")
        gout_done, gout_ready, fused_ready = sem("gout_done"), sem("gout_ready"), sem("fused_ready")
        back_done, x3_ready = sem("back_done"), sem("x3_ready")
        adj3 = [adjT[a][:, i] for i in range(2) for a in range(LANES)]
        adj3_loaded = [sem(f"adj3_loaded{i}") for i in range(4)]

        def load_adj3(sp, i, b):
            sp.dma_start(adj3[i], adjT_rows[:, ds(b, 1)].rearrange("p b c n -> p (b c) n"))\
                .then_inc(adj3_loaded[i], 16)

        def rows(q):
            return slice(q * R, (q + 1) * R)

        def add_fused(dve, i):
            dve.wait_ge(back_done, 1)
            x = X[0:GN, 4 * i:4 * i + 4, 0, :]
            nc.vector.tensor_tensor(x, x, L[0:GN, i, :].rearrange("p (b d) -> p b d", b=4),
                                    ALU.add).then_inc(x3_ready, 1)

        with nc.Block() as block:

            @block.sync
            def _(sp):
                sp.wait_ge(S_ready, C * STEPS * PAIRS)
                sp.wait_ge(pen_ready, C * B)
                for i in range(4):
                    load_adj3(sp, i, i)

            @block.tensor
            def _(pe):
                mm = nc.tensor.matmul
                pe.wait_ge(xn25_ready, 2)
                pe.wait_ge(PT_ready, C * B)
                for b in range(B):
                    ins = nc.tensor.transpose(M[:, b * GN:(b + 1) * GN], xn25[:, b, :],
                                              ident[0:GN, 0:GN])
                ins.then_inc(x25T_done, 1)
                pe.wait_ge(blocks_ready, 1)
                pe.wait_ge(x2_ready, C * B + FREE)
                for i in range(GQ):
                    ins = nc.tensor.transpose(L[0:R, i // G, (i % G) * R:(i % G + 1) * R],
                                              adj_blocks[:, i, :], ident[0:R, 0:R])
                ins.then_inc(adjTr_done, 1)
                pe.wait_ge(h25_ready, 1)

                def support1(g):
                    if g:
                        pe.wait_ge(sup1_ready, g)
                    for q in range(BLK):
                        ins = mm(Y[0:R, q // 2, (q % 2) * HID:(q % 2 + 1) * HID],
                                 h25T[:, rows(q)], w1g[:, g, :], start=True, stop=True)
                    ins.then_inc(sup1_done, 1)

                def hidden(g):
                    pe.wait_ge(sup1_ready, g + 1)
                    if g:
                        pe.wait_ge(hid_ready, g)
                    for f in range(2):
                        for q in range(BLK):
                            ins = mm(L[:, f, rows(q)], sup1[:, q, f * D:(f + 1) * D],
                                     normT[:, q * G + g, :], start=True, stop=True)
                    ins.then_inc(hid_done, 1)

                def support2(g):
                    pe.wait_ge(hid_ready, g + 1)
                    if g:
                        pe.wait_ge(sup2_ready, g)
                    for q in range(BLK):
                        for f in range(2):
                            ins = mm(Z[0:R, q, :], hidT[:, f, rows(q)], w2g[:, g, f, :],
                                     start=(f == 0), stop=(f == 1))
                    ins.then_inc(sup2_done, 1)

                def group_out(g):
                    pe.wait_ge(sup2_ready, g + 1)
                    if g:
                        pe.wait_ge(gout_ready, g)
                    for q in range(BLK):
                        ins = mm(M[:, rows(q)], sup2[:, q, :], normT[:, q * G + g, :],
                                 start=True, stop=True)
                    ins.then_inc(gout_done, 1)

                support1(0)
                pe.wait_ge(normT_ready, 1)
                hidden(0)
                support1(1)
                for g in range(G):
                    support2(g)
                    if g + 1 < G:
                        hidden(g + 1)
                    group_out(g)
                    if g + 2 < G:
                        support1(g + 2)
                pe.wait_ge(fused_ready, G)
                for b in range(B):
                    ins = nc.tensor.transpose(L[0:GN, b // 4, (b % 4) * D:(b % 4 + 1) * D],
                                              fused[:, b * GN:(b + 1) * GN], ident[:])
                ins.then_inc(back_done, 1)

            @block.scalar
            def _(act):
                fn = nc.scalar.activation
                act.wait_ge(consts_loaded, consts_value)
                act.wait_ge(fmax_ready, 1)
                fn(fexp[:], fw[:], ACT.Exp, bias=fsum[:, 1:2], accum_out=fsum[:, 2:3])\
                    .then_inc(fexp_ready, 1)
                act.wait_ge(x25T_done, 1)
                fn(h25T[:], M[:, 0:B * GN], ACT.Relu).then_inc(h25_ready, 1)

                def hidden_out(g):
                    act.wait_ge(hid_done, g + 1)
                    for f in range(2):
                        ins = fn(hidT[:, f, :], L[:, f, 0:B * GN], ACT.Relu,
                                 bias=b1g[:, g, f:f + 1])
                    ins.then_inc(hid_ready, 1)

                hidden_out(0)
                for g in range(G):
                    if g + 1 < G:
                        hidden_out(g + 1)
                    act.wait_ge(gout_done, g + 1)
                    if g:
                        act.wait_ge(fused_ready, g)
                    fn(gout[:], M[:, 0:B * GN], ACT.Relu, bias=b2g[:, g:g + 1])\
                        .then_inc(gout_ready, 1)

            @block.vector
            def _(dve):
                tt, ts, stt = (nc.vector.tensor_tensor, nc.vector.tensor_scalar,
                               nc.vector.scalar_tensor_tensor)
                steps = [0]

                def link(ins):
                    steps[0] += 1
                    ins.then_inc(l2_step, 1)
                    dve.wait_ge(l2_step, steps[0])

                link(nc.vector.reduce_max(fsum[:, 0:1], fw[:], AX_X))
                ts(fsum[:, 1:2], fsum[:, 0:1], -1.0, None, ALU.mult).then_inc(fmax_ready, 1)
                per_row = dinv[:].rearrange("p (i o) -> p i o", o=1)
                dve.wait_ge(dinv_ready, 2)
                dve.wait_ge(adjTr_done, 1)
                for q in range(BLK):
                    ins = tt(normT[:, q * G:(q + 1) * G, :],
                             L[0:R, q, 0:G * R].rearrange("p (g n) -> p g n", g=G),
                             per_row[:, q * G:(q + 1) * G, :].to_broadcast([R, G, R]), ALU.mult)
                ins.then_inc(normT_ready, 1)

                def add_group(g):
                    wm = wmask[:, g:g + 1, :].to_broadcast([D, B, GN])
                    rows_of = gout[:].rearrange("p (b n) -> p b n", b=B)
                    fused_of = fused[:].rearrange("p (b n) -> p b n", b=B)
                    dve.wait_ge(gout_ready, g + 1)
                    if g == 0:
                        link(tt(fused_of, rows_of, wm, ALU.mult))
                    else:
                        link(tt(rows_of, rows_of, wm, ALU.mult))
                        link(tt(fused[:], fused[:], gout[:], ALU.add))
                    dve.sem_inc(fused_ready, 1)


                def sup1_out(g):
                    dve.wait_ge(sup1_done, g + 1)
                    nc.vector.tensor_copy(sup1[:].rearrange("p (h q) e -> p h (q e)", h=2),
                                          Y[0:R, :, :]).then_inc(sup1_ready, 1)

                sup1_out(0)
                dve.wait_ge(fexp_ready, 1)
                link(nc.vector.reciprocal(fsum[:, 3:4], fsum[:, 2:3]))
                link(ts(fexp[:], fexp[:], fsum[:, 3:4], None, ALU.mult))
                for g in range(G):
                    ins = ts(wmask[:, g, :], node_mask[:, g, :], fexp[:, g:g + 1], None, ALU.mult)
                link(ins)
                dve.wait_ge(hid_done, 1)
                sup1_out(1)
                for g in range(G):
                    dve.wait_ge(sup2_done, g + 1)
                    if g:
                        dve.wait_ge(gout_done, g)
                    nc.vector.tensor_copy(sup2[:], Z[0:R, :, :]).then_inc(sup2_ready, 1)
                    if g + 2 < G:
                        dve.wait_ge(hid_done, g + 2)
                        sup1_out(g + 2)
                    add_group(g)
                add_fused(dve, 0)

        SLOTS = 4
        TURNS = B // SLOTS
        var3 = [sb(f"var3_{i}", [P, C]) for i in range(2)]
        rstd3 = [sb(f"rstd3_{i}", [P, C]) for i in range(2)]
        mv3 = [sb(f"mv3_{i}", [P, C, 2]) for i in range(2)]
        st3 = sb("st3", [P, C, 6])
        st_h = sb("st_h", [P, C, 6])
        mv_h = sb("mv_h", [P, C, 2])
        var_h = sb("var_h", [P, C])
        rstd_h = sb("rstd_h", [P, C])
        h1 = [sb(f"h1_{i}", [P, C, D]) for i in range(2)]
        xh = [sb(f"xh_{i}", [P, C, D]) for i in range(SLOTS)]
        hn = sb("hn", [P, C, D])
        hT = sb("hT", [D, N])
        hw = sb("hw", [P, C, D])
        cT = sb("cT", [D, N])
        ob = [sb(f"ob_{i}", [P, C, D]) for i in range(2)]

        st3_ready, mv3_ready, var3_ready, rstd3_ready = (sem("st3_ready"), sem("mv3_ready"),
                                                         sem("var3_ready"), sem("rstd3_ready"))
        xn3_ready, h1_ready, xh_ready = sem("xn3_ready"), sem("h1_ready"), sem("xh_ready")
        sth_ready, mvh_ready, varh_ready, rstdh_ready = (sem("sth_ready"), sem("mvh_ready"),
                                                         sem("varh_ready"), sem("rstdh_ready"))
        hn_ready, hnT_done, hT_ready = sem("hn_ready"), sem("hnT_done"), sem("hT_ready")
        hw_done, hw_ready, conv_done, cT_ready = (sem("hw_done"), sem("hw_ready"),
                                                  sem("conv_done"), sem("cT_ready"))
        cback_done, out_ready = sem("cback_done"), sem("out_ready")
        out_stored = [sem(f"out_stored{i}") for i in range(2)]
        out_rows = out.rearrange("b (c p) d -> p b c d", p=P)
        conv_out = [L[:, 0, 0:N], L[:, 1, 0:N]]
        back_out = [Y[0:P, 0, :].rearrange("p (c d) -> p c d", c=C),
                    Y[0:P, 1, :].rearrange("p (c d) -> p c d", c=C)]

        def turns(eng, body):
            body(0, True, False)
            with eng.Fori(1, TURNS - 1) as u:
                body(u, False, False)
            body(TURNS - 1, False, True)

        with nc.Block() as block:

            @block.sync
            def _(sp):
                def store(m, i):
                    sp.wait_ge(out_ready, m + 1)
                    sp.dma_start(out_rows[:, ds(m, 1)].rearrange("p b c d -> p (b c) d"),
                                 ob[i % 2][:]).then_inc(out_stored[i % 2], 16)

                def body(u, first, last):
                    for i in range(SLOTS):
                        m = SLOTS * u + i
                        if not (first and i == 0):
                            store(m - 1, i - 1)
                        if not last:
                            sp.wait_ge(conv_done, m + 1)
                            load_adj3(sp, i, m + SLOTS)

                turns(sp, body)
                store(B - 1, SLOTS - 1)
                for i in range(2):
                    sp.wait_ge(out_stored[i], 16 * (B // 2))

            @block.gpsimd
            def _(pool):
                def pow_x(m, i):
                    pool.wait_ge(var3_ready, m + 1)
                    nc.gpsimd.tensor_tensor(rstd3[i % 2][:], var3[i % 2][:], neg_half[0:P, 0:C],
                                            ALU.pow).then_inc(rstd3_ready, 1)

                def pow_h(m):
                    pool.wait_ge(varh_ready, m + 1)
                    nc.gpsimd.tensor_tensor(rstd_h[:], var_h[:], neg_half[0:P, 0:C],
                                            ALU.pow).then_inc(rstdh_ready, 1)

                def add_xh(m, i, first):
                    pool.wait_ge(h1_ready, m + 1)
                    if not first:
                        pool.wait_ge(out_ready, m - SLOTS + 1)
                    nc.gpsimd.tensor_tensor(
                        xh[i % SLOTS][:], h1[i % 2][:],
                        X[:, ds(m, 1), :, :].rearrange("p b c d -> p (b c) d"), ALU.add)\
                        .then_inc(xh_ready, 1)

                pow_x(0, 0)
                pow_x(1, 1)
                pow_h(0)
                pow_x(2, 2)
                add_xh(0, 0, True)
                pow_h(1)
                add_xh(1, 1, True)

                def body(u, first, last):
                    for i in range(SLOTS):
                        m = SLOTS * u + i
                        if not (last and i + 3 >= SLOTS):
                            pow_x(m + 3, i + 3)
                        if not (last and i + 2 >= SLOTS):
                            pow_h(m + 2)
                            add_xh(m + 2, i + 2, first and i + 2 < SLOTS)

                turns(pool, body)

            @block.tensor
            def _(pe):
                mm = nc.tensor.matmul

                def norm_transpose(m):
                    pe.wait_ge(hn_ready, m + 1)
                    for c in range(C):
                        ins = nc.tensor.transpose(M[:, chunk(c)], hn[:, c, :], ident[0:P, 0:P])
                    ins.then_inc(hnT_done, 1)

                def back(m, i):
                    pe.wait_ge(cT_ready, m + 1)
                    for c in range(C):
                        ins = nc.tensor.transpose(back_out[i % 2][:, c, :], cT[:, chunk(c)],
                                                  ident[:])
                    ins.then_inc(cback_done, 1)

                def body(u, first, last):
                    for i in range(SLOTS):
                        m = SLOTS * u + i
                        pe.wait_ge(hT_ready, m + 1)
                        for c in range(C):
                            ins = mm(Z[0:P, c, :], hT[:, chunk(c)], w_rel[:], start=True,
                                     stop=True)
                        ins.then_inc(hw_done, 1)
                        mm(conv_out[i % 2], w_root[:], hT[:], start=True, stop=False)
                        if not (last and i == SLOTS - 1):
                            norm_transpose(m + 1)
                        if not (first and i == 0):
                            back(m - 1, i - 1)
                        pe.wait_ge(hw_ready, m + 1)
                        pe.wait_ge(adj3_loaded[i], 16 * u + 16)
                        for c in range(C):
                            ins = mm(conv_out[i % 2], hw[:, c, :], adj3[i][:, c, :], start=False,
                                     stop=(c == C - 1))
                        ins.then_inc(conv_done, 1)

                norm_transpose(0)
                turns(pe, body)
                pe.wait_ge(out_ready, B - 2)
                back(B - 1, SLOTS - 1)

            @block.scalar
            def _(act):
                fn = nc.scalar.activation

                def scale_shift(m):
                    act.wait_ge(hnT_done, m + 1)
                    fn(hT[:], M[:, 0:N], ACT.Identity, bias=beta[:], scale=gamma[:])\
                        .then_inc(hT_ready, 1)

                def body(u, first, last):
                    for i in range(SLOTS):
                        m = SLOTS * u + i
                        act.wait_ge(hw_done, m + 1)
                        fn(hw[:], Z[0:P, :, :], ACT.Copy).then_inc(hw_ready, 1)
                        if not (last and i == SLOTS - 1):
                            scale_shift(m + 1)
                        act.wait_ge(conv_done, m + 1)
                        if not (first and i == 0):
                            act.wait_ge(cback_done, m)
                        fn(cT[:], conv_out[i % 2], ACT.Relu, bias=b_rel[:]).then_inc(cT_ready, 1)

                scale_shift(0)
                turns(act, body)

            @block.vector
            def _(dve):
                tt, ts = nc.vector.tensor_tensor, nc.vector.tensor_scalar

                def stats_x(m, i):
                    for c in range(C):
                        ins = nc.vector.bn_stats(
                            st3[:, c, :], X[:, ds(m, 1), c, :].rearrange("p b d -> p (b d)"))
                    ins.then_inc(st3_ready, 1)
                    dve.wait_ge(st3_ready, m + 1)
                    pass_gate(dve, dve_passed)
                    for c in range(C):
                        ins = nc.vector.bn_aggr(mv3[i % 2][:, c, :], st3[:, c, :])
                    ins.then_inc(mv3_ready, 1)
                    dve.wait_ge(mv3_ready, m + 1)
                    ts(var3[i % 2][:], mv3[i % 2][:, :, 1], EPS_LN, None, ALU.add)\
                        .then_inc(var3_ready, 1)

                def outer_norm(m, i, first):
                    h = h1[i % 2]
                    dve.wait_ge(rstd3_ready, m + 1)
                    if not first:
                        dve.wait_ge(xh_ready, m - 1)
                    for c in range(C):
                        ins = ts(h[:, c, :], X[:, ds(m, 1), c, :].rearrange("p b d -> p (b d)"),
                                 mv3[i % 2][:, c, 0:1], rstd3[i % 2][:, c:c + 1], ALU.subtract,
                                 ALU.mult)
                    ins.then_inc(xn3_ready, 1)
                    dve.wait_ge(xn3_ready, m + 1)
                    ts(h[:], h[:], 0.0, None, ALU.max).then_inc(h1_ready, 1)
                    dve.wait_ge(h1_ready, m + 1)
                    pass_gate(dve, dve_passed)
                    for c in range(C):
                        ins = nc.vector.bn_stats(st_h[:, c, :], h[:, c, :])
                    ins.then_inc(sth_ready, 1)
                    dve.wait_ge(sth_ready, m + 1)
                    pass_gate(dve, dve_passed)
                    for c in range(C):
                        ins = nc.vector.bn_aggr(mv_h[:, c, :], st_h[:, c, :])
                    ins.then_inc(mvh_ready, 1)
                    dve.wait_ge(mvh_ready, m + 1)
                    ts(var_h[:], mv_h[:, :, 1], EPS_LN, None, ALU.add).then_inc(varh_ready, 1)

                def inner_norm(m, i, first):
                    dve.wait_ge(rstdh_ready, m + 1)
                    if not first:
                        dve.wait_ge(hnT_done, m)
                    for c in range(C):
                        ins = ts(hn[:, c, :], h1[i % 2][:, c, :], mv_h[:, c, 0:1],
                                 rstd_h[:, c:c + 1], ALU.subtract, ALU.mult)
                    ins.then_inc(hn_ready, 1)

                def finish(m, i, u, free):
                    dve.wait_ge(cback_done, m + 1)
                    dve.wait_ge(xh_ready, m + 1)
                    if not free:
                        dve.wait_ge(out_stored[i % 2], 16 * (SLOTS // 2 * u + i // 2))
                    tt(ob[i % 2][:], back_out[i % 2], xh[i % SLOTS][:], ALU.add)\
                        .then_inc(out_ready, 1)

                def body(u, first, last):
                    for i in range(SLOTS):
                        m = SLOTS * u + i
                        if not (last and i + 1 >= SLOTS):
                            inner_norm(m + 1, i + 1, False)
                        if not (last and i + 3 >= SLOTS):
                            stats_x(m + 3, i + 3)
                        if not (last and i + 2 >= SLOTS):
                            outer_norm(m + 2, i + 2, False)
                        if not (first and i == 0):
                            if i == 0:
                                finish(m - 1, SLOTS - 1, u - 1, False)
                            else:
                                finish(m - 1, i - 1, u, first and i <= 2)

                stats_x(0, 0)
                for i in range(1, 4):
                    add_fused(dve, i)
                dve.wait_ge(x3_ready, 4)
                stats_x(1, 1)
                outer_norm(0, 0, True)
                stats_x(2, 2)
                inner_norm(0, 0, True)
                outer_norm(1, 1, True)
                turns(dve, body)
                finish(B - 1, SLOTS - 1, TURNS - 1, False)


def kernel(**inputs):
    import concourse.bacc as bacc
    from concourse.bass_utils import run_bass_kernel_spmd

    a = {k: np.asarray(v) for k, v in inputs.items()}

    def rep(v, rows):
        return np.broadcast_to(v, (rows,) + v.shape)

    member = np.zeros((G, GN), np.float32)
    for g, nodes in enumerate(GROUPS):
        member[g, nodes] = 1.0
    pair_mask = member[:, :, None] * member[:, None, :]
    blocks = np.zeros((GB, GN, GB, GN), np.float32)
    for i in range(GB):
        blocks[i, :, i, :] = 1.0
    a_l1 = a["L1_gnn_a"]
    layout = {
        "x": a["x"],
        "adj": a["adj"],
        "adjT": a["adj"].transpose(0, 2, 1),
        "ident": np.eye(128, dtype=np.float32),
        "off_diag": 1 - np.eye(P, dtype=np.float32),
        "wqT": a["L0_gnn_W_attn"].transpose(2, 0, 1),
        "w0T": a["L0_gnn_W0"].transpose(2, 0, 1),
        "w1T": a["L0_gnn_W1"].transpose(2, 0, 1),
        "bq": a["L0_gnn_b_attn"].T,
        "b0": a["L0_gnn_b0"].T,
        "b1": a["L0_gnn_b1"].T,
        "wfT": a["L0_gnn_Wf"].T,
        "bf_rows": rep(a["L0_gnn_bf"], P),
        "w_l1": a["L1_gnn_W"],
        "w_l1T": a["L1_gnn_W"].T,
        "a_rep": np.concatenate([np.broadcast_to(a_l1[D:], (D, D)), a_l1[:D]], axis=1),
        "w1g": a["L2_gnn_W1"].transpose(1, 0, 2),
        "w2g": a["L2_gnn_W2"].reshape(G, 2, D, D).transpose(2, 0, 1, 3),
        "b1g": a["L2_gnn_b1"].reshape(G, 2, D).transpose(2, 0, 1),
        "b2g": a["L2_gnn_b2"].T,
        "fw": rep(a["L2_gnn_fusion_w"], D),
        "gmask": np.tile(pair_mask.transpose(1, 0, 2), (GB, 1, 1)),
        "eye25": np.tile(np.eye(GN, dtype=np.float32), (GB, 1)),
        "block_mask": blocks.reshape(R, GB, GN),
        "node_mask": rep(member, D),
        "adj25": a["adj"][:, :GN, :GN].reshape(BLK, R, GN).transpose(1, 0, 2),
        "w_rel": a["L3_gnn_W_rel"],
        "w_root": a["L3_gnn_W_root"],
        "b_rel": a["L3_gnn_b_rel"][:, None],
        "gamma": a["L3_gnn_ln_gamma"][:, None],
        "beta": a["L3_gnn_ln_beta"][:, None],
    }
    nc = bacc.Bacc("TRN2", target_bir_lowering=False, num_devices=1)
    arrays, t = {}, {}
    for name, v in layout.items():
        v = np.ascontiguousarray(v)
        arrays[f"in_{name}"] = v
        t[name] = nc.dram_tensor(f"in_{name}", v.shape, mybir.dt.from_np(v.dtype),
                                 kind="ExternalInput").ap()
    out = nc.dram_tensor("out_x", (B, N, D), F32, kind="ExternalOutput").ap()
    build(nc, t, out)
    r = run_bass_kernel_spmd(nc, [arrays], core_ids=[0])
    return r.results[0]["out_x"]
```
